# Optimizing a Trainium2 kernel written in Bass

```python
import numpy as np
import jax
import jax.numpy as jnp

def _softmax(x, axis=-1):
    return jax.nn.softmax(x, axis=axis)

def _gelu(x):
    return jax.nn.gelu(x, approximate=True)

def _silu(x):
    return jax.nn.silu(x)

def _sigmoid(x):
    return jax.nn.sigmoid(x)

def _layernorm(x, axis=-1, eps=1e-05):
    m = jnp.mean(x, axis=axis, keepdims=True)
    v = jnp.var(x, axis=axis, keepdims=True)
    return (x - m) / jnp.sqrt(v + eps)

def _scatter_add(tgt, idx, src, axis=0):
    return tgt.at[idx].add(src)

def _segment_sum(src, seg, n):
    return jax.ops.segment_sum(src, seg, n)
kernel_name = 'mk_gps_d2_gnn_r8_799b79'

def setup_inputs(seed: int=0):
    np.random.seed(seed)
    _w = jnp.asarray

    def _rec_inputs():
        import jax
        import jax.numpy as jnp
        _gk = jax.random.key(seed)
        x = -6.415e-05 + 1 * jax.random.normal(jax.random.fold_in(_gk, 1), (1250, 1024), jnp.float32)
        _s = jax.random.randint(jax.random.fold_in(_gk, 2), (10000,), 0, 1250, jnp.int32)
        _d = jax.random.randint(jax.random.fold_in(_gk, 3), (10000,), 0, 1250, jnp.int32)
        _loop = jnp.arange(1250, dtype=jnp.int32)
        src = jnp.concatenate([_s, _d, _loop])
        dst = jnp.concatenate([_d, _s, _loop])
        _o = jnp.argsort(dst, stable=True)
        src = src[_o]
        dst = dst[_o]
        return (x, src, dst)
    x, src, dst = _rec_inputs()

    def _L0_gnn_setup():
        import jax, jax.numpy as jnp
        import numpy as np
        N_NODES = 1250
        N_EDGES = 20000
        DIM = 1024
        key = jax.random.key(seed)
        k1, k2, k3 = jax.random.split(key, 3)
        x = jax.random.normal(k1, (N_NODES, DIM), dtype=jnp.float32)
        edge_index = jax.random.randint(k2, (2, N_EDGES), 0, N_NODES, dtype=jnp.int64)
        W = jax.random.normal(k3, (DIM, DIM), dtype=jnp.float32) * (1.0 / np.sqrt(DIM))
        b = jnp.zeros((DIM,), dtype=jnp.float32)
        return {'x': x, 'edge_index': edge_index, 'W': W, 'b': b}
    _L0_gnn_all = _L0_gnn_setup()
    _L0_gnn_in = {k: v for k, v in _L0_gnn_all.items() if k in ('W', 'b')}
    del _L0_gnn_all

    def _L0_mix_setup():
        import jax, jax.numpy as jnp
        import numpy as np
        EMBED_DIM = 1024
        NUM_HEADS = 16
        HEAD_DIM = EMBED_DIM // NUM_HEADS
        NUM_FEATS = 256
        YAT_EPS = 0.1
        BATCH = 4
        SEQ = 512

        def _spherical_features(x, projection):
            x_norm = x / (jnp.linalg.norm(x, axis=-1, keepdims=True) + 1e-08)
            proj = jnp.einsum('bhsd,hfd->bhsf', x_norm, projection)
            return jax.nn.relu(proj) + YAT_EPS
        key = jax.random.key(seed)
        ks = jax.random.split(key, 6)
        s = 1.0 / np.sqrt(EMBED_DIM)
        return {'x': jax.random.normal(ks[0], (BATCH, SEQ, EMBED_DIM), jnp.float32), 'Wq': jax.random.normal(ks[1], (EMBED_DIM, EMBED_DIM), jnp.float32) * s, 'bq': jnp.zeros((EMBED_DIM,), jnp.float32), 'Wk': jax.random.normal(ks[2], (EMBED_DIM, EMBED_DIM), jnp.float32) * s, 'bk': jnp.zeros((EMBED_DIM,), jnp.float32), 'Wv': jax.random.normal(ks[3], (EMBED_DIM, EMBED_DIM), jnp.float32) * s, 'bv': jnp.zeros((EMBED_DIM,), jnp.float32), 'Wo': jax.random.normal(ks[4], (EMBED_DIM, EMBED_DIM), jnp.float32) * s, 'bo': jnp.zeros((EMBED_DIM,), jnp.float32), 'projection': jax.random.normal(ks[5], (NUM_HEADS, NUM_FEATS, HEAD_DIM), jnp.float32)}
    _L0_mix_all = _L0_mix_setup()
    _L0_mix_in = {k: v for k, v in _L0_mix_all.items() if k in ('Wq', 'bq', 'Wk', 'bk', 'Wv', 'bv', 'Wo', 'bo', 'projection')}
    del _L0_mix_all

    def _L0_ffn_setup():
        import jax, jax.numpy as jnp
        import numpy as np
        NUM_EXPERTS = 8
        TOP_K = 2
        CAPACITY_FACTOR = 1.25
        key = jax.random.key(seed)
        k1, k2, k3, k4, k5 = jax.random.split(key, 5)
        B, S, H, I, E = (4, 256, 1024, 512, NUM_EXPERTS)
        return {'hidden_states': jax.random.normal(k1, (B, S, H), dtype=jnp.float32), 'router_gate': jax.random.normal(k2, (H, E), dtype=jnp.float32) * 0.02, 'gate_w': jax.random.normal(k3, (E, H, I), dtype=jnp.float32) * 0.02, 'up_w': jax.random.normal(k4, (E, H, I), dtype=jnp.float32) * 0.02, 'down_w': jax.random.normal(k5, (E, I, H), dtype=jnp.float32) * 0.02}
    _L0_ffn_all = _L0_ffn_setup()
    _L0_ffn_in = {k: v for k, v in _L0_ffn_all.items() if k in ('router_gate', 'gate_w', 'up_w', 'down_w')}
    del _L0_ffn_all

    def _L1_gnn_setup():
        import jax, jax.numpy as jnp
        import numpy as np
        N_NODES = 3125
        N_EDGES = 50000
        D = 1024

        def _sage_layer(h, edge_src, edge_dst, deg_inv, W_self, W_neigh, b):
            msg = h[edge_src]
            agg = jax.ops.segment_sum(msg, edge_dst, num_segments=h.shape[0])
            mean = agg * deg_inv[:, None]
            return h @ W_self + mean @ W_neigh + b
        key = jax.random.key(seed)
        ks = jax.random.split(key, 8)
        s = 1.0 / np.sqrt(D)
        return {'x': jax.random.normal(ks[0], (N_NODES, D), dtype=jnp.float32), 'edge_src': jax.random.randint(ks[1], (N_EDGES,), 0, N_NODES, dtype=jnp.int32), 'edge_dst': jax.random.randint(ks[2], (N_EDGES,), 0, N_NODES, dtype=jnp.int32), 'W_self0': jax.random.normal(ks[3], (D, D), dtype=jnp.float32) * s, 'W_neigh0': jax.random.normal(ks[4], (D, D), dtype=jnp.float32) * s, 'b0': jnp.zeros((D,), dtype=jnp.float32), 'W_self1': jax.random.normal(ks[5], (D, D), dtype=jnp.float32) * s, 'W_neigh1': jax.random.normal(ks[6], (D, D), dtype=jnp.float32) * s, 'b1': jnp.zeros((D,), dtype=jnp.float32)}
    _L1_gnn_all = _L1_gnn_setup()
    _L1_gnn_in = {k: v for k, v in _L1_gnn_all.items() if k in ('W_self0', 'W_neigh0', 'b0', 'W_self1', 'W_neigh1', 'b1')}
    del _L1_gnn_all

    def _L1_mix_setup():
        import jax, jax.numpy as jnp
        import numpy as np
        import math
        DIM = 1024
        H = 16
        HD = DIM // H
        M = 64
        B, S = (4, 512)

        def _feature_map(t, P):
            proj = jnp.einsum('bhsd,hmd->bhsm', t, P)
            return jax.nn.relu(proj) * (1.0 / math.sqrt(P.shape[1]))
        key = jax.random.key(seed)
        ks = jax.random.split(key, 10)
        sc = 1.0 / math.sqrt(DIM)
        return {'x': jax.random.normal(ks[0], (B, S, DIM), dtype=jnp.float32), 'Wq': jax.random.normal(ks[1], (DIM, DIM), dtype=jnp.float32) * sc, 'bq': jax.random.normal(ks[2], (DIM,), dtype=jnp.float32) * 0.01, 'Wk': jax.random.normal(ks[3], (DIM, DIM), dtype=jnp.float32) * sc, 'bk': jax.random.normal(ks[4], (DIM,), dtype=jnp.float32) * 0.01, 'Wv': jax.random.normal(ks[5], (DIM, DIM), dtype=jnp.float32) * sc, 'bv': jax.random.normal(ks[6], (DIM,), dtype=jnp.float32) * 0.01, 'Wo': jax.random.normal(ks[7], (DIM, DIM), dtype=jnp.float32) * sc, 'bo': jax.random.normal(ks[8], (DIM,), dtype=jnp.float32) * 0.01, 'P': jax.random.normal(ks[9], (H, M, HD), dtype=jnp.float32)}
    _L1_mix_all = _L1_mix_setup()
    _L1_mix_in = {k: v for k, v in _L1_mix_all.items() if k in ('Wq', 'bq', 'Wk', 'bk', 'Wv', 'bv', 'Wo', 'bo', 'P')}
    del _L1_mix_all

    def _L1_ffn_setup():
        import jax, jax.numpy as jnp
        import numpy as np
        TOP_K = 2
        key = jax.random.key(seed)
        k1, k2, k3, k4 = jax.random.split(key, 4)
        B, T, D, H, E = (2, 256, 1024, 256, 8)
        x = jax.random.normal(k1, (B, T, D), dtype=jnp.float32)
        w12 = jax.random.normal(k2, (E, 2 * H, D), dtype=jnp.float32) * D ** (-0.5)
        w3 = jax.random.normal(k3, (E, D, H), dtype=jnp.float32) * H ** (-0.5)
        gate_w = jax.random.normal(k4, (E, D), dtype=jnp.float32) * D ** (-0.5)
        return {'x': x, 'w12': w12, 'w3': w3, 'gate_w': gate_w}
    _L1_ffn_all = _L1_ffn_setup()
    _L1_ffn_in = {k: v for k, v in _L1_ffn_all.items() if k in ('w12', 'w3', 'gate_w')}
    del _L1_ffn_all
    return {'x': x, 'src': src, 'dst': dst, 'L0_gnn_W': _L0_gnn_in['W'], 'L0_gnn_b': _L0_gnn_in['b'], 'L0_mix_Wq': _L0_mix_in['Wq'], 'L0_mix_bq': _L0_mix_in['bq'], 'L0_mix_Wk': _L0_mix_in['Wk'], 'L0_mix_bk': _L0_mix_in['bk'], 'L0_mix_Wv': _L0_mix_in['Wv'], 'L0_mix_bv': _L0_mix_in['bv'], 'L0_mix_Wo': _L0_mix_in['Wo'], 'L0_mix_bo': _L0_mix_in['bo'], 'L0_mix_projection': _L0_mix_in['projection'], 'L0_ffn_router_gate': _L0_ffn_in['router_gate'], 'L0_ffn_gate_w': _L0_ffn_in['gate_w'], 'L0_ffn_up_w': _L0_ffn_in['up_w'], 'L0_ffn_down_w': _L0_ffn_in['down_w'], 'L1_gnn_W_self0': _L1_gnn_in['W_self0'], 'L1_gnn_W_neigh0': _L1_gnn_in['W_neigh0'], 'L1_gnn_b0': _L1_gnn_in['b0'], 'L1_gnn_W_self1': _L1_gnn_in['W_self1'], 'L1_gnn_W_neigh1': _L1_gnn_in['W_neigh1'], 'L1_gnn_b1': _L1_gnn_in['b1'], 'L1_mix_Wq': _L1_mix_in['Wq'], 'L1_mix_bq': _L1_mix_in['bq'], 'L1_mix_Wk': _L1_mix_in['Wk'], 'L1_mix_bk': _L1_mix_in['bk'], 'L1_mix_Wv': _L1_mix_in['Wv'], 'L1_mix_bv': _L1_mix_in['bv'], 'L1_mix_Wo': _L1_mix_in['Wo'], 'L1_mix_bo': _L1_mix_in['bo'], 'L1_mix_P': _L1_mix_in['P'], 'L1_ffn_w12': _L1_ffn_in['w12'], 'L1_ffn_w3': _L1_ffn_in['w3'], 'L1_ffn_gate_w': _L1_ffn_in['gate_w']}

def reference(x, src, dst, L0_gnn_W, L0_gnn_b, L0_mix_Wq, L0_mix_bq, L0_mix_Wk, L0_mix_bk, L0_mix_Wv, L0_mix_bv, L0_mix_Wo, L0_mix_bo, L0_mix_projection, L0_ffn_router_gate, L0_ffn_gate_w, L0_ffn_up_w, L0_ffn_down_w, L1_gnn_W_self0, L1_gnn_W_neigh0, L1_gnn_b0, L1_gnn_W_self1, L1_gnn_W_neigh1, L1_gnn_b1, L1_mix_Wq, L1_mix_bq, L1_mix_Wk, L1_mix_bk, L1_mix_Wv, L1_mix_bv, L1_mix_Wo, L1_mix_bo, L1_mix_P, L1_ffn_w12, L1_ffn_w3, L1_ffn_gate_w):
    import jax
    import jax.numpy as jnp

    def _L0_gnn_ref(x, edge_index, W, b):
        import jax, jax.numpy as jnp
        import numpy as np
        N_NODES = 1250
        N_EDGES = 20000
        DIM = 1024
        'GCNConv (add_self_loops=True, symmetric norm) -> Dropout(eval=identity) -> ReLU.'
        n = x.shape[0]
        loops = jnp.arange(n, dtype=edge_index.dtype)
        src = jnp.concatenate([edge_index[0], loops])
        dst = jnp.concatenate([edge_index[1], loops])
        deg = jax.ops.segment_sum(jnp.ones_like(dst, dtype=x.dtype), dst, num_segments=n)
        dinv = jnp.where(deg > 0, jax.lax.rsqrt(deg), jnp.zeros_like(deg))
        norm = dinv[src] * dinv[dst]
        h = x @ W
        msg = h[src] * norm[:, None]
        out = jax.ops.segment_sum(msg, dst, num_segments=n) + b
        return jax.nn.relu(out)

    def _L0_mix_ref(x, Wq, bq, Wk, bk, Wv, bv, Wo, bo, projection):
        import jax, jax.numpy as jnp
        import numpy as np
        EMBED_DIM = 1024
        NUM_HEADS = 16
        HEAD_DIM = EMBED_DIM // NUM_HEADS
        NUM_FEATS = 256
        YAT_EPS = 0.1
        BATCH = 4
        SEQ = 512

        def _spherical_features(x, projection):
            x_norm = x / (jnp.linalg.norm(x, axis=-1, keepdims=True) + 1e-08)
            proj = jnp.einsum('bhsd,hfd->bhsf', x_norm, projection)
            return jax.nn.relu(proj) + YAT_EPS
        b, s, _ = x.shape

        def heads(t):
            return jnp.transpose(t.reshape(b, s, NUM_HEADS, HEAD_DIM), (0, 2, 1, 3))
        Q = heads(x @ Wq + bq)
        K = heads(x @ Wk + bk)
        V = heads(x @ Wv + bv)
        Qp = _spherical_features(Q, projection)
        Kp = _spherical_features(K, projection)
        KV = jnp.einsum('bhsf,bhsd->bhfd', Kp, V)
        QKV = jnp.einsum('bhsf,bhfd->bhsd', Qp, KV)
        K_sum = jnp.sum(Kp, axis=2)
        normalizer = jnp.einsum('bhsf,bhf->bhs', Qp, K_sum)[..., None]
        normalizer = jnp.maximum(normalizer, 1e-06)
        out = QKV / normalizer
        out = jnp.transpose(out, (0, 2, 1, 3)).reshape(b, s, EMBED_DIM)
        return out @ Wo + bo

    def _L0_ffn_ref(hidden_states, router_gate, gate_w, up_w, down_w):
        import jax, jax.numpy as jnp
        import numpy as np
        NUM_EXPERTS = 8
        TOP_K = 2
        CAPACITY_FACTOR = 1.25
        B, S, H = hidden_states.shape
        E = router_gate.shape[1]
        K = TOP_K
        x = hidden_states.reshape(-1, H)
        T = x.shape[0]
        cap = int(CAPACITY_FACTOR * ((T * K + E - 1) // E))
        probs = jax.nn.softmax(x @ router_gate, axis=-1)
        topw, topi = jax.lax.top_k(probs, K)
        topw = topw / (topw.sum(-1, keepdims=True) + 1e-09)
        gates = jnp.zeros((T, E), x.dtype).at[jnp.arange(T)[:, None], topi].set(topw)
        top_g, tok_idx = jax.lax.top_k(gates.T, cap)
        xe = x[tok_idx]
        h = jax.nn.silu(jnp.einsum('ech,ehi->eci', xe, gate_w)) * jnp.einsum('ech,ehi->eci', xe, up_w)
        ye = jnp.einsum('eci,eih->ech', h, down_w) * top_g[..., None]
        out = jnp.zeros_like(x).at[tok_idx.reshape(-1)].add(ye.reshape(-1, H))
        return out.reshape(B, S, H)

    def _L1_gnn_ref(x, edge_src, edge_dst, W_self0, W_neigh0, b0, W_self1, W_neigh1, b1):
        import jax, jax.numpy as jnp
        import numpy as np
        N_NODES = 3125
        N_EDGES = 50000
        D = 1024

        def _sage_layer(h, edge_src, edge_dst, deg_inv, W_self, W_neigh, b):
            msg = h[edge_src]
            agg = jax.ops.segment_sum(msg, edge_dst, num_segments=h.shape[0])
            mean = agg * deg_inv[:, None]
            return h @ W_self + mean @ W_neigh + b
        N = x.shape[0]
        deg = jax.ops.segment_sum(jnp.ones_like(edge_dst, dtype=x.dtype), edge_dst, num_segments=N)
        deg_inv = 1.0 / jnp.maximum(deg, 1.0)
        h = jax.nn.relu(_sage_layer(x, edge_src, edge_dst, deg_inv, W_self0, W_neigh0, b0))
        out = _sage_layer(h, edge_src, edge_dst, deg_inv, W_self1, W_neigh1, b1)
        return out

    def _L1_mix_ref(x, Wq, bq, Wk, bk, Wv, bv, Wo, bo, P):
        import jax, jax.numpy as jnp
        import numpy as np
        import math
        DIM = 1024
        H = 16
        HD = DIM // H
        M = 64
        B, S = (4, 512)

        def _feature_map(t, P):
            proj = jnp.einsum('bhsd,hmd->bhsm', t, P)
            return jax.nn.relu(proj) * (1.0 / math.sqrt(P.shape[1]))
        b, s, dim = x.shape
        h, m, hd = P.shape

        def split_heads(y):
            return y.reshape(b, s, h, hd).transpose(0, 2, 1, 3)
        q = split_heads(x @ Wq.T + bq)
        k = split_heads(x @ Wk.T + bk)
        v = split_heads(x @ Wv.T + bv)
        q_prime = _feature_map(q, P)
        k_prime = _feature_map(k, P)
        kv = jnp.einsum('bhsm,bhsd->bhmd', k_prime, v)
        attn = jnp.einsum('bhsm,bhmd->bhsd', q_prime, kv)
        attn = attn.transpose(0, 2, 1, 3).reshape(b, s, dim)
        return attn @ Wo.T + bo

    def _L1_ffn_ref(x, w12, w3, gate_w):
        import jax, jax.numpy as jnp
        import numpy as np
        TOP_K = 2
        E = gate_w.shape[0]
        H = w3.shape[-1]
        scores = jnp.einsum('btd,ed->bte', x, gate_w)
        topk_scores, topk_idx = jax.lax.top_k(scores, TOP_K)
        topk_probs = jax.nn.softmax(topk_scores, axis=-1)
        total_probs = jnp.sum(jax.nn.one_hot(topk_idx, E, dtype=topk_probs.dtype) * topk_probs[..., None], axis=-2)
        h12 = jnp.einsum('btd,ehd->bteh', x, w12)
        h1, h2 = (h12[..., :H], h12[..., H:])
        hidden = jax.nn.silu(h1) * h2
        expert_out = jnp.einsum('bteh,edh->bted', hidden, w3)
        y = jnp.sum(total_probs[..., None] * expert_out, axis=-2)
        return y
    edge_index = jnp.stack([src, dst])
    xn = _layernorm(x, axis=-1)
    x = x + _L0_gnn_ref(xn, edge_index, L0_gnn_W, L0_gnn_b) + _L0_mix_ref(xn[None], L0_mix_Wq, L0_mix_bq, L0_mix_Wk, L0_mix_bk, L0_mix_Wv, L0_mix_bv, L0_mix_Wo, L0_mix_bo, L0_mix_projection)[0]
    x = x + _L0_ffn_ref(_layernorm(x, axis=-1)[None], L0_ffn_router_gate, L0_ffn_gate_w, L0_ffn_up_w, L0_ffn_down_w)[0]
    xn = _layernorm(x, axis=-1)
    x = x + _L1_gnn_ref(xn, src, dst, L1_gnn_W_self0, L1_gnn_W_neigh0, L1_gnn_b0, L1_gnn_W_self1, L1_gnn_W_neigh1, L1_gnn_b1) + _L1_mix_ref(xn[None], L1_mix_Wq, L1_mix_bq, L1_mix_Wk, L1_mix_bk, L1_mix_Wv, L1_mix_bv, L1_mix_Wo, L1_mix_bo, L1_mix_P)[0]
    x = x + _L1_ffn_ref(_layernorm(x, axis=-1)[None], L1_ffn_w12, L1_ffn_w3, L1_ffn_gate_w)[0]
    return x

_drawn_inputs = setup_inputs


def setup_inputs(seed=0):
    import zlib

    import numpy as np

    out = dict(_drawn_inputs(seed))
    spreads = {'L0_gnn_b': (0.0, 0.1),
     'L0_mix_bq': (0.0, 2.0),
     'L0_mix_bk': (0.0, 2.0),
     'L0_mix_bv': (0.0, 0.1),
     'L0_mix_bo': (0.0, 0.1),
     'L1_gnn_b0': (0.0, 2.0),
     'L1_gnn_b1': (0.0, 2.0)}
    factors = {'L0_mix_Wq': 64.0,
     'L0_mix_Wk': 2.893,
     'L0_mix_projection': 2.987,
     'L0_ffn_router_gate': 2.953,
     'L1_gnn_W_self0': 26.701,
     'L1_gnn_W_neigh0': 64.0,
     'L1_gnn_W_self1': 21.458,
     'L1_gnn_W_neigh1': 33.911,
     'L1_mix_bq': 25.944,
     'L1_mix_bk': 8.0,
     'L1_mix_bo': 64.0,
     'L1_ffn_w12': 8.0,
     'L1_ffn_w3': 8.0,
     'L1_ffn_gate_w': 8.0}
    for name, (base, spread) in spreads.items():
        noise = np.random.default_rng([zlib.crc32(name.encode()), seed]).standard_normal(out[name].shape)
        drawn = base * np.exp(spread * noise) if base else spread * noise
        out[name] = jnp.asarray(drawn.astype(out[name].dtype))
    for name, factor in factors.items():
        out[name] = (out[name] * factor).astype(out[name].dtype)
    return out
```

```python
from contextlib import ExitStack

import concourse.bass as bass
from concourse import mybir

F32 = mybir.dt.float32
I32 = mybir.dt.int32
U32 = mybir.dt.uint32
ALU = mybir.AluOpType
ACT = mybir.ActivationFunctionType
AX = mybir.AxisListType.X

P = 128
T = 1250
D = 1024
R = 125
NT = T // R
KD = D // P
HALF = 512
NH, HD = 16, 64
F0 = 256
E = 8
EDGES = 21250
GROUPS = 168
TABLE = 128 * 13056
DUMP = T * T + 1
CAP, CAPR = 391, 392
CH = [(0, 418), (418, 416), (834, 416)]
AC = 250
NSLOT = 3
SLOT = 4096


class Chain:

    def __init__(self, eng, sem):
        self.eng, self.sem, self.n = eng, sem, 0

    def __call__(self, ins):
        ins.then_inc(self.sem, 1)
        self.n += 1
        return self.n

    def sync(self):
        self.eng.wait_ge(self.sem, self.n)


class Bank:

    def __init__(self, tensor, full, free):
        self.t, self.full, self.free, self.n = tensor, full, free, 0

    def take(self, pe):
        if self.n >= 3:
            pe.wait_ge(self.free, self.n - 2)
        self.n += 1
        return self.t[:, (self.n - 1) % 3, :]

    def read(self, eng):
        eng.wait_ge(self.full, self.n + 1)
        self.n += 1
        return self.t[:, (self.n - 1) % 3, :]


def build(nc, A, out):
    ctx = ExitStack()
    with ctx:
        def sb(name, shape, dt=F32):
            return ctx.enter_context(nc.sbuf_tensor(name, shape, dt))

        def sem(name):
            return ctx.enter_context(nc.semaphore(name))

        def dram(name, shape, dt=F32):
            return nc.dram_tensor(name, shape, dt).ap()

        B1 = sb("B1", [P, 161 * 64])
        B2 = sb("B2", [P, KD * T])
        B3 = sb("B3", [P, NT * D])
        W = sb("W", [P, NSLOT, SLOT])
        KV = sb("KV", [P, NH, 2, P])
        PT = sb("PT", [P, KD, F0])
        RB = sb("RB", [P, 4, HALF])
        BI = sb("BI", [P, 2, HALF])
        ident = sb("ident", [P, P])
        ones = sb("ones", [P, P])
        low = sb("low", [P, P])
        up = sb("up", [P, P])
        ecnt = sb("ecnt", [P, GROUPS])
        eidx = sb("eidx", [P, GROUPS], I32)
        dcol = sb("dcol", [P, NT])
        dinv = sb("dinv", [P, NT])
        gate_sb = sb("gate_sb", [P, KD, E])
        bcol = sb("bcol", [P, 2, KD])
        hs8 = sb("hs8", [P, 8])
        nr8 = sb("nr8", [P, 8])
        wk = sb("wk", [P, 2, NT])
        sidx = sb("sidx", [P, 2, NT], I32)
        gidx = sb("gidx", [P, 2, NT], I32)
        tok = sb("tok", [P, NT], I32)
        dumpc = sb("dumpc", [P, 1])
        tidx = sb("tidx", [P, 34], I32)
        eblk = sb("eblk", [P, 17], I32)
        iot8 = sb("iot8", [P, E])

        PV = ctx.enter_context(nc.psum_tensor("PV", [P, 3, HALF], F32))
        PS = ctx.enter_context(nc.psum_tensor("PS", [P, 3, HALF], F32))
        PA = ctx.enter_context(nc.psum_tensor("PA", [P, 2, HALF], F32))

        at_d = dram("at_d", [TABLE, 1])
        xn_d = dram("xn_d", [T, D])
        x2_d = dram("x2_d", [T, D])
        xm_d = dram("xm_d", [T, D])
        deg_d = dram("deg_d", [1, T])
        slots_d = [dram("slots0_d", [128 * 49, 1], I32), dram("slots1_d", [128 * 49, 1], I32)]
        y_d = [dram("y0_d", [E * CAPR, D]), dram("y1_d", [17 * 256, D])]

        def rows(buf):
            return buf[0:R, 0:NT * D].rearrange("p (i d) -> p i d", d=D)

        def cols(buf):
            return buf[:, 0:KD * T].rearrange("p (k t) -> p k t", t=T)

        v_heads = B1[0:R, :].rearrange("p (n d) -> p n d", d=HD)
        at_rows = at_d[0:T * T, :].rearrange("(j p d) o -> p j (d o)", p=R, d=T)
        rbf = RB[:, :, :].rearrange("p a b -> p (a b)")

        v_full, v_free = sem("v_full"), sem("v_free")
        s_full, s_free = sem("s_full"), sem("s_free")
        dv, ac, pl = sem("dve_step"), sem("act_step"), sem("pool_step")
        w_full = [sem(f"w_full{i}") for i in range(NSLOT)]
        b_full = [sem(f"b_full{i}") for i in range(2)]
        x_in = [sem(f"x_in{i}") for i in range(5)]
        edges_in, small_in, pt_in, gate_in, rg1_in = (sem(n) for n in
                                                      ("edges_in", "small_in", "pt_in", "gate_in", "rg1_in"))
        consts = sem("consts")
        key_ready = sem("key_ready")
        eidx_ready, zero_ready, table_zero, scattered = (sem(n) for n in
                                                         ("eidx_ready", "zero_ready", "table_zero", "scattered"))
        ln_var, ln_std, xn_ready, xn_stored = (sem(n) for n in ("ln_var", "ln_std", "xn_ready", "xn_stored"))
        ones_col = sem("ones_col")
        sq_done, ss_done, nrm_done, qn_done = (sem(n) for n in ("sq_done", "ss_done", "nrm_done", "qn_done"))
        kp_used, kv_free, qp_used, acc_free = (sem(n) for n in ("kp_used", "kv_free", "qp_used", "acc_free"))
        res_full = [sem(f"res_full{i}") for i in range(4)]
        res_used = sem("res_used")
        deg_stored, dg_in, dg_sqrt = sem("deg_stored"), sem("dg_in"), sem("dg_sqrt")
        sm_in, sm_exp, route_ready, ids_ready = (sem(n) for n in ("sm_in", "sm_exp", "route_ready", "ids_ready"))
        gates_ready = sem("gates_ready")
        ids_scat, ids_in = sem("ids_scat"), sem("ids_in")
        xe_full = [sem("xe_full0"), sem("xe_full1")]
        y_st = [sem("y_st0"), sem("y_st1")]
        yg_full = [sem(f"yg_full{i}") for i in range(4)]
        yg_used = sem("yg_used")
        x2_stored, xm_ready, xm_stored, xn_back, dinv_in, h1_ready, kvbd_ready, x3_ready = (
            sem(n) for n in ("x2_stored", "xm_ready", "xm_stored", "xn_back", "dinv_in", "h1_ready",
                             "kvbd_ready", "x3_ready"))
        eblk_ready, out_stored = sem("eblk_ready"), sem("out_stored")

        block = ctx.enter_context(nc.Block())
        mark = {}
        slot_end = []
        bias_end = []
        gather_end = {}
        up_at = {}

        @block.tensor
        def _(pe):
            v, s = Bank(PV, v_full, v_free), Bank(PS, s_full, s_free)
            loads = [0]

            def slot():
                n = loads[0]
                loads[0] += 1
                pe.wait_ge(w_full[n % NSLOT], 16 * (n // NSLOT + 1))
                return W[:, n % NSLOT, :]

            def slot_done(k=1):
                for _ in range(k):
                    slot_end.append((v_full, v.n))

            def turn_rows(src, sem_, base):
                for i in range(NT):
                    pe.wait_ge(sem_, base + i + 1)
                    for ring, k0 in ((v, 0), (s, 4)):
                        bank = ring.take(pe)
                        for k in range(4):
                            mm = pe.transpose(bank[:, k * R:(k + 1) * R],
                                              src[:, i, (k0 + k) * P:(k0 + k + 1) * P], ident[0:R, 0:R])
                        mm.then_inc(ring.full, 1)

            def rows_group(bank, pairs, i, n=HALF):
                last = len(pairs) * KD - 1
                for q in range(last + 1):
                    lhs, w = pairs[q // KD]
                    k = q % KD
                    mm = pe.matmul(bank[0:R, 0:n], lhs[:, k, i * R:(i + 1) * R], w[:, k, 0:n],
                                   start=(q == 0), stop=(q == last))
                return mm

            def linear_rows(lhss, bias=True):
                for half in range(2):
                    ws = [slot().rearrange("p (k n) -> p k n", k=KD) for _ in lhss]
                    for i in range(NT):
                        rows_group(v.take(pe), list(zip(lhss, ws)), i).then_inc(v_full, 1)
                    slot_done(len(lhss))
                    if bias:
                        bias_end.append(v.n)

            def linear_cols(lhs):
                for half in range(2):
                    w = slot().rearrange("p (k n) -> p k n", k=KD)
                    for m in range(4):
                        for c0, cn in CH:
                            bank = v.take(pe)
                            for k in range(KD):
                                mm = pe.matmul(bank[:, 0:cn], w[:, k, m * P:(m + 1) * P], lhs[:, k, c0:c0 + cn],
                                               start=(k == 0), stop=(k == KD - 1))
                            mm.then_inc(v_full, 1)
                    slot_done()

            def neighbours_cols(src):
                for c in range(T // AC):
                    at = slot()[0:R, 0:NT * AC].rearrange("p (j d) -> p j d", d=AC)
                    for f in range(KD):
                        bank = v.take(pe)
                        for j in range(NT):
                            mm = pe.matmul(bank[:, 0:AC], src[:, j, f * P:(f + 1) * P], at[:, j, :],
                                           start=(j == 0), stop=(j == NT - 1))
                        mm.then_inc(v_full, 1)
                    slot_done()

            def router():
                bank = v.take(pe)
                for i in range(NT):
                    for k in range(KD):
                        mm = pe.matmul(bank[0:R, i * E:(i + 1) * E], cols(B2)[:, k, i * R:(i + 1) * R],
                                       gate_sb[:, k, :], start=(k == 0), stop=(k == KD - 1))
                mm.then_inc(v_full, 1)

            def experts(layer, blocks, tiles, r, hidden, xbuf):
                wid, mt = tiles * r, hidden // P
                xe = xbuf[:, 0:2 * SLOT].rearrange("p (b t d) -> p b t d", b=2, d=D)
                xeT = B2[:, 0:2 * KD * CAPR].rearrange("p (b k t) -> p b k t", b=2, k=KD)
                hT = B2[:, 2 * KD * CAPR:2 * KD * CAPR + 8 * CAPR].rearrange("p (b k t) -> p b k t", b=2, k=4)
                for b in range(blocks):
                    done = 16 * (4 * 4 * layer + tiles * (b // 2 + 1))
                    pe.wait_ge(xe_full[b % 2], done)
                    for k in range(KD):
                        ring = (v, s)[k % 2]
                        bank = ring.take(pe)
                        for t in range(tiles):
                            mm = pe.transpose(bank[:, t * r:(t + 1) * r], xe[0:r, b % 2, t, k * P:(k + 1) * P],
                                              ident[0:r, 0:r])
                        mm.then_inc(ring.full, 1)
                    gather_end[layer, b] = (s_full, s.n)
                    pe.wait_ge(v_free, v.n)
                    pe.wait_ge(s_free, s.n)
                    if layer == 0:
                        wg = slot().rearrange("p (k n) -> p k n", k=KD)
                        wu = slot().rearrange("p (k n) -> p k n", k=KD)
                    else:
                        w12 = slot().rearrange("p (k n) -> p k n", k=KD)
                        wg, wu = w12[:, :, 0:hidden], w12[:, :, hidden:2 * hidden]
                    for m in range(mt):
                        for ring, w in ((s, wg), (v, wu)):
                            bank = ring.take(pe)
                            for k in range(KD):
                                mm = pe.matmul(bank[:, 0:wid], w[:, k, m * P:(m + 1) * P], xeT[:, b % 2, k, 0:wid],
                                               start=(k == 0), stop=(k == KD - 1))
                            mm.then_inc(ring.full, 1)
                        up_at[layer, b * mt + m] = v.n
                    slot_done(2 if layer == 0 else 1)
                    wd = slot()[:, 0:mt * D].rearrange("p (k n) -> p k n", k=mt)
                    pe.wait_ge(v_free, v.n)
                    for t in range(tiles):
                        for ring, n0 in ((v, 0), (s, HALF)):
                            bank = ring.take(pe)
                            for k in range(mt):
                                mm = pe.matmul(bank[0:r, :], hT[:, b % 2, k, t * r:(t + 1) * r],
                                               wd[:, k, n0:n0 + HALF], start=(k == 0), stop=(k == mt - 1))
                            mm.then_inc(ring.full, 1)
                    slot_end.append((s_full, s.n))

            pe.wait_ge(consts, 8)
            pe.wait_ge(key_ready, 1)
            keyf = B1[:, 0:GROUPS]
            for g in range(GROUPS // 4):
                bank = v.take(pe)
                for q in range(4):
                    mm = pe.matmul(bank[:, q * P:(q + 1) * P], keyf[:, 4 * g + q:4 * g + q + 1].to_broadcast([P, P]),
                                   ident[:, :], start=True, stop=True)
                mm.then_inc(v_full, 1)

            mark["ln1"] = (v.n, s.n)
            turn_rows(rows(B3), xn_ready, 0)
            pe.wait_ge(v_free, v.n)
            pe.wait_ge(s_free, s.n)
            linear_rows([cols(B2)])
            for which in range(2):
                for n in range(2 * NT + 1):
                    if n < 2 * NT:
                        if n % NT == 0:
                            w = slot().rearrange("p (k n) -> p k n", k=KD)
                        rows_group(v.take(pe), [(cols(B2), w)], n % NT).then_inc(v_full, 1)
                        if n % NT == NT - 1:
                            slot_done()
                            bias_end.append(v.n)
                    if n >= 1:
                        m = n - 1
                        pe.wait_ge(qn_done, 2 * NT * which + m + 1)
                        bank = s.take(pe)
                        for k in range(4):
                            mm = pe.transpose(bank[:, k * R:(k + 1) * R], RB[0:R, m % 2, k * P:(k + 1) * P],
                                              ident[0:R, 0:R])
                        mm.then_inc(s_full, 1)
                pe.wait_ge(s_free, s.n)
                if which == 0:
                    pe.wait_ge(pt_in, 16)
                    pe.wait_ge(ones_col, 1)
                    mark["kp"] = v.n
                    for n in range(NH * NT + 2):
                        if n < NH * NT:
                            h, i = divmod(n, NT)
                            half = slice(64 * (h % 2), 64 * (h % 2) + 64)
                            pe.matmul(v.take(pe)[0:R, 0:F0], cols(B3)[half, h // 2, i * R:(i + 1) * R],
                                      PT[half, h // 2, :], start=True, stop=True).then_inc(v_full, 1)
                        if n >= 2:
                            m = n - 2
                            h, i = divmod(m, NT)
                            pe.wait_ge(v_free, mark["kp"] + m + 1)
                            if i == 0 and h >= 2:
                                pe.wait_ge(kv_free, h - 1)
                            at = i * NH + h
                            for f in range(2):
                                mm = pe.matmul(PA[:, h % 2, f * P:(f + 1) * P].rearrange("p (c d) -> p c d", c=2),
                                               RB[0:R, m % 4, f * P:(f + 1) * P],
                                               v_heads[:, at:161:160 - at, :],
                                               start=(i == 0 and f == 0), stop=(i == NT - 1),
                                               skip_group_check=True)
                            mm.then_inc(kp_used, 1)
            mark["qp"] = v.n
            pe.wait_ge(kv_free, NH)
            for n in range(NH * 6 + 2):
                if n < NH * 6:
                    h, c, f = n // 6, n // 2 % 3, n % 2
                    c0, cn = CH[c]
                    half = slice(64 * (h % 2), 64 * (h % 2) + 64)
                    pe.matmul(v.take(pe)[:, 0:cn], PT[half, h // 2, f * P:(f + 1) * P],
                              cols(B3)[half, h // 2, c0:c0 + cn], start=True, stop=True).then_inc(v_full, 1)
                if n >= 2:
                    m = n - 2
                    h, c, f = m // 6, m // 2 % 3, m % 2
                    pe.wait_ge(v_free, mark["qp"] + m + 1)
                    if f == 0 and m // 2 >= 2:
                        pe.wait_ge(acc_free, m // 2 - 1)
                    pe.matmul(PA[:, m // 2 % 2, 0:CH[c][1]], KV[:, h, f, :], RB[:, m % 3, 0:CH[c][1]],
                              start=(f == 0), stop=(f == 1)).then_inc(qp_used, 1)
            pe.wait_ge(acc_free, NH * 3)
            linear_rows([cols(B1)])

            mark["deg"] = v.n
            for c in range(T // AC):
                at = slot()[0:R, 0:NT * AC].rearrange("p (j d) -> p j d", d=AC)
                bank = v.take(pe)
                for j in range(NT):
                    mm = pe.matmul(bank[:, 0:AC], ones[0:R, :], at[:, j, :], start=(j == 0), stop=(j == NT - 1))
                mm.then_inc(v_full, 1)
                slot_done()
            pe.wait_ge(v_free, v.n)
            for g in range(3):
                bank = v.take(pe)
                for q in range(min(4, NT - 4 * g)):
                    i = 4 * g + q
                    mm = pe.transpose(bank[0:R, q * P:(q + 1) * P], rbf[:, i * R:(i + 1) * R], ident[:, :])
                mm.then_inc(v_full, 1)
            mark["deg_turned"] = v.n
            linear_rows([cols(B2)], bias=False)
            pe.wait_ge(v_free, v.n)
            for c in range(T // AC):
                at = slot()[0:R, 0:NT * AC].rearrange("p (j d) -> p j d", d=AC)
                for t in range(2):
                    for half in range(2):
                        bank = v.take(pe)
                        for j in range(NT):
                            mm = pe.matmul(bank[0:R, :], at[:, j, t * R:(t + 1) * R],
                                           rows(B1)[:, j, half * HALF:(half + 1) * HALF],
                                           start=(j == 0), stop=(j == NT - 1))
                        mm.then_inc(v_full, 1)
                slot_done()
            bias_end.extend([v.n + 1, v.n + 1])

            turn_rows(rows(B1), xn_ready, NT)
            pe.wait_ge(v_free, v.n)
            pe.wait_ge(s_free, s.n)
            pe.wait_ge(gate_in, 16)
            router()
            mark["router0"] = v.n
            pe.wait_ge(gates_ready, 1)
            gts = rbf[0:R, 1024:1024 + 3 * NT * E].rearrange("p (a i e) -> p a i e", a=3, e=E)
            for a in range(3):
                for g in range(3):
                    bank = v.take(pe)
                    for q in range(min(4, NT - 4 * g)):
                        mm = pe.transpose(bank[0:E, q * R:(q + 1) * R], gts[:, a, 4 * g + q, :], ident[0:R, 0:R])
                    mm.then_inc(v_full, 1)
            pe.wait_ge(v_free, v.n)
            gT = B2[0:E, 0:3 * T].rearrange("p (a t) -> p a t", t=T)
            mark["rank"] = v.n
            for n in range(2 * NT):
                k, i = divmod(n, NT)
                for c0 in range(0, T, HALF):
                    cn = min(HALF, T - c0)
                    pe.matmul(v.take(pe)[0:R, 0:cn], gT[:, 1 + k, i * R:(i + 1) * R], gT[:, 0, c0:c0 + cn],
                              start=True, stop=True).then_inc(v_full, 1)
            mark["ffn0"] = (v.n, s.n)
            experts(0, E, 4, CAPR // 4, 512, B1)

            turn_rows(rows(B1), xn_ready, 2 * NT)
            pe.wait_ge(v_free, v.n)
            pe.wait_ge(s_free, s.n)
            linear_rows([cols(B2)])
            pe.wait_ge(small_in, 32)
            linear_cols(cols(B2))
            pe.wait_ge(v_free, v.n)
            pe.wait_ge(pt_in, 32)
            pbd = PT[:, :, 0:P]
            mark["kp1"] = v.n
            for n in range(2 * NT + 2):
                if n < 2 * NT:
                    i, half = divmod(n, 2)
                    bank = v.take(pe)
                    for q in range(4):
                        pr = 4 * half + q
                        mm = pe.matmul(bank[0:R, q * P:(q + 1) * P], cols(B3)[:, pr, i * R:(i + 1) * R],
                                       pbd[:, pr, :], start=True, stop=True)
                    mm.then_inc(v_full, 1)
                if n >= 2:
                    m = n - 2
                    i, half = divmod(m, 2)
                    pe.wait_ge(v_free, mark["kp1"] + m + 1)
                    for q in range(4):
                        pr = 4 * half + q
                        mm = pe.matmul(PA[:, half, q * P:(q + 1) * P], RB[0:R, m % 4, q * P:(q + 1) * P],
                                       rows(B1)[:, i, pr * P:(pr + 1) * P], start=(i == 0 and q == 0),
                                       stop=(i == NT - 1), skip_group_check=True)
                    mm.then_inc(kp_used, 1)
            linear_cols(cols(B2))
            pe.wait_ge(v_free, v.n)
            pe.wait_ge(kvbd_ready, NH)
            mark["qp1"] = v.n
            kvbd = KV[:, :, :, :].rearrange("p h f d -> p (h f) d")
            for n in range(3 * KD + 2):
                if n < 3 * KD:
                    pr, c = divmod(n, 3)
                    c0, cn = CH[c]
                    pe.matmul(v.take(pe)[:, 0:cn], pbd[:, pr, :], cols(B3)[:, pr, c0:c0 + cn],
                              start=True, stop=True).then_inc(v_full, 1)
                if n >= 2:
                    m = n - 2
                    pr, c = divmod(m, 3)
                    pe.wait_ge(v_free, mark["qp1"] + m + 1)
                    pe.matmul(s.take(pe)[:, 0:CH[c][1]], kvbd[:, pr, :], RB[:, m % 4, 0:CH[c][1]],
                              start=True, stop=True).then_inc(s_full, 1)
            pe.wait_ge(s_free, s.n)
            mark["qp1_s"] = s.n
            linear_rows([cols(B1)])
            mark["wo1"] = v.n

            pe.wait_ge(xn_back, 16)
            neighbours_cols(rows(B1))
            pe.wait_ge(v_free, v.n)
            linear_rows([cols(B2), cols(B3)])
            turn_rows(rows(B1), h1_ready, 0)
            neighbours_cols(rows(B1))
            mark["agg2"] = v.n
            pe.wait_ge(v_free, v.n)
            pe.wait_ge(s_free, s.n)
            linear_rows([cols(B2), cols(B3)])
            mark["sage"] = v.n

            turn_rows(rows(B3), xn_ready, 3 * NT)
            pe.wait_ge(v_free, v.n)
            pe.wait_ge(s_free, s.n)
            pe.wait_ge(rg1_in, 16)
            router()
            mark["router1"] = v.n
            pe.wait_ge(gates_ready, 2)
            bank = v.take(pe)
            osum = rbf[0:R, 1024:1024 + NT * E]
            pe.matmul(bank[0:R, 0:NT * E], up[0:R, 0:R], osum, start=True, stop=True)
            pe.matmul(bank[0:R, P:P + NT * E], ones[0:R, 0:R], osum, start=True, stop=True).then_inc(v_full, 1)
            mark["ffn1"] = (v.n, s.n)
            experts(1, 17, 2, P, 256, B3)

        @block.sync
        def _(sp):
            n_slot, n_bias = [0], [0]

            def weights(*parts):
                n = n_slot[0]
                n_slot[0] += 1
                if n >= NSLOT:
                    sp.wait_ge(*slot_end[n - NSLOT])
                dst, src = parts
                sp.dma_start(dst(W[:, n % NSLOT, :]), src).then_inc(w_full[n % NSLOT], 16)

            def bias(vec, half):
                n = n_bias[0]
                n_bias[0] += 1
                if n >= 2:
                    sp.wait_ge(v_free, bias_end[n - 2])
                sp.dma_start(BI[0:R, n % 2, :], vec[half * HALF:(half + 1) * HALF].partition_broadcast(R))\
                  .then_inc(b_full[n % 2], 16)

            def square(w, half):
                weights(lambda s: s.rearrange("p (k n) -> p k n", k=KD),
                        w[:, half * HALF:(half + 1) * HALF].rearrange("(k p) n -> p k n", p=P))

            def linear(w, vec=None):
                for half in range(2):
                    if vec is not None:
                        bias(vec, half)
                    square(w, half)

            def counts():
                for c in range(T // AC):
                    weights(lambda s: s[0:R, 0:NT * AC].rearrange("p (j d) -> p j d", d=AC),
                            at_rows[:, :, c * AC:(c + 1) * AC])

            x_v = A["x"].rearrange("(i p) d -> p i d", p=R)
            sp.dma_start(B1[:, 512:512 + GROUPS].bitcast(I32), A["src"]).then_inc(edges_in, 16)
            sp.dma_start(B1[:, 1024:1024 + GROUPS].bitcast(I32), A["dst"]).then_inc(edges_in, 16)
            for g in range(5):
                sp.dma_start(rows(B3)[:, 2 * g:2 * g + 2, :], x_v[:, 2 * g:2 * g + 2, :]).then_inc(x_in[g], 16)
            linear(A["L0_mix_Wv"], A["L0_mix_bv"])
            sp.dma_start(PT[:, :, :], A["L0_mix_projection"]).then_inc(pt_in, 16)
            sp.dma_start(gate_sb[:, :, :], A["L0_ffn_router_gate"].rearrange("(k p) e -> p k e", p=P))\
              .then_inc(gate_in, 16)
            sp.dma_start(bcol[:, 0, :], A["L1_mix_bk"]).then_inc(small_in, 16)
            sp.dma_start(bcol[:, 1, :], A["L1_mix_bq"]).then_inc(small_in, 16)
            linear(A["L0_mix_Wk"], A["L0_mix_bk"])
            linear(A["L0_mix_Wq"], A["L0_mix_bq"])
            linear(A["L0_mix_Wo"], A["L0_mix_bo"])
            sp.wait_ge(scattered, 16 * GROUPS)
            counts()
            linear(A["L0_gnn_W"])
            bias(A["L0_gnn_b"], 0)
            bias(A["L0_gnn_b"], 1)
            counts()
            for e in range(E):
                for w in (A["L0_ffn_gate_w"], A["L0_ffn_up_w"]):
                    weights(lambda s: s.rearrange("p (k n) -> p k n", k=KD),
                            w[e].rearrange("(k p) n -> p k n", p=P))
                weights(lambda s: s.rearrange("p (k n) -> p k n", k=4),
                        A["L0_ffn_down_w"][e].rearrange("(k p) n -> p k n", p=P))
            linear(A["L1_mix_Wv"], A["L1_mix_bv"])
            sp.wait_ge(v_full, mark["router0"])
            sp.dma_start(gate_sb[:, :, :], A["L1_ffn_gate_w"].rearrange("(k p) e -> p k e", p=P)).then_inc(rg1_in, 16)
            sp.dma_start(PT[:, :, 0:P], A["L1_mix_P"]).then_inc(pt_in, 16)
            linear(A["L1_mix_Wk"])
            linear(A["L1_mix_Wq"])
            linear(A["L1_mix_Wo"], A["L1_mix_bo"])
            sp.wait_ge(v_full, mark["wo1"])
            sp.wait_ge(xn_stored, 16 * 2 * NT)
            sp.dma_start(rows(B1)[:, :, :], xn_d.rearrange("(i p) d -> p i d", p=R)).then_inc(xn_back, 16)
            counts()
            for ws, wn, b, again in (("L1_gnn_W_self0", "L1_gnn_W_neigh0", "L1_gnn_b0", True),
                                     ("L1_gnn_W_self1", "L1_gnn_W_neigh1", "L1_gnn_b1", False)):
                for half in range(2):
                    bias(A[b], half)
                    square(A[ws], half)
                    square(A[wn], half)
                if again:
                    counts()
            sp.wait_ge(eblk_ready, 1)
            for b in range(17):
                e = sp.value_load(eblk[0:1, b:b + 1], min_val=0, max_val=E - 1)
                weights(lambda s: s.rearrange("p (a k n) -> p a k n", a=1, k=KD),
                        A["L1_ffn_w12"][bass.DynSlice(e, 1)].rearrange("a (k p) n -> p a k n", p=P))
                weights(lambda s: s[:, 0:2 * D].rearrange("p (a k n) -> p a k n", a=1, k=2),
                        A["L1_ffn_w3"][bass.DynSlice(e, 1)].rearrange("a (k p) n -> p a k n", p=P))
            for i in range(NT):
                sp.wait_ge(yg_used, 2 * NT + 2 * (i + 1))
                sp.dma_start(out[i * R:(i + 1) * R, :], rows(B1)[:, i, :]).then_inc(out_stored, 16)
            sp.wait_ge(out_stored, 16 * NT)

        @block.gpsimd
        def _(pool):
            p = Chain(pool, pl)
            pool.memset(ident[:, :], 0.0).then_inc(consts, 1)
            pool.memset(ones[:, :], 1.0).then_inc(consts, 1)
            pool.iota(tok[:, :], [[R, NT]], base=0, channel_multiplier=1).then_inc(consts, 1)
            pool.iota(iot8[:, :], [[1, E]], base=0, channel_multiplier=0,
                      allow_small_or_imprecise_dtypes=True).then_inc(consts, 1)
            pool.wait_ge(consts, 4)
            pool.affine_select(out=ident[:, :], in_=ident[:, :], compare_op=ALU.not_equal, fill=1.0, base=0,
                               pattern=[[-1, P]], channel_multiplier=1).then_inc(consts, 1)
            pool.affine_select(out=low[:, :], in_=ones[:, :], compare_op=ALU.is_gt, fill=0.0, base=0,
                               pattern=[[-1, P]], channel_multiplier=1).then_inc(consts, 1)
            pool.affine_select(out=up[:, :], in_=ones[:, :], compare_op=ALU.is_gt, fill=0.0, base=0,
                               pattern=[[1, P]], channel_multiplier=-1).then_inc(consts, 1)
            pool.iota(dumpc[:, :], [[0, 1]], base=DUMP, channel_multiplier=1,
                      allow_small_or_imprecise_dtypes=True).then_inc(consts, 1)
            pool.wait_ge(table_zero, 16 * 5)
            pool.wait_ge(eidx_ready, 2)
            for g in range(GROUPS):
                if g:
                    pool.wait_ge(scattered, 16 * g)
                pool.indirect_dma_start(out=at_d, out_offset=bass.IndirectOffsetOnAxis(ap=eidx[:, g:g + 1], axis=0),
                                        in_=ecnt[:, g:g + 1], in_offset=None, compute_op=ALU.add)\
                    .then_inc(scattered, 16)

            for layer in range(2):
                blocks, tiles, r = ((E, 4, CAPR // 4), (17, 2, P))[layer]
                xbuf = (B1, B3)[layer]
                xe = xbuf[:, 0:2 * SLOT].rearrange("p (b t d) -> p b t d", b=2, d=D)
                ntile = blocks * tiles
                pool.wait_ge(route_ready, 2 * layer + 2)
                for n in range(2 * NT):
                    k, i = divmod(n, NT)
                    pool.indirect_dma_start(out=slots_d[layer],
                                            out_offset=bass.IndirectOffsetOnAxis(ap=sidx[0:R, k, i:i + 1], axis=0),
                                            in_=tok[0:R, i:i + 1], in_offset=None).then_inc(ids_scat, 16)
                pool.wait_ge(ids_scat, 16 * 2 * NT * (layer + 1))
                with nc.allow_non_contiguous_dma(reason="a few thousand token numbers, turned"):
                    pool.dma_start(tidx[0:r, 0:ntile].unsqueeze(2),
                                   slots_d[layer][0:ntile * r, :].rearrange("(b p) o -> p b o", p=r))\
                        .then_inc(ids_in, 16)
                pool.wait_ge(ids_in, 16 * (layer + 1))
                pool.wait_ge(xn_stored, 16 * NT * (1 if layer == 0 else 3))
                for b in range(blocks):
                    if b >= 2:
                        pool.wait_ge(*gather_end[layer, b - 2])
                    for t in range(tiles):
                        c = b * tiles + t
                        pool.indirect_dma_start(out=xe[0:r, b % 2, t, :], out_offset=None, in_=xn_d,
                                                in_offset=bass.IndirectOffsetOnAxis(ap=tidx[0:r, c:c + 1], axis=0))\
                            .then_inc(xe_full[b % 2], 16)
                y0 = ntile // 2 if layer == 0 else 16 + ntile // 2
                pool.wait_ge(y_st[0], 16 * y0)
                pool.wait_ge(y_st[1], 16 * y0)
                for n in range(2 * NT):
                    i, k = divmod(n, 2)
                    if n >= 4:
                        pool.wait_ge(yg_used, 2 * NT * layer + n - 3)
                    pool.indirect_dma_start(out=xbuf[0:R, (n % 4) * D:(n % 4 + 1) * D], out_offset=None,
                                            in_=y_d[layer],
                                            in_offset=bass.IndirectOffsetOnAxis(ap=gidx[0:R, k, i:i + 1], axis=0))\
                        .then_inc(yg_full[n % 4], 16)

        @block.scalar
        def _(act):
            s = Bank(PS, s_full, s_free)
            n_res, n_ln = [0], [0]

            def ln_sqrt():
                var, std = rbf[0:R, 160:170], rbf[0:R, 176:186]
                n_ln[0] += 1
                act.wait_ge(ln_var, n_ln[0])
                act.activation(std, var, ACT.Sqrt).then_inc(ln_std, 1)

            def turned(dst):
                for i in range(NT):
                    act.copy(dst[:, 4:8, i * R:(i + 1) * R],
                             s.read(act)[:, 0:4 * R].rearrange("p (k t) -> p k t", t=R)).then_inc(s_free, 1)

            def residual(src):
                for m in range(2 * NT):
                    half, i = divmod(m, NT)
                    n = n_res[0]
                    n_res[0] += 1
                    if m >= 4:
                        act.wait_ge(res_used, n - 3)
                    act.dma_start(RB[0:R, m % 4, :], src[i * R:(i + 1) * R, half * HALF:(half + 1) * HALF])\
                       .then_inc(res_full[m % 4], 16)

            def store_rows(dst, src, sem_, base, done):
                for i in range(NT):
                    act.wait_ge(sem_, base + i + 1)
                    act.dma_start(dst[i * R:(i + 1) * R, :], src[:, i, :]).then_inc(done, 16)

            def experts(layer, blocks, tiles, r, hidden, xbuf):
                wid, mt = tiles * r, hidden // P
                xeT = B2[:, 0:2 * KD * CAPR].rearrange("p (b k t) -> p b k t", b=2, k=KD)
                ysb = xbuf[:, 2 * SLOT:2 * SLOT + 2 * D].rearrange("p (b d) -> p b d", d=D)
                for b in range(blocks):
                    for k in range(1, KD, 2):
                        act.copy(xeT[:, b % 2, k, 0:wid], s.read(act)[:, 0:wid]).then_inc(s_free, 1)
                    for m in range(mt):
                        n = b * mt + m
                        if n >= 4:
                            act.wait_ge(v_free, up_at[layer, n - 4])
                        act.activation(RB[:, n % 4, 0:wid], s.read(act)[:, 0:wid], ACT.Silu).then_inc(s_free, 1)
                    for t in range(tiles):
                        j = b * tiles + t
                        past = 16 * (16 * layer + j // 2)
                        if past:
                            act.wait_ge(y_st[j % 2], past)
                        act.copy(ysb[0:r, j % 2, HALF:D], s.read(act)[0:r, :]).then_inc(s_free, 1)
                        act.wait_ge(s_free, s.n)
                        act.wait_ge(v_free, up_at[layer, n] + t + 1)
                        act.dma_start(y_d[layer][j * r:(j + 1) * r, :], ysb[0:r, j % 2, :]).then_inc(y_st[j % 2], 16)

            act.wait_ge(zero_ready, 1)
            zt = B2[:, 0:4352]
            for q in range(3):
                act.dma_start(at_d.rearrange("(p c) o -> p (c o)", p=P)[:, q * 4352:(q + 1) * 4352], zt)\
                   .then_inc(table_zero, 16)
            for q in range(2):
                act.dma_start(slots_d[q].rearrange("(p c) o -> p (c o)", p=P), zt[:, 0:49].bitcast(I32))\
                   .then_inc(table_zero, 16)
            ln_sqrt()
            act.wait_ge(table_zero, 16 * 5)
            turned(cols(B2))
            for which in range(2):
                for n in range(2 * NT):
                    half, i = divmod(n, NT)
                    g = 2 * NT * which + n
                    act.wait_ge(v_free, mark["ln1"][0] + NT + 2 * NT + (NH * NT * which) + g + 1)
                    act.activation(RB[0:R, 2 + n % 2, :], RB[0:R, n % 2, :], ACT.Square).then_inc(sq_done, 1)
                    act.wait_ge(ss_done, g + 1)
                    act.activation(nr8[0:R, :], hs8[0:R, :], ACT.Sqrt).then_inc(nrm_done, 1)
                    act.copy(cols(B3)[:, 4 * half:4 * half + 4, i * R:(i + 1) * R],
                             s.read(act)[:, 0:4 * R].rearrange("p (k t) -> p k t", t=R)).then_inc(s_free, 1)
                if which == 0:
                    for h in range(NH):
                        act.wait_ge(kp_used, NT * (h + 1))
                        kvp = PA[:, h % 2, 0:2 * P].rearrange("p (f c d) -> p f c d", f=2, c=2)
                        dst = KV[:, h, :, :].rearrange("p f (c d) -> p f c d", c=2)
                        if h % 2 == 0:
                            act.copy(dst, kvp).then_inc(kv_free, 1)
                        else:
                            act.copy(dst[:, :, 1, :], kvp[:, :, 0, :]).then_inc(ac, 1)
                            act.copy(dst[:, :, 0, :], kvp[:, :, 1, :]).then_inc(kv_free, 1)
            act.wait_ge(acc_free, NH * 3)
            residual(A["x"])
            act.wait_ge(v_free, mark["deg"] + 5)
            act.dma_start(deg_d, rbf[0:1, 0:T]).then_inc(deg_stored, 16)
            act.wait_ge(dg_in, 1)
            act.activation(dinv[0:R, :], dcol[0:R, :], ACT.Sqrt).then_inc(dg_sqrt, 1)
            ln_sqrt()
            store_rows(xn_d, rows(B1), xn_ready, NT, xn_stored)
            turned(cols(B2))
            pe_ = rbf[0:R, 512:512 + NT * E]
            act.wait_ge(sm_in, 1)
            act.activation(pe_, pe_, ACT.Exp).then_inc(sm_exp, 1)
            experts(0, E, 4, CAPR // 4, 512, B1)
            ln_sqrt()
            store_rows(x2_d, rows(B3), yg_used, NT, x2_stored)
            store_rows(xn_d, rows(B1), xn_ready, 2 * NT, xn_stored)
            turned(cols(B2))
            for m in range(3 * KD):
                pr, c = divmod(m, 3)
                c0, cn = CH[c]
                act.copy(cols(B1)[:, pr, c0:c0 + cn], s.read(act)[:, 0:cn]).then_inc(s_free, 1)
            act.wait_ge(x2_stored, 16 * NT)
            residual(x2_d)
            for m in range(2 * NT):
                half, i = divmod(m, NT)
                act.wait_ge(res_used, 2 * NT + m + 1)
                act.dma_start(xm_d[i * R:(i + 1) * R, half * HALF:(half + 1) * HALF],
                              rows(B3)[:, i, half * HALF:(half + 1) * HALF]).then_inc(xm_stored, 16)
            act.wait_ge(deg_stored, 16)
            act.dma_start(rbf[:, 0:T], deg_d[0, :].partition_broadcast(P)).then_inc(dinv_in, 16)
            turned(cols(B2))
            act.wait_ge(xm_stored, 16 * 2 * NT)
            act.wait_ge(v_free, mark["agg2"])
            residual(xm_d)
            ln_sqrt()
            store_rows(xn_d, rows(B3), xn_ready, 3 * NT, xn_stored)
            turned(cols(B2))
            act.wait_ge(sm_in, 2)
            d2 = rbf[0:R, 512:512 + NT]
            act.activation(d2, d2, ACT.Exp).then_inc(sm_exp, 1)
            experts(1, 17, 2, P, 256, B3)

        @block.vector
        def _(ve):
            d = Chain(ve, dv)
            v = Bank(PV, v_full, v_free)
            n_bias, n_res, n_ln = [0], [0], [0]

            def bias():
                n = n_bias[0]
                n_bias[0] += 1
                ve.wait_ge(b_full[n % 2], 16 * (n // 2 + 1))
                return BI[0:R, n % 2, :]

            def emptied(ins):
                ins.then_inc(v_free, 1)

            def layer_norm(x, xn, first=False):
                st = rbf[0:R, 0:120].rearrange("p (i c s) -> p i c s", i=NT, c=2)
                mv = rbf[0:R, 128:148].rearrange("p (i s) -> p i s", s=2)
                var, std, rstd = rbf[0:R, 160:170], rbf[0:R, 176:186], rbf[0:R, 192:202]
                n_ln[0] += 1
                d.sync()
                for i in range(NT):
                    if first and i % 2 == 0:
                        ve.wait_ge(x_in[i // 2], 16)
                    for c in range(2):
                        d(ve.bn_stats(st[:, i, c, :], x[:, i, c * HALF:(c + 1) * HALF]))
                d.sync()
                for i in range(NT):
                    d(ve.bn_aggr(mv[:, i, :], st[:, i, :, :]))
                d.sync()
                ve.tensor_scalar(var, mv[:, :, 1], 1e-5, None, ALU.add).then_inc(ln_var, 1)
                ve.wait_ge(ln_std, n_ln[0])
                d(ve.reciprocal(rstd, std))
                d.sync()
                for i in range(NT):
                    ve.tensor_scalar(xn[:, i, :], x[:, i, :], mv[:, i, 0:1], rstd[:, i:i + 1],
                                     ALU.subtract, ALU.mult).then_inc(xn_ready, 1)

            def turned(dst):
                for i in range(NT):
                    emptied(ve.tensor_copy(dst[:, 0:4, i * R:(i + 1) * R],
                                           v.read(ve)[:, 0:4 * R].rearrange("p (k t) -> p k t", t=R)))

            def add_residual(dst):
                for half in range(2):
                    bi = bias()
                    for i in range(NT):
                        m = half * NT + i
                        o = dst[:, i, half * HALF:(half + 1) * HALF]
                        emptied(ve.tensor_tensor(o, v.read(ve)[0:R, :], bi, ALU.add))
                        ve.wait_ge(v_free, v.n)
                        ve.wait_ge(res_full[m % 4], 16 * (5 * n_res[0] + m // 4 + 1))
                        ve.tensor_tensor(o, o, RB[0:R, m % 4, :], ALU.add).then_inc(res_used, 1)
                n_res[0] += 1
                ve.wait_ge(res_used, 2 * NT * n_res[0])

            def experts(layer, blocks, tiles, r, hidden, xbuf, res):
                wid, mt = tiles * r, hidden // P
                xeT = B2[:, 0:2 * KD * CAPR].rearrange("p (b k t) -> p b k t", b=2, k=KD)
                hT = B2[:, 2 * KD * CAPR:2 * KD * CAPR + 8 * CAPR].rearrange("p (b k t) -> p b k t", b=2, k=4)
                ysb = xbuf[:, 2 * SLOT:2 * SLOT + 2 * D].rearrange("p (b d) -> p b d", d=D)
                s_n = mark[f"ffn{layer}"][1]
                for b in range(blocks):
                    for k in range(0, KD, 2):
                        emptied(ve.tensor_copy(xeT[:, b % 2, k, 0:wid], v.read(ve)[:, 0:wid]))
                    s_n += KD // 2
                    for m in range(mt):
                        s_n += 1
                        bank = v.read(ve)
                        ve.wait_ge(s_free, s_n)
                        emptied(ve.tensor_tensor(hT[:, b % 2, m, 0:wid], bank[:, 0:wid],
                                                 RB[:, (b * mt + m) % 4, 0:wid], ALU.mult))
                    for t in range(tiles):
                        s_n += 1
                        j = b * tiles + t
                        past = 16 * (16 * layer + j // 2)
                        if past:
                            ve.wait_ge(y_st[j % 2], past)
                        emptied(ve.tensor_copy(ysb[0:r, j % 2, 0:HALF], v.read(ve)[0:r, :]))
                for n in range(2 * NT):
                    i, k = divmod(n, 2)
                    ve.wait_ge(yg_full[n % 4], 16 * (5 * layer + n // 4 + 1))
                    if k:
                        ve.wait_ge(yg_used, 2 * NT * layer + n)
                    ve.scalar_tensor_tensor(out=res[:, i, :], in0=xbuf[0:R, (n % 4) * D:(n % 4 + 1) * D],
                                            scalar=wk[0:R, k, i:i + 1], in1=res[:, i, :],
                                            op0=ALU.mult, op1=ALU.add).then_inc(yg_used, 1)
                ve.wait_ge(yg_used, 2 * NT * (layer + 1))

            small = {}

            def sm(name, n, at):
                small[name] = rbf[0:R, at:at + n]
                return small[name]

            def top2(val):
                mx = sm("mx", NT * E, 1280).rearrange("p (i e) -> p i e", e=E)
                mi = rbf[0:R, 1376:1376 + NT * E].bitcast(U32).rearrange("p (i e) -> p i e", e=E)
                ek = sm("ek", 2 * NT, 1472).rearrange("p (k i) -> p k i", k=2)
                for i in range(NT):
                    d(ve.max(mx[:, i, :], val[:, i, :]))
                d.sync()
                for i in range(NT):
                    d(ve.max_index(mi[:, i, :], mx[:, i, :], val[:, i, :]))
                d.sync()
                d(ve.tensor_copy(ek, mi[:, :, 0:2].rearrange("p i k -> p k i")))
                d.sync()
                return mx, ek

            def onehots(o, ek, k):
                d(ve.tensor_tensor(o, iot8[0:R, :].unsqueeze(1).to_broadcast([R, NT, E]),
                                   ek[:, k, :].unsqueeze(2).to_broadcast([R, NT, E]), ALU.is_equal))

            keyf, first = B1[:, 0:GROUPS], B1[:, 256:256 + GROUPS]
            srcf, dstf = B1[:, 512:512 + GROUPS], B1[:, 1024:1024 + GROUPS]
            srcc = B1[:, 1536:1536 + GROUPS]
            ve.memset(B2[:, 0:4352], 0.0).then_inc(zero_ready, 1)
            ve.wait_ge(edges_in, 32)
            d(ve.tensor_copy(srcc, srcf.bitcast(I32)))
            d(ve.tensor_copy(keyf, dstf.bitcast(I32)))
            d.sync()
            ve.scalar_tensor_tensor(out=keyf, in0=srcc, scalar=float(T), in1=keyf, op0=ALU.mult, op1=ALU.add)\
              .then_inc(key_ready, 1)
            ve.wait_ge(key_ready, 1)
            ve.wait_ge(consts, 8)
            for g in range(GROUPS // 4):
                k4 = slice(4 * g, 4 * g + 4)
                eq = RB[:, 0, :].rearrange("p (q c) -> p q c", q=4)
                eql = RB[:, 1, :].rearrange("p (q c) -> p q c", q=4)
                bank = v.read(ve)
                d.sync()
                emptied(ve.tensor_tensor(eq, bank.rearrange("p (q c) -> p q c", q=4),
                                         keyf[:, k4].unsqueeze(2).to_broadcast([P, 4, P]), ALU.is_equal))
                ve.wait_ge(v_free, v.n)
                d(ve.tensor_reduce(ecnt[:, k4], eq, AX, ALU.add))
                d(ve.tensor_tensor(eql, eq, low[:, :].unsqueeze(1).to_broadcast([P, 4, P]), ALU.mult))
                d.sync()
                d(ve.tensor_reduce(first[:, k4], eql, AX, ALU.add))
            d.sync()
            d(ve.tensor_scalar(first, first, 0.0, None, ALU.is_equal))
            d.sync()
            ve.tensor_tensor(ecnt[:, :], ecnt[:, :], first, ALU.mult).then_inc(eidx_ready, 1)
            d(ve.scalar_tensor_tensor(out=srcc, in0=keyf, scalar=dumpc[:, 0:1], in1=first,
                                      op0=ALU.subtract, op1=ALU.mult))
            d.sync()
            ve.tensor_scalar(eidx[:, :], srcc, dumpc[:, 0:1], None, ALU.add).then_inc(eidx_ready, 1)

            layer_norm(rows(B3), rows(B3), first=True)
            ve.wait_ge(table_zero, 16 * 5)
            turned(cols(B2))
            ve.memset(v_heads[:, 160, :], 1.0).then_inc(ones_col, 1)
            for half in range(2):
                bi = bias()
                for i in range(NT):
                    emptied(ve.tensor_tensor(rows(B1)[:, i, half * HALF:(half + 1) * HALF], v.read(ve)[0:R, :], bi,
                                             ALU.add))
            turns = mark["ln1"][1] + NT
            for which in range(2):
                for n in range(2 * NT):
                    g = 2 * NT * which + n
                    if n % NT == 0:
                        bi = bias()
                    t, sq = RB[0:R, n % 2, :], RB[0:R, 2 + n % 2, :]
                    t8 = t.rearrange("p (h e) -> p h e", e=HD)
                    if n >= 2:
                        ve.wait_ge(s_full, turns + g - 1)
                    emptied(ve.tensor_tensor(t, v.read(ve)[0:R, :], bi, ALU.add))
                    ve.wait_ge(sq_done, g + 1)
                    ve.tensor_reduce(hs8[0:R, :], sq.rearrange("p (h e) -> p h e", e=HD), AX, ALU.add)\
                      .then_inc(ss_done, 1)
                    ve.wait_ge(nrm_done, g + 1)
                    d(ve.tensor_scalar(nr8[0:R, :], nr8[0:R, :], 1e-8, None, ALU.add))
                    d.sync()
                    d(ve.reciprocal(nr8[0:R, :], nr8[0:R, :]))
                    d.sync()
                    ve.tensor_tensor(t8, t8, nr8[0:R, :].unsqueeze(2).to_broadcast([R, 8, HD]), ALU.mult)\
                      .then_inc(qn_done, 1)
                if which == 0:
                    for n in range(NH * NT):
                        if n >= 4:
                            ve.wait_ge(kp_used, n - 3)
                        emptied(ve.tensor_scalar(RB[0:R, n % 4, 0:F0], v.read(ve)[0:R, 0:F0], 0.0, 0.1,
                                                 ALU.max, ALU.add))

            def attend(m):
                h, c = divmod(m, 3)
                c0, cn = CH[c]
                num = slice(64 * (h % 2), 64 * (h % 2) + 64)
                den = slice(64 - 64 * (h % 2), 128 - 64 * (h % 2))
                acc = PA[:, m % 2, :]
                rd = RB[num, 3, 0:cn]
                ve.wait_ge(qp_used, 2 * (m + 1))
                if m:
                    ve.wait_ge(acc_free, m)
                d(ve.tensor_scalar(rd, acc[den, 0:cn], 1e-6, None, ALU.max))
                d.sync()
                d(ve.reciprocal(rd, rd))
                d.sync()
                ve.tensor_tensor(cols(B1)[num, h // 2, c0:c0 + cn], acc[num, 0:cn], rd, ALU.mult).then_inc(acc_free, 1)

            for n in range(NH * 6):
                cn = CH[n // 2 % 3][1]
                if n >= 3:
                    ve.wait_ge(qp_used, n - 2)
                emptied(ve.tensor_scalar(RB[:, n % 3, 0:cn], v.read(ve)[:, 0:cn], 0.0, 0.1, ALU.max, ALU.add))
                if n >= 3 and n % 2 == 1:
                    attend((n - 3) // 2)
            attend(NH * 3 - 1)
            add_residual(rows(B3))

            for c in range(T // AC):
                emptied(ve.tensor_copy(rbf[:, c * AC:(c + 1) * AC], v.read(ve)[:, 0:AC]))
            for g in range(3):
                nq = min(4, NT - 4 * g)
                emptied(ve.tensor_copy(dcol[0:R, 4 * g:4 * g + nq],
                                       v.read(ve)[0:R, 0:nq * P].rearrange("p (q c) -> p q c", c=P)[:, :, 0]))
            ve.wait_ge(v_free, v.n)
            ve.tensor_scalar(dcol[0:R, :], dcol[0:R, :], 1.0, None, ALU.add).then_inc(dg_in, 1)
            ve.wait_ge(dg_sqrt, 1)
            d(ve.reciprocal(dinv[0:R, :], dinv[0:R, :]))
            d.sync()
            for half in range(2):
                for i in range(NT):
                    emptied(ve.tensor_scalar(rows(B1)[:, i, half * HALF:(half + 1) * HALF], v.read(ve)[0:R, :],
                                             dinv[0:R, i:i + 1], None, ALU.mult))
            ve.wait_ge(deg_stored, 16)
            bis = [bias(), bias()]
            for i in range(NT):
                for half in range(2):
                    hc = slice(half * HALF, (half + 1) * HALF)
                    t = RB[0:R, (2 * i + half) % 4, :]
                    emptied(ve.tensor_tensor(t, v.read(ve)[0:R, :], rows(B1)[:, i, hc], ALU.add))
                    ve.wait_ge(v_free, v.n)
                    d(ve.scalar_tensor_tensor(out=t, in0=t, scalar=dinv[0:R, i:i + 1], in1=bis[half],
                                              op0=ALU.mult, op1=ALU.add))
                    d.sync()
                    d(ve.scalar_tensor_tensor(out=rows(B3)[:, i, hc], in0=t, scalar=0.0, in1=rows(B3)[:, i, hc],
                                              op0=ALU.max, op1=ALU.add))
            bias_last = v.n

            layer_norm(rows(B3), rows(B1))
            turned(cols(B2))
            lg = sm("lg", NT * E, 512).rearrange("p (i e) -> p i e", e=E)
            pr = sm("pr", NT * E, 608).rearrange("p (i e) -> p i e", e=E)
            z = sm("z", NT, 704)
            emptied(ve.tensor_copy(small["lg"], v.read(ve)[0:R, 0:NT * E]))
            ve.wait_ge(v_free, v.n)
            d(ve.tensor_reduce(z, lg, AX, ALU.max))
            d.sync()
            ve.tensor_tensor(lg, lg, z.unsqueeze(2).to_broadcast([R, NT, E]), ALU.subtract).then_inc(sm_in, 1)
            ve.wait_ge(sm_exp, 1)
            d(ve.tensor_reduce(z, lg, AX, ALU.add))
            d.sync()
            d(ve.reciprocal(z, z))
            d.sync()
            d(ve.tensor_tensor(pr, lg, z.unsqueeze(2).to_broadcast([R, NT, E]), ALU.mult))
            d.sync()
            mx, ek = top2(pr)
            d(ve.tensor_tensor(z, mx[:, :, 0], mx[:, :, 1], ALU.add))
            d.sync()
            d(ve.tensor_scalar(z, z, 1e-9, None, ALU.add))
            d.sync()
            d(ve.reciprocal(z, z))
            d.sync()
            gts = rbf[0:R, 1024:1024 + 3 * NT * E].rearrange("p (a i e) -> p a i e", a=3, e=E)
            for k in range(2):
                d(ve.tensor_tensor(wk[0:R, k, :], mx[:, :, k], z, ALU.mult))
                onehots(gts[:, 1 + k, :, :], ek, k)
            d.sync()
            d(ve.tensor_tensor(gts[:, 0, :, :], gts[:, 1, :, :],
                               wk[0:R, 0, :].unsqueeze(2).to_broadcast([R, NT, E]), ALU.mult))
            d(ve.tensor_tensor(pr, gts[:, 2, :, :], wk[0:R, 1, :].unsqueeze(2).to_broadcast([R, NT, E]), ALU.mult))
            d.sync()
            ve.tensor_tensor(gts[:, 0, :, :], gts[:, 0, :, :], pr, ALU.add).then_inc(gates_ready, 1)
            gT = B2[0:E, 0:3 * T].rearrange("p (a t) -> p a t", t=T)
            for a in range(3):
                for g in range(3):
                    w = min(4, NT - 4 * g) * R
                    emptied(ve.tensor_copy(gT[:, a, 4 * g * R:4 * g * R + w], v.read(ve)[0:E, 0:w]))
            rk = sm("rk", 7 * 2 * NT, 0).rearrange("p (a k i) -> p a k i", a=7, k=2)
            scr = RB[0:R, 3, :]
            scr2 = B2[0:R, 4000:4000 + HALF]
            d(ve.memset(small["rk"], 0.0))
            d.sync()
            for n in range(2 * NT):
                k, i = divmod(n, NT)
                for c0 in range(0, T, HALF):
                    cn = min(HALF, T - c0)
                    ve.wait_ge(v_free, v.n)
                    d.sync()
                    bank = v.read(ve)[0:R, :]
                    own = (i * R, (i + 1) * R)
                    c = c0 // HALF
                    g = wk[0:R, k, i:i + 1]
                    a, b = max(own[0], c0), min(own[1], c0 + cn)
                    if a < b:
                        d(ve.scalar_tensor_tensor(out=scr2[:, 0:b - a], in0=bank[:, a - c0:b - c0], scalar=g,
                                                  in1=low[0:R, a - own[0]:b - own[0]], op0=ALU.is_equal, op1=ALU.mult,
                                                  accum_out=rk[:, 5 if a > own[0] else 6, k, i:i + 1]))
                    m = min(max(own[0] - c0, 0), cn)
                    parts = [(0, m, ALU.is_ge), (m, cn, ALU.is_gt)]
                    parts = [x for x in parts if x[0] < x[1]]
                    for q, (a, b, op) in enumerate(parts):
                        dst = rk[:, c if (q == 0) else 3 + 0, k, i:i + 1]
                        ins = ve.tensor_scalar(scr[:, a:b], bank[:, a:b], g, None, op, ALU.add, accum_out=dst)
                        if q == len(parts) - 1:
                            emptied(ins)
                        else:
                            d(ins)
            d.sync()
            ve.wait_ge(v_free, v.n)
            rank = sm("rank", 2 * NT, 160).rearrange("p (k i) -> p k i", k=2)
            keep = sm("keep", 2 * NT, 192).rearrange("p (k i) -> p k i", k=2)
            slot = sm("slot", 2 * NT, 224).rearrange("p (k i) -> p k i", k=2)
            dump = sm("dump", 2 * NT, 256).rearrange("p (k i) -> p k i", k=2)
            d(ve.tensor_tensor(rank, rk[:, 0, :, :], rk[:, 1, :, :], ALU.add))
            for a in range(2, 7):
                d.sync()
                d(ve.tensor_tensor(rank, rank, rk[:, a, :, :], ALU.add))
            d.sync()
            d(ve.tensor_scalar(keep, rank, float(CAP), None, ALU.is_lt))
            d(ve.scalar_tensor_tensor(out=slot, in0=ek, scalar=float(CAPR), in1=rank, op0=ALU.mult, op1=ALU.add))
            d(ve.tensor_copy(dump[:, 0, :], tok[0:R, :]))
            d.sync()
            d(ve.tensor_scalar(dump[:, 1, :], dump[:, 0, :], float(E * CAPR + T), None, ALU.add))
            d(ve.tensor_scalar(dump[:, 0, :], dump[:, 0, :], float(E * CAPR), None, ALU.add))
            d.sync()
            d(ve.tensor_tensor(wk[0:R, :, :], wk[0:R, :, :], keep, ALU.mult))
            d(ve.tensor_tensor(rank, slot, dump, ALU.subtract))
            d.sync()
            d(ve.tensor_tensor(rank, rank, keep, ALU.mult))
            ve.tensor_tensor(gidx[0:R, :, :], slot, keep, ALU.mult).then_inc(route_ready, 1)
            d.sync()
            ve.tensor_tensor(sidx[0:R, :, :], rank, dump, ALU.add).then_inc(route_ready, 1)
            experts(0, E, 4, CAPR // 4, 512, B1, rows(B3))

            layer_norm(rows(B3), rows(B1))
            turned(cols(B2))
            ve.wait_ge(xn_stored, 16 * 2 * NT)
            for half in range(2):
                bi = bias()
                for i in range(NT):
                    emptied(ve.tensor_tensor(rows(B1)[:, i, half * HALF:(half + 1) * HALF], v.read(ve)[0:R, :], bi,
                                             ALU.add))

            ve.wait_ge(small_in, 32)
            ve.wait_ge(x2_stored, 16 * NT)

            def heads_cols(which):
                for m in range(KD):
                    for c0, cn in CH:
                        emptied(ve.tensor_scalar(cols(B3)[:, m, c0:c0 + cn], v.read(ve)[:, 0:cn],
                                                 bcol[:, which, m:m + 1], None, ALU.add))

            heads_cols(0)
            d(ve.memset(KV[:, :, :, :].rearrange("p h f d -> p (h f) d")[:, 0:KD, :], 0.0))
            for n in range(2 * NT):
                if n >= 4:
                    ve.wait_ge(kp_used, NH * NT + n - 3)
                emptied(ve.tensor_scalar(RB[0:R, n % 4, :], v.read(ve)[0:R, :], 0.0, 0.125, ALU.max, ALU.mult))
            ve.wait_ge(kp_used, NH * NT + 2 * NT)
            d.sync()
            kvbd = KV[:, :, :, :].rearrange("p h f d -> p (h f) d")
            for half in range(2):
                for q in range(4):
                    for hh in range(2):
                        b = slice(64 * hh, 64 * hh + 64)
                        ve.tensor_copy(kvbd[b, 4 * half + q, 64 * hh:64 * hh + 64],
                                       PA[b, half, q * P + 64 * hh:q * P + 64 * hh + 64]).then_inc(kvbd_ready, 1)
            heads_cols(1)
            for n in range(3 * KD):
                cn = CH[n % 3][1]
                if n >= 4:
                    ve.wait_ge(s_full, mark["qp1_s"] - 3 * KD + n - 3)
                emptied(ve.tensor_scalar(RB[:, n % 4, 0:cn], v.read(ve)[:, 0:cn], 0.0, 0.125, ALU.max, ALU.mult))
            add_residual(rows(B3))

            dg = rbf[:, 0:T]
            ve.wait_ge(dinv_in, 16)
            d(ve.tensor_scalar(dg, dg, 1.0, None, ALU.max))
            d.sync()
            d(ve.reciprocal(dg, dg))
            d.sync()
            ve.wait_ge(xm_stored, 16 * 2 * NT)

            def means():
                for c in range(T // AC):
                    for f in range(KD):
                        emptied(ve.tensor_tensor(cols(B3)[:, f, c * AC:(c + 1) * AC], v.read(ve)[:, 0:AC],
                                                 dg[:, c * AC:(c + 1) * AC], ALU.mult))

            means()
            for half in range(2):
                bi = bias()
                for i in range(NT):
                    o = rows(B1)[:, i, half * HALF:(half + 1) * HALF]
                    emptied(ve.tensor_tensor(o, v.read(ve)[0:R, :], bi, ALU.add))
                    ve.wait_ge(v_free, v.n)
                    ins = ve.tensor_scalar(o, o, 0.0, None, ALU.max)
                    if half:
                        ins.then_inc(h1_ready, 1)
                    else:
                        d(ins)
            turned(cols(B2))
            means()
            add_residual(rows(B1))

            layer_norm(rows(B1), rows(B3))
            turned(cols(B2))
            emptied(ve.tensor_copy(small["lg"], v.read(ve)[0:R, 0:NT * E]))
            ve.wait_ge(v_free, v.n)
            d(ve.tensor_copy(pr, lg))
            d.sync()
            mx, ek = top2(pr)
            d2 = rbf[0:R, 512:512 + NT]
            ve.tensor_tensor(d2, mx[:, :, 1], mx[:, :, 0], ALU.subtract).then_inc(sm_in, 1)
            ve.wait_ge(sm_exp, 2)
            d(ve.tensor_scalar(z, d2, 1.0, None, ALU.add))
            d.sync()
            d(ve.reciprocal(z, z))
            d.sync()
            d(ve.tensor_copy(wk[0:R, 0, :], z))
            d(ve.tensor_tensor(wk[0:R, 1, :], d2, z, ALU.mult))
            osum = rbf[0:R, 1024:1024 + NT * E].rearrange("p (i e) -> p i e", e=E)
            oh = [rbf[0:R, 1104 + 80 * k:1184 + 80 * k].rearrange("p (i e) -> p i e", e=E) for k in range(2)]
            for k in range(2):
                onehots(oh[k], ek, k)
            d.sync()
            ve.tensor_tensor(osum, oh[0], oh[1], ALU.add).then_inc(gates_ready, 1)
            pos = sm("pos", NT * E, 800).rearrange("p (i e) -> p i e", e=E)
            tot = sm("tot", NT * E, 896).rearrange("p (i e) -> p i e", e=E)
            bank = v.read(ve)
            d(ve.tensor_copy(small["pos"], bank[0:R, 0:NT * E]))
            emptied(ve.tensor_copy(small["tot"], bank[0:R, P:P + NT * E]))
            ve.wait_ge(v_free, v.n)
            run = sm("run", E, 720)
            nb = sm("nb", E, 736)
            cmp = sm("cmp", E, 752)
            start = sm("start", E, 768)
            d(ve.memset(run, 0.0))
            d.sync()
            for i in range(NT):
                d(ve.tensor_tensor(pos[:, i, :], pos[:, i, :], run, ALU.add))
                d.sync()
                d(ve.tensor_tensor(run, run, tot[:, i, :], ALU.add))
                d.sync()
            d(ve.tensor_scalar(nb, run, 0.0, None, ALU.is_gt))
            for j in range(1, -(-T // 256)):
                d(ve.tensor_scalar(cmp, run, 256.0 * j, None, ALU.is_gt))
                d.sync()
                d(ve.tensor_tensor(nb, nb, cmp, ALU.add))
                d.sync()
            d(ve.memset(start, 0.0))
            d.sync()
            for e in range(1, E):
                d(ve.tensor_tensor(start[:, e:e + 1], start[:, e - 1:e], nb[:, e - 1:e], ALU.add))
                d.sync()
            bl, be, bc = sm("bl", 17, 256), sm("be", 17, 288), sm("bc", 17, 320)
            d(ve.memset(be, 0.0))
            d(ve.tensor_tensor_scan(bl, ones[0:R, 0:17], ones[0:R, 0:17], -1.0, ALU.mult, ALU.add))
            d.sync()
            for e in range(1, E):
                d(ve.tensor_scalar(bc, bl, start[:, e:e + 1], None, ALU.is_ge))
                d.sync()
                d(ve.tensor_tensor(be, be, bc, ALU.add))
                d.sync()
            ve.tensor_copy(eblk[0:R, :], be).then_inc(eblk_ready, 1)
            d(ve.tensor_scalar(start, start, 256.0, None, ALU.mult))
            d.sync()
            d(ve.tensor_tensor(pos, pos, start.unsqueeze(1).to_broadcast([R, NT, E]), ALU.add))
            d.sync()
            slot = sm("slot", 2 * NT, 224).rearrange("p (k i) -> p k i", k=2)
            for k in range(2):
                d(ve.tensor_tensor(oh[k], oh[k], pos, ALU.mult))
                d.sync()
                d(ve.tensor_reduce(slot[:, k, :], oh[k], AX, ALU.add))
            d.sync()
            ve.tensor_copy(gidx[0:R, :, :], slot).then_inc(route_ready, 1)
            ve.tensor_copy(sidx[0:R, :, :], slot).then_inc(route_ready, 1)
            experts(1, 17, 2, P, 256, B3, rows(B1))


_NAMES = ['x', 'src', 'dst', 'L0_gnn_W', 'L0_gnn_b', 'L0_mix_Wq', 'L0_mix_bq', 'L0_mix_Wk', 'L0_mix_bk',
          'L0_mix_Wv', 'L0_mix_bv', 'L0_mix_Wo', 'L0_mix_bo', 'L0_mix_projection', 'L0_ffn_router_gate',
          'L0_ffn_gate_w', 'L0_ffn_up_w', 'L0_ffn_down_w', 'L1_gnn_W_self0', 'L1_gnn_W_neigh0', 'L1_gnn_b0',
          'L1_gnn_W_self1', 'L1_gnn_W_neigh1', 'L1_gnn_b1', 'L1_mix_Wq', 'L1_mix_bq', 'L1_mix_Wk', 'L1_mix_bk',
          'L1_mix_Wv', 'L1_mix_bv', 'L1_mix_Wo', 'L1_mix_bo', 'L1_mix_P', 'L1_ffn_w12', 'L1_ffn_w3',
          'L1_ffn_gate_w']


def _layout(name, a, np):
    if name in ("src", "dst"):
        pad = np.full(P * GROUPS - EDGES, T if name == "src" else 0, a.dtype)
        return np.concatenate([a, pad]).reshape(P, GROUPS)
    if name == "L0_mix_projection":
        return a.reshape(KD, 2, F0, HD).transpose(1, 3, 0, 2).reshape(P, KD, F0)
    if name == "L1_mix_P":
        o = np.zeros((2, HD, KD, 2, HD), a.dtype)
        for h in range(2):
            o[h, :, :, h, :] = a.reshape(KD, 2, HD, HD)[:, h].transpose(2, 0, 1)
        return o.reshape(P, KD, P)
    if name in ("L1_mix_bk", "L1_mix_bq"):
        return a.reshape(KD, P).T
    if name in ("L1_mix_Wq", "L1_mix_Wk", "L1_mix_Wv", "L1_mix_Wo", "L1_ffn_gate_w"):
        return a.T
    if name in ("L1_ffn_w12", "L1_ffn_w3"):
        return a.transpose(0, 2, 1)
    return a


def kernel(**inputs):
    import numpy as np
    import concourse.bacc as bacc
    from concourse.bass_utils import run_bass_kernel_spmd

    nc = bacc.Bacc("TRN2", target_bir_lowering=False, num_devices=1)
    arrays, aps = {}, {}
    for name in _NAMES:
        a = np.ascontiguousarray(_layout(name, np.asarray(inputs[name]), np))
        arrays[f"in_{name}"] = a
        aps[name] = nc.dram_tensor(f"in_{name}", a.shape, mybir.dt.from_np(a.dtype), kind="ExternalInput").ap()
    out = nc.dram_tensor("out_x", (T, D), F32, kind="ExternalOutput").ap()
    build(nc, aps, out)
    r = run_bass_kernel_spmd(nc, [arrays], core_ids=[0])
    return r.results[0]["out_x"]
```

```python
from contextlib import ExitStack

import concourse.bass as bass
from concourse import mybir

F32 = mybir.dt.float32
F32R = mybir.dt.float32r
I32 = mybir.dt.int32
U32 = mybir.dt.uint32
ALU = mybir.AluOpType
ACT = mybir.ActivationFunctionType
AX = mybir.AxisListType.X

P = 128
T = 1250
D = 1024
R = 125
NT = T // R
NB = NT // 2
KD = D // P
HALF = 512
QC = 256
NQ = D // QC
NH, HD = 16, 64
F0 = 256
E = 8
EDGES = 21250
GROUPS = 168
TABLE = 128 * 13056
DUMP = T * T + 1
CAP, CAPR = 391, 392
CH = [(0, 418), (418, 416), (834, 416)]
AC = 250
UNIT = 2048
PIECE = 500
NPIECE = 20
BLK = 17

B1 = 0
B2 = B1 + 161 * 64
KVO = B2 + NT * D
PTO = KVO + NH * 2 * P
B3 = PTO + KD * F0
ARENA = B3 + NT * D


class Arena:

    def __init__(self, buffers):
        self.buffers = buffers

    def __getitem__(self, index):
        parts, cols = index
        start, t = [x for x in self.buffers if x[0] <= cols.start][-1]
        return t[parts, cols.start - start:cols.stop - start]


class Chain:

    def __init__(self, eng, sem):
        self.eng, self.sem, self.n = eng, sem, 0

    def __call__(self, ins):
        ins.then_inc(self.sem, 1)
        self.n += 1
        return self.n

    def sync(self):
        self.eng.wait_ge(self.sem, self.n)


class Bank:

    def __init__(self, tensor, full, free, size=3):
        self.t, self.full, self.free, self.size, self.n = tensor, full, free, size, 0

    def take(self, pe):
        if self.n >= self.size:
            pe.wait_ge(self.free, self.n - self.size + 1)
        self.n += 1
        return self.t[:, (self.n - 1) % self.size, :]

    def read(self, eng):
        eng.wait_ge(self.full, self.n + 1)
        self.n += 1
        return self.t[:, (self.n - 1) % self.size, :]


class Unit:

    def __init__(self, kind, stage, place, number):
        self.kind, self.stage, self.place, self.number, self.end = kind, stage, place, number, None


def build(nc, A, out):
    ctx = ExitStack()
    with ctx:
        def sb(name, shape, dt=F32):
            return ctx.enter_context(nc.sbuf_tensor(name, shape, dt))

        def sem(name):
            return ctx.enter_context(nc.semaphore(name))

        def dram(name, shape, dt=F32):
            return nc.dram_tensor(name, shape, dt).ap()

        with nc.sbuf_tensor("b1", [P, B2 - B1], F32) as b1, nc.sbuf_tensor("b2", [P, B3 - B2], F32) as b2:
            pass
        FR = Arena([(B1, sb("b1_split", [P, B2 - B1], F32R)), (B2, sb("b2_split", [P, B3 - B2], F32R))])
        F = Arena([(B1, b1), (B2, b2), (B3, sb("b3", [P, ARENA - B3]))])
        WS = sb("WS", [P, 2, UNIT])
        WH = sb("WH", [P, 2, 2 * UNIT], F32R)
        RB = sb("RB", [P, 4, HALF])
        BI = sb("BI", [P, 2, QC])
        ident = sb("ident", [P, P])
        ones = sb("ones", [P, P])
        low = sb("low", [P, P])
        up = sb("up", [P, P])
        ecnt = sb("ecnt", [P, GROUPS])
        eidx = sb("eidx", [P, GROUPS], I32)
        dcol = sb("dcol", [P, NT])
        dinv = sb("dinv", [P, NT])
        gate_sb = sb("gate_sb", [P, KD, E])
        bcol = sb("bcol", [P, 2, KD])
        hs8 = sb("hs8", [P, 8])
        nr8 = sb("nr8", [P, 8])
        wk = sb("wk", [P, 2, NT])
        sidx = sb("sidx", [P, 2, NT], I32)
        gidx = sb("gidx", [P, 2, NT], I32)
        tok = sb("tok", [P, NT], I32)
        dmaxf = sb("dmaxf", [P, 1])
        dmax = sb("dmax", [P, 1], I32)
        dumpc = sb("dumpc", [P, 1])
        tidx = sb("tidx", [P, 34], I32)
        eblk = sb("eblk", [P, BLK], I32)
        iot8 = sb("iot8", [P, E])

        PV = ctx.enter_context(nc.psum_tensor("PV", [P, 3, HALF], F32))
        PS = ctx.enter_context(nc.psum_tensor("PS", [P, 3, HALF], F32))
        PA = ctx.enter_context(nc.psum_tensor("PA", [P, 2, HALF], F32))

        at_d = dram("at_d", [TABLE, 1])
        xn_d = dram("xn_d", [T, D])
        x2_d = dram("x2_d", [T, D])
        xm_d = dram("xm_d", [T, D])
        xs_d = dram("xs_d", [T, D])
        hs_d = dram("hs_d", [T, D])
        deg_d = dram("deg_d", [1, T])
        slots_d = [dram("slots0_d", [128 * 49, 1], I32), dram("slots1_d", [128 * 49, 1], I32)]
        y_d = [dram("y0_d", [E * CAPR, D]), dram("y1_d", [BLK * 256, D])]

        def rows(at, t=F):
            return t[0:R, at:at + NT * D].rearrange("p (i d) -> p i d", d=D)

        def cols(at, t=F):
            return t[:, at:at + KD * T].rearrange("p (k t) -> p k t", t=T)

        def split_ring(g):
            at = KVO + (g % 4) * 2 * PIECE
            return FR[:, at:at + PIECE], FR[:, at + PIECE:at + 2 * PIECE]

        def unit_parts(u):
            return WH[:, u.place % 2, 0:UNIT], WH[:, u.place % 2, UNIT:2 * UNIT]

        def row_pieces(at):
            return [cols(at)[:, 4 * kh:4 * kh + 4, i * R:(i + 1) * R]
                    for q in range(NQ) for i in range(NT) for kh in range(2)]

        def col_pieces(at):
            return [cols(at)[:, 2 * kq:2 * kq + 2, c * AC:(c + 1) * AC]
                    for q in range(NQ) for c in range(T // AC) for kq in range(4)]

        def pair(at, q, b):
            return rows(at)[:, 2 * b:2 * b + 2, q * QC:(q + 1) * QC]

        def dpair(t, q, b):
            return t[2 * b * R:2 * (b + 1) * R, q * QC:(q + 1) * QC].rearrange("(t p) n -> p t n", p=R)

        def two(ap):
            return ap.rearrange("p (t n) -> p t n", t=2)

        KV = F[:, KVO:PTO].rearrange("p (h f d) -> p h f d", h=NH, f=2)
        PT = F[:, PTO:B3].rearrange("p (k f) -> p k f", f=F0)
        kvbd = PT[:, :, P:2 * P]
        pbd = PT[:, :, 0:P]
        gcn_b = F[0:R, PTO:PTO + D]
        degs = F[:, PTO:PTO + T]
        v_heads = F[0:R, B1:B2].rearrange("p (n d) -> p n d", d=HD)
        at_rows = at_d[0:T * T, :].rearrange("(j p d) o -> p j (d o)", p=R, d=T)
        rbf = RB[:, :, :].rearrange("p a b -> p (a b)")
        eqs = F[:, PTO + 5 * GROUPS:PTO + 5 * GROUPS + 8 * P].rearrange("p (q c) -> p q c", c=P)
        keyf, first, srcf, dstf, srcc = (F[:, PTO + a * GROUPS:PTO + (a + 1) * GROUPS] for a in range(5))

        def edge_batches(j):
            return max(0, j - NPIECE) * (GROUPS // 4) // ((NQ - 1) * NPIECE)

        def ffn_shape(layer):
            return ((E, 4, CAPR // 4, 512, B1), (BLK, 2, P, 256, B3))[layer]

        def ffn_xe(layer, b):
            _, tiles, _, _, at = ffn_shape(layer)
            at += (b % 2) * tiles * D
            return F[:, at:at + tiles * D].rearrange("p (t d) -> p t d", d=D)

        def ffn_y(layer, slot):
            at = ffn_shape(layer)[4] + 8 * D + slot * HALF
            return F[:, at:at + HALF]

        def ffn_xeT(layer, b):
            _, tiles, r, _, _ = ffn_shape(layer)
            n = 2 * KD * tiles * r
            at = B2 + (b % 2) * n
            return FR[:, at:at + n].rearrange("p (a k t) -> p a k t", a=2, k=KD)

        def ffn_hT(layer):
            _, tiles, r, hidden, _ = ffn_shape(layer)
            at = B2 + 4 * KD * tiles * r
            n = 2 * hidden // P * tiles * r
            return FR[:, at:at + n].rearrange("p (a k t) -> p a k t", a=2, k=hidden // P)

        def y_slot(layer, n):
            if layer == 1:
                at = B3 + (n % 4) * D
            elif n < 12:
                at = B1 + (6 + n % 4) * D
            else:
                at = (PTO, PTO + D, B1 + 8 * D, B1 + 9 * D)[n % 4]
            return F[0:R, at:at + D]

        v_full, v_free = sem("v_full"), sem("v_free")
        s_full, s_free = sem("s_full"), sem("s_free")
        eq_full, eq_free = sem("eq_full"), sem("eq_free")
        dv, pl, ac = sem("dve_step"), sem("pool_step"), sem("act_step")
        ws_full = [sem(f"ws_full{i}") for i in range(2)]
        wc_full = [sem(f"wc_full{i}") for i in range(2)]
        wh_done, wl_done = sem("wh_done"), sem("wl_done")
        xh_done, xl_done, xs_used = sem("xh_done"), sem("xl_done"), sem("xs_used")
        rh_done, rl_done = sem("rh_done"), sem("rl_done")
        b_full = [sem(f"b_full{i}") for i in range(2)]
        x_in = [sem(f"x_in{i}") for i in range(5)]
        edges_in, small_in, pt_in, gate_in, rg1_in = (sem(n) for n in
                                                      ("edges_in", "small_in", "pt_in", "gate_in", "rg1_in"))
        gcn_b_in = sem("gcn_b_in")
        consts = sem("consts")
        key_ready = sem("key_ready")
        eidx_ready, zero_ready, table_zero, scattered = (sem(n) for n in
                                                         ("eidx_ready", "zero_ready", "table_zero", "scattered"))
        ln_var, ln_std, xn_ready = (sem(n) for n in ("ln_var", "ln_std", "xn_ready"))
        xn_st = [sem(f"xn_st{i}") for i in range(NB)]
        ones_col = sem("ones_col")
        sq_done, ss_done, nrm_done, qn_done = (sem(n) for n in ("sq_done", "ss_done", "nrm_done", "qn_done"))
        kp_used, kv_free, qp_used, acc_free, den_done = (
            sem(n) for n in ("kp_used", "kv_free", "qp_used", "acc_free", "den_done"))
        res_full = [sem(f"res_full{i}") for i in range(4)]
        res_used = sem("res_used")
        hs_st = [sem(f"hs_st{i}") for i in range(4)]
        deg_stored, dg_in, dg_sqrt = sem("deg_stored"), sem("dg_in"), sem("dg_sqrt")
        dmax_ready = sem("dmax_ready")
        sm_in, sm_exp, route_ready = (sem(n) for n in ("sm_in", "sm_exp", "route_ready"))
        gates_ready = sem("gates_ready")
        ids_scat, ids_in = sem("ids_scat"), sem("ids_in")
        xe_full = [sem("xe_full0"), sem("xe_full1")]
        th_done, hh_done, hl_done = sem("th_done"), sem("hh_done"), sem("hl_done")
        y_st = [sem(f"y_st{i}") for i in range(4)]
        yg_full = [sem(f"yg_full{i}") for i in range(4)]
        yg_used = sem("yg_used")
        x2_stored, xm_stored, xs_stored, xn_back, dinv_in, kvbd_ready = (
            sem(n) for n in ("x2_stored", "xm_stored", "xs_stored", "xn_back", "dinv_in", "kvbd_ready"))
        eblk_ready, out_stored = sem("eblk_ready"), sem("out_stored")

        block = ctx.enter_context(nc.Block())
        mark = {}
        units = []
        places = []
        staged = []
        xs_end = []
        bias_end = []
        gather_end = {}
        t_at, gate_at, up_at, y_at = {}, {}, {}, {}

        @block.tensor
        def _(pe):
            v, s = Bank(PV, v_full, v_free), Bank(PS, s_full, s_free)
            eq = Bank(PA, eq_full, eq_free, 2)
            count = {"split": 0, "used": 0, "piece": 0, "counts": [0, 0]}

            def unit(kind):
                u = Unit(kind, len(staged), len(places), count["split"])
                units.append(u)
                if kind != "counts":
                    staged.append(u)
                if kind != "raw":
                    places.append(u)
                if kind == "split":
                    count["split"] += 1
                    pe.wait_ge(wl_done, 2 * count["split"])
                elif kind == "raw":
                    pe.wait_ge(ws_full[u.stage % 2], 16 * (u.stage // 2 + 1))
                else:
                    at = u.place % 2
                    count["counts"][at] += 1
                    pe.wait_ge(wc_full[at], 16 * count["counts"][at])
                return u

            def piece():
                count["piece"] += 1
                pe.wait_ge(xl_done, count["piece"])
                return split_ring(count["piece"] - 1)

            def piece_used(mm, ends_bank):
                if ends_bank:
                    mm.then_inc(v_full, 1)
                    xs_end.append((v_full, v.n))
                else:
                    mm.then_inc(xs_used, 1)
                    count["used"] += 1
                    xs_end.append((xs_used, count["used"]))

            def three(o, a, b, start, stop, **kw):
                pe.matmul(o, a[0], b[0], start=start, stop=False, **kw)
                pe.matmul(o, a[0], b[1], start=False, stop=False, **kw)
                return pe.matmul(o, a[1], b[0], start=False, stop=stop, **kw)

            def turn_tile(src, i, ring_of):
                for ring, k0 in ring_of:
                    bank = ring.take(pe)
                    for k in range(4):
                        mm = pe.transpose(bank[:, k * R:(k + 1) * R],
                                          src[:, i, (k0 + k) * P:(k0 + k + 1) * P], ident[0:R, 0:R])
                    mm.then_inc(ring.full, 1)

            def turn_rows(src, sem_, base):
                for i in range(NT):
                    pe.wait_ge(sem_, base + i + 1)
                    turn_tile(src, i, ((v, 0), (s, 4)))

            def linear_rows(name, bias=True, lead=None, between=None, after_piece=None):
                mark[name] = v.n
                for q in range(NQ):
                    if lead is None or q:
                        u = unit("split")
                        w = [h.rearrange("p (k n) -> p k n", k=KD) for h in unit_parts(u)]
                    for b in range(NB):
                        if lead is not None and q == 0:
                            lead(b)
                            if b == 0:
                                u = unit("split")
                                w = [h.rearrange("p (k n) -> p k n", k=KD) for h in unit_parts(u)]
                        bank = two(v.take(pe))
                        for t in range(2):
                            for kh in range(2):
                                x = [h.rearrange("p (k t) -> p k t", k=4) for h in piece()]
                                for k in range(4):
                                    mm = three(bank[0:R, t, :], [h[:, k, :] for h in x],
                                               [h[:, 4 * kh + k, :] for h in w],
                                               kh + k == 0, kh * 4 + k == KD - 1)
                                piece_used(mm, t + kh == 2)
                                if after_piece:
                                    after_piece((q * NT + 2 * b + t) * 2 + kh)
                        if between:
                            between(q * NB + b)
                    u.end = (v_full, v.n)
                    if bias:
                        bias_end.append(v.n)

            def linear_cols():
                for q in range(NQ):
                    u = unit("split")
                    w = [h.rearrange("p (k n) -> p k n", k=KD) for h in unit_parts(u)]
                    for c in range(T // AC):
                        bank = v.take(pe)
                        for kq in range(4):
                            x = [h.rearrange("p (k t) -> p k t", k=2) for h in piece()]
                            for k2 in range(2):
                                k = 2 * kq + k2
                                for m in range(2):
                                    mm = three(bank[:, m * AC:(m + 1) * AC],
                                               [h[:, k, m * P:(m + 1) * P] for h in w], [h[:, k2, :] for h in x],
                                               k + m == 0, k == KD - 1, skip_group_check=True)
                            piece_used(mm, kq == 3)
                    u.end = (v_full, v.n)

            def count_rows(u):
                return WH[0:R, u.place % 2, 0:NT * AC].rearrange("p (j d) -> p j d", d=AC)

            def either(product):
                before = v.n, len(units), len(places), count["counts"][:]
                most = pe.value_load(dmax[0:1, 0:1], min_val=0, max_val=EDGES)
                with pe.If(most < 4097):
                    product(F32R)
                v.n, count["counts"] = before[0], before[3]
                del units[before[1]:], places[before[2]:]
                with pe.Else():
                    product(F32)

            def neighbours_cols(parts, base, dt):
                for c in range(T // AC):
                    u = unit("counts")
                    at = count_rows(u).bitcast(dt)
                    for f in range(KD):
                        if c == 0 and f % 4 == 0:
                            pe.wait_ge(rl_done, base + NT * (1 + f // 4))
                        bank = v.take(pe)
                        for j in range(NT):
                            for a, part in enumerate(parts):
                                mm = pe.matmul(bank[:, 0:AC], part[:, j, f * P:(f + 1) * P].bitcast(dt), at[:, j, :],
                                               start=(j + a == 0), stop=(j + a == NT))
                        mm.then_inc(v_full, 1)
                    u.end = (v_full, v.n)

            def router():
                bank = v.take(pe)
                for i in range(NT):
                    for k in range(KD):
                        mm = pe.matmul(bank[0:R, i * E:(i + 1) * E], cols(B2)[:, k, i * R:(i + 1) * R],
                                       gate_sb[:, k, :], start=(k == 0), stop=(k == KD - 1))
                mm.then_inc(v_full, 1)

            def experts(layer):
                blocks, tiles, r, hidden, _ = ffn_shape(layer)
                wid, mt = tiles * r, hidden // P
                hT = ffn_hT(layer)
                hidden_base = 0 if layer == 0 else E * 4

                def turn_block(b):
                    pe.wait_ge(xe_full[b % 2], 16 * (4 * 4 * layer + tiles * (b // 2 + 1)))
                    t_at[layer, b] = v.n
                    xe = ffn_xe(layer, b)
                    for k in range(KD):
                        bank = v.take(pe)
                        for t in range(tiles):
                            mm = pe.transpose(bank[:, t * r:(t + 1) * r], xe[0:r, t, k * P:(k + 1) * P],
                                              ident[0:r, 0:r])
                        mm.then_inc(v_full, 1)
                    gather_end[layer, b] = (v_full, v.n)

                turn_block(0)
                for b in range(blocks):
                    xeT = ffn_xeT(layer, b)
                    pe.wait_ge(v_free, t_at[layer, b] + KD)
                    for mh in range(mt // 2):
                        for ring in (s, v):
                            u = unit("split")
                            w = [h.rearrange("p (k n) -> p k n", k=KD) for h in unit_parts(u)]
                            for m in range(2):
                                bank = ring.take(pe)
                                for k in range(KD):
                                    mm = three(bank[:, 0:wid], [h[:, k, m * P:(m + 1) * P] for h in w],
                                               [xeT[:, a, k, :] for a in range(2)], k == 0, k == KD - 1)
                                mm.then_inc(ring.full, 1)
                                if ring is s:
                                    gate_at[layer, b * mt + 2 * mh + m] = s.n
                                else:
                                    up_at[layer, b * mt + 2 * mh + m] = v.n
                            u.end = (ring.full, ring.n)
                    if b + 1 < blocks:
                        turn_block(b + 1)
                    pe.wait_ge(hl_done, hidden_base + mt * (b + 1))
                    dcols = UNIT // mt
                    for nd in range(D // dcols):
                        u = unit("split")
                        w = [h.rearrange("p (k n) -> p k n", k=mt) for h in unit_parts(u)]
                        for t in range(tiles):
                            for n0 in range(0, dcols, HALF):
                                j = len(y_at)
                                ring = (v, s)[j % 2]
                                bank = ring.take(pe)
                                for k in range(mt):
                                    mm = three(bank[0:r, :], [hT[:, a, k, t * r:(t + 1) * r] for a in range(2)],
                                               [h[:, k, n0:n0 + HALF] for h in w], k == 0, k == mt - 1)
                                mm.then_inc(ring.full, 1)
                                y_at[j] = ring.n
                        u.end = (ring.full, ring.n)

            pe.wait_ge(consts, 8)

            def lead_norm(b, base, src):
                for i in (2 * b, 2 * b + 1):
                    pe.wait_ge(xn_ready, base + i + 1)
                    turn_tile(src, i, ((s, 0), (s, 4)))
                if b == NB - 1:
                    mark["lead_s"] = s.n

            def edge_keys(j):
                for m in range(edge_batches(j), edge_batches(j + 1)):
                    if m == 0:
                        pe.wait_ge(key_ready, 1)
                    bank = eq.take(pe)
                    for q in range(4):
                        mm = pe.matmul(bank[:, q * P:(q + 1) * P],
                                       keyf[:, 4 * m + q:4 * m + q + 1].to_broadcast([P, P]),
                                       ident[:, :], start=True, stop=True)
                    mm.then_inc(eq_full, 1)

            linear_rows("v0", lead=lambda b: lead_norm(b, 0, rows(B3)), after_piece=edge_keys)
            pe.wait_ge(eq_free, GROUPS // 4)

            def turn_heads(n):
                pe.wait_ge(qn_done, n + 1)
                bank = s.take(pe)
                for kk in range(2):
                    for t in range(2):
                        mm = pe.transpose(bank[:, (2 * kk + t) * R:(2 * kk + t + 1) * R],
                                          RB[0:R, n % 2, t * QC + kk * P:t * QC + (kk + 1) * P], ident[0:R, 0:R])
                mm.then_inc(s_full, 1)

            mark["k_s"] = s.n
            linear_rows("k0", between=lambda n: turn_heads(n - 2) if n >= 2 else None)
            turn_heads(NQ * NB - 2)
            turn_heads(NQ * NB - 1)
            pe.wait_ge(s_free, s.n)
            pe.wait_ge(pt_in, 16)
            pe.wait_ge(ones_col, 1)
            mark["kp"] = v.n
            for n in range(NH * NT + 2):
                if n < NH * NT:
                    h, i = divmod(n, NT)
                    half = slice(64 * (h % 2), 64 * (h % 2) + 64)
                    pe.matmul(v.take(pe)[0:R, 0:F0], cols(B3)[half, h // 2, i * R:(i + 1) * R],
                              PT[half, h // 2, :], start=True, stop=True).then_inc(v_full, 1)
                if n >= 2:
                    m = n - 2
                    h, i = divmod(m, NT)
                    pe.wait_ge(v_free, mark["kp"] + m + 1)
                    if i == 0 and h >= 2:
                        pe.wait_ge(kv_free, h - 1)
                    at = i * NH + h
                    for f in range(2):
                        mm = pe.matmul(PA[:, h % 2, f * P:(f + 1) * P].rearrange("p (c d) -> p c d", c=2),
                                       RB[0:R, m % 4, f * P:(f + 1) * P],
                                       v_heads[:, at:161:160 - at, :],
                                       start=(i == 0 and f == 0), stop=(i == NT - 1),
                                       skip_group_check=True)
                    mm.then_inc(kp_used, 1)
            mark["q"] = v.n
            for n in range(NQ * NB + 1):
                if n < NQ * NB:
                    q, b = divmod(n, NB)
                    if b == 0:
                        u = unit("raw")
                        w = WS[:, u.stage % 2, :].rearrange("p (k n) -> p k n", k=KD)
                    bank = two(v.take(pe))
                    for t in range(2):
                        i = 2 * b + t
                        for k in range(KD):
                            mm = pe.matmul(bank[0:R, t, :], cols(B2)[:, k, i * R:(i + 1) * R], w[:, k, :],
                                           start=(k == 0), stop=(k == KD - 1))
                    mm.then_inc(v_full, 1)
                    if b == NB - 1:
                        u.end = (v_full, v.n)
                        bias_end.append(v.n)
                if n >= 1:
                    turn_heads(NQ * NB + n - 1)
            pe.wait_ge(s_free, s.n)
            mark["qp"] = v.n
            pe.wait_ge(kv_free, NH)
            for n in range(NH * 6 + 2):
                if n < NH * 6:
                    step, hh, f = n // 4, n // 2 % 2, n % 2
                    pr, c = divmod(step, 3)
                    c0, cn = CH[c]
                    half = slice(64 * hh, 64 * hh + 64)
                    pe.matmul(v.take(pe)[:, 0:cn], PT[half, pr, f * P:(f + 1) * P],
                              cols(B3)[half, pr, c0:c0 + cn], start=True, stop=True).then_inc(v_full, 1)
                if n >= 2:
                    m = n - 2
                    step, hh, f = m // 4, m // 2 % 2, m % 2
                    pr, c = divmod(step, 3)
                    pe.wait_ge(v_free, mark["qp"] + m + 1)
                    if m % 4 == 0 and step >= 2:
                        pe.wait_ge(acc_free, 2 * (step - 1))
                    pe.matmul((PA, PS)[step % 2][:, hh, 0:CH[c][1]], KV[:, 2 * pr + hh, f, :],
                              RB[:, m % 3, 0:CH[c][1]],
                              start=(f == 0), stop=(f == 1)).then_inc(qp_used, 1)
            pe.wait_ge(acc_free, NH * 3)
            linear_rows("wo0")

            linear_rows("gcn", bias=False)
            mark["deg"] = v.n
            mark["xl_gcn"] = count["piece"]
            for c in range(T // AC):
                u = unit("counts")
                at = count_rows(u).bitcast(F32)
                bank = v.take(pe)
                for j in range(NT):
                    mm = pe.matmul(bank[:, 0:AC], ones[0:R, :], at[:, j, :], start=(j == 0), stop=(j == NT - 1))
                mm.then_inc(v_full, 1)
                u.end = (v_full, v.n)
            pe.wait_ge(v_free, v.n)
            for g in range(3):
                bank = v.take(pe)
                for q in range(min(4, NT - 4 * g)):
                    i = 4 * g + q
                    mm = pe.transpose(bank[0:R, q * P:(q + 1) * P], rbf[:, i * R:(i + 1) * R], ident[:, :])
                mm.then_inc(v_full, 1)

            def neighbours_rows(dt):
                for c in range(T // AC):
                    u = unit("counts")
                    at = count_rows(u).bitcast(dt)
                    for half in range(2):
                        if c == 0:
                            pe.wait_ge(rl_done, NT * (1 + half))
                        for t in range(2):
                            bank = v.take(pe)
                            for j in range(NT):
                                for a, part in enumerate((rows(B2, FR), rows(B1, FR))):
                                    mm = pe.matmul(bank[0:R, :], at[:, j, t * R:(t + 1) * R],
                                                   part[:, j, half * HALF:(half + 1) * HALF].bitcast(dt),
                                                   start=(j + a == 0), stop=(j + a == NT))
                            mm.then_inc(v_full, 1)
                    u.end = (v_full, v.n)

            pe.wait_ge(dmax_ready, 1)
            either(neighbours_rows)
            mark["gcn_end"] = v.n

            turn_rows(rows(B1), xn_ready, NT)
            pe.wait_ge(v_free, v.n)
            pe.wait_ge(s_free, s.n)
            pe.wait_ge(gate_in, 16)
            router()
            mark["router0"] = v.n
            pe.wait_ge(gates_ready, 1)
            gts = rbf[0:R, 1024:1024 + 3 * NT * E].rearrange("p (a i e) -> p a i e", a=3, e=E)
            for a in range(3):
                for g in range(3):
                    bank = v.take(pe)
                    for q in range(min(4, NT - 4 * g)):
                        mm = pe.transpose(bank[0:E, q * R:(q + 1) * R], gts[:, a, 4 * g + q, :], ident[0:R, 0:R])
                    mm.then_inc(v_full, 1)
            pe.wait_ge(v_free, v.n)
            gT = F[0:E, B2:B2 + 3 * T].rearrange("p (a t) -> p a t", t=T)
            for n in range(2 * NT):
                k, i = divmod(n, NT)
                for c0 in range(0, T, HALF):
                    cn = min(HALF, T - c0)
                    pe.matmul(v.take(pe)[0:R, 0:cn], gT[:, 1 + k, i * R:(i + 1) * R], gT[:, 0, c0:c0 + cn],
                              start=True, stop=True).then_inc(v_full, 1)
            experts(0)

            linear_rows("v1", lead=lambda b: lead_norm(b, 2 * NT, rows(B1)))
            pe.wait_ge(small_in, 32)
            linear_cols()
            pe.wait_ge(v_free, v.n)
            pe.wait_ge(pt_in, 32)
            mark["kp1"] = v.n
            for n in range(2 * NT + 2):
                if n < 2 * NT:
                    i, half = divmod(n, 2)
                    bank = v.take(pe)
                    for q in range(4):
                        pr = 4 * half + q
                        mm = pe.matmul(bank[0:R, q * P:(q + 1) * P], cols(B3)[:, pr, i * R:(i + 1) * R],
                                       pbd[:, pr, :], start=True, stop=True)
                    mm.then_inc(v_full, 1)
                if n >= 2:
                    m = n - 2
                    i, half = divmod(m, 2)
                    pe.wait_ge(v_free, mark["kp1"] + m + 1)
                    for q in range(4):
                        pr = 4 * half + q
                        mm = pe.matmul(PA[:, half, q * P:(q + 1) * P], RB[0:R, m % 4, q * P:(q + 1) * P],
                                       rows(B1)[:, i, pr * P:(pr + 1) * P], start=(i == 0 and q == 0),
                                       stop=(i == NT - 1), skip_group_check=True)
                    mm.then_inc(kp_used, 1)
            linear_cols()
            pe.wait_ge(v_free, v.n)
            pe.wait_ge(kvbd_ready, NH)
            mark["qp1"] = v.n
            for n in range(3 * KD + 2):
                if n < 3 * KD:
                    pr, c = divmod(n, 3)
                    c0, cn = CH[c]
                    pe.matmul(v.take(pe)[:, 0:cn], pbd[:, pr, :], cols(B3)[:, pr, c0:c0 + cn],
                              start=True, stop=True).then_inc(v_full, 1)
                if n >= 2:
                    m = n - 2
                    pr, c = divmod(m, 3)
                    pe.wait_ge(v_free, mark["qp1"] + m + 1)
                    pe.matmul(s.take(pe)[:, 0:CH[c][1]], kvbd[:, pr, :], RB[:, m % 4, 0:CH[c][1]],
                              start=True, stop=True).then_inc(s_full, 1)
            mark["qp1_s"] = s.n
            linear_rows("wo1")
            mark["xl_wo1"] = count["piece"]

            linear_rows("ws0")
            mark["xl_ws0"] = count["piece"]
            either(lambda dt: neighbours_cols((rows(B2, FR), rows(B1, FR)), 2 * NT, dt))
            mark["agg1"] = v.n
            linear_rows("wn0", bias=False)

            def lead_h1(b):
                pe.wait_ge(res_used, 2 * NQ * NB + (NQ - 1) * NB + b + 1)
                for i in (2 * b, 2 * b + 1):
                    turn_tile(rows(B1), i, ((s, 0), (s, 4)))
                if b == NB - 1:
                    mark["lead_s"] = s.n

            linear_rows("ws1", lead=lead_h1)
            mark["xl_ws1"] = count["piece"]
            either(lambda dt: neighbours_cols((rows(B2, FR), rows(B1, FR)), 4 * NT, dt))
            mark["agg2"] = v.n
            linear_rows("wn1", bias=False)

            turn_rows(rows(B3), xn_ready, 3 * NT)
            pe.wait_ge(v_free, v.n)
            pe.wait_ge(s_free, s.n)
            pe.wait_ge(rg1_in, 16)
            router()
            pe.wait_ge(gates_ready, 2)
            bank = v.take(pe)
            osum = rbf[0:R, 1024:1024 + NT * E]
            pe.matmul(bank[0:R, 0:NT * E], up[0:R, 0:R], osum, start=True, stop=True)
            pe.matmul(bank[0:R, P:P + NT * E], ones[0:R, 0:R], osum, start=True, stop=True).then_inc(v_full, 1)
            mark["routed"] = len(units)
            experts(1)

        @block.sync
        def _(sp):
            n_unit, n_bias = [0], [0]
            n_counts = [0, 0]

            def load(src, k=KD, lead=None):
                u = units[n_unit[0]]
                n_unit[0] += 1
                if u.stage >= 2:
                    last = staged[u.stage - 2]
                    if last.kind == "raw":
                        sp.wait_ge(*last.end)
                    else:
                        sp.wait_ge(wl_done, 2 * (last.number + 1))
                dst = WS[:, u.stage % 2, :]
                if lead:
                    dst = dst.rearrange("p (a k n) -> p a k n", a=1, k=k)
                else:
                    dst = dst.rearrange("p (k n) -> p k n", k=k)
                sp.dma_start(dst, src).then_inc(ws_full[u.stage % 2], 16)

            def counts():
                for c in range(T // AC):
                    u = units[n_unit[0]]
                    n_unit[0] += 1
                    sp.wait_ge(*places[u.place - 2].end)
                    sp.dma_start(WH[0:R, u.place % 2, 0:NT * AC].bitcast(F32).rearrange("p (j d) -> p j d", d=AC),
                                 at_rows[:, :, c * AC:(c + 1) * AC]).then_inc(wc_full[u.place % 2], 16)

            def bias(vec, q):
                n = n_bias[0]
                n_bias[0] += 1
                if n >= 2:
                    sp.wait_ge(v_free, bias_end[n - 2])
                sp.dma_start(BI[0:R, n % 2, :], vec[q * QC:(q + 1) * QC].partition_broadcast(R))\
                  .then_inc(b_full[n % 2], 16)

            def square(w, q):
                load(w[:, q * QC:(q + 1) * QC].rearrange("(k p) n -> p k n", p=P))

            def linear(w, vec=None):
                for q in range(NQ):
                    square(w, q)
                    if vec is not None:
                        bias(vec, q)

            x_v = A["x"].rearrange("(i p) d -> p i d", p=R)
            for g in range(NB):
                sp.dma_start(rows(B3)[:, 2 * g:2 * g + 2, :], x_v[:, 2 * g:2 * g + 2, :]).then_inc(x_in[g], 16)
                if g == 1:
                    square(A["L0_mix_Wv"], 0)
                    bias(A["L0_mix_bv"], 0)
            sp.dma_start(srcf.bitcast(I32), A["src"]).then_inc(edges_in, 16)
            sp.dma_start(dstf.bitcast(I32), A["dst"]).then_inc(edges_in, 16)
            for q in range(1, NQ):
                square(A["L0_mix_Wv"], q)
                bias(A["L0_mix_bv"], q)
            sp.dma_start(gate_sb[:, :, :], A["L0_ffn_router_gate"].rearrange("(k p) e -> p k e", p=P))\
              .then_inc(gate_in, 16)
            sp.dma_start(bcol[:, 0, :], A["L1_mix_bk"]).then_inc(small_in, 16)
            sp.dma_start(bcol[:, 1, :], A["L1_mix_bq"]).then_inc(small_in, 16)
            for q in range(NQ):
                square(A["L0_mix_Wk"], q)
                bias(A["L0_mix_bk"], q)
                if q == 2:
                    sp.wait_ge(eidx_ready, 2)
                    sp.dma_start(PT[:, :, :], A["L0_mix_projection"]).then_inc(pt_in, 16)
            linear(A["L0_mix_Wq"], A["L0_mix_bq"])
            linear(A["L0_mix_Wo"], A["L0_mix_bo"])
            linear(A["L0_gnn_W"])
            sp.wait_ge(scattered, 16 * GROUPS)
            counts()
            sp.wait_ge(v_full, mark["deg"])
            sp.dma_start(gcn_b, A["L0_gnn_b"].partition_broadcast(R)).then_inc(gcn_b_in, 16)
            counts()
            for e in range(E):
                for m in range(2):
                    for w in (A["L0_ffn_gate_w"], A["L0_ffn_up_w"]):
                        square(w[e], m)
                for m in range(2):
                    load(A["L0_ffn_down_w"][e][:, m * HALF:(m + 1) * HALF].rearrange("(k p) n -> p k n", p=P), 4)
            for q in range(NQ):
                if q == 2:
                    sp.wait_ge(v_full, mark["router0"])
                    sp.wait_ge(yg_used, 2 * NT)
                    sp.dma_start(gate_sb[:, :, :], A["L1_ffn_gate_w"].rearrange("(k p) e -> p k e", p=P))\
                      .then_inc(rg1_in, 16)
                    sp.dma_start(pbd, A["L1_mix_P"]).then_inc(pt_in, 16)
                square(A["L1_mix_Wv"], q)
                bias(A["L1_mix_bv"], q)
            linear(A["L1_mix_Wk"])
            linear(A["L1_mix_Wq"])
            linear(A["L1_mix_Wo"], A["L1_mix_bo"])
            for q in range(NQ):
                square(A["L1_gnn_W_self0"], q)
                bias(A["L1_gnn_b0"], q)
                if q == 1:
                    sp.wait_ge(xl_done, mark["xl_wo1"])
                    for g in range(NB):
                        sp.wait_ge(xn_st[g], 16 * 2)
                    sp.dma_start(rows(B1)[:, :, :], xn_d.rearrange("(i p) d -> p i d", p=R)).then_inc(xn_back, 16)
            counts()
            linear(A["L1_gnn_W_neigh0"])
            linear(A["L1_gnn_W_self1"], A["L1_gnn_b1"])
            counts()
            linear(A["L1_gnn_W_neigh1"])
            sp.wait_ge(eblk_ready, 1)
            for b in range(BLK):
                e = sp.value_load(eblk[0:1, b:b + 1], min_val=0, max_val=E - 1)
                for m in range(2):
                    load(A["L1_ffn_w12"][bass.DynSlice(e, 1)][:, :, m * QC:(m + 1) * QC]
                         .rearrange("a (k p) n -> p a k n", p=P), KD, True)
                load(A["L1_ffn_w3"][bass.DynSlice(e, 1)].rearrange("a (k p) n -> p a k n", p=P), 2, True)
            for i in range(NT):
                sp.wait_ge(yg_used, 2 * NT + 2 * (i + 1))
                sp.dma_start(out[i * R:(i + 1) * R, :], rows(B1)[:, i, :]).then_inc(out_stored, 16)
            sp.wait_ge(out_stored, 16 * NT)

        @block.gpsimd
        def _(pool):
            pool.memset(F[:, B1:B1 + 4352], 0.0).then_inc(zero_ready, 1)
            pool.memset(ident[:, :], 0.0).then_inc(consts, 1)
            pool.memset(ones[:, :], 1.0).then_inc(consts, 1)
            pool.iota(tok[:, :], [[R, NT]], base=0, channel_multiplier=1).then_inc(consts, 1)
            pool.iota(iot8[:, :], [[1, E]], base=0, channel_multiplier=0,
                      allow_small_or_imprecise_dtypes=True).then_inc(consts, 1)
            pool.wait_ge(consts, 4)
            pool.affine_select(out=ident[:, :], in_=ident[:, :], compare_op=ALU.not_equal, fill=1.0, base=0,
                               pattern=[[-1, P]], channel_multiplier=1).then_inc(consts, 1)
            pool.affine_select(out=low[:, :], in_=ones[:, :], compare_op=ALU.is_gt, fill=0.0, base=0,
                               pattern=[[-1, P]], channel_multiplier=1).then_inc(consts, 1)
            pool.affine_select(out=up[:, :], in_=ones[:, :], compare_op=ALU.is_gt, fill=0.0, base=0,
                               pattern=[[1, P]], channel_multiplier=-1).then_inc(consts, 1)
            pool.iota(dumpc[:, :], [[0, 1]], base=DUMP, channel_multiplier=1,
                      allow_small_or_imprecise_dtypes=True).then_inc(consts, 1)
            pool.wait_ge(zero_ready, 1)
            pool.wait_ge(x_in[NB - 1], 16)
            zt = F[:, B1:B1 + 4352]
            for q in range(3):
                pool.dma_start(at_d.rearrange("(p c) o -> p (c o)", p=P)[:, q * 4352:(q + 1) * 4352], zt)\
                    .then_inc(table_zero, 16)
            for q in range(2):
                pool.dma_start(slots_d[q].rearrange("(p c) o -> p (c o)", p=P), zt[:, 0:49].bitcast(I32))\
                    .then_inc(table_zero, 16)
            pool.wait_ge(table_zero, 16 * 5)
            pool.wait_ge(eidx_ready, 2)
            for g in range(GROUPS):
                if g:
                    pool.wait_ge(scattered, 16 * g)
                pool.indirect_dma_start(out=at_d, out_offset=bass.IndirectOffsetOnAxis(ap=eidx[:, g:g + 1], axis=0),
                                        in_=ecnt[:, g:g + 1], in_offset=None, compute_op=ALU.add)\
                    .then_inc(scattered, 16)

            for layer in range(2):
                blocks, tiles, r, _, _ = ffn_shape(layer)
                ntile = blocks * tiles
                pool.wait_ge(route_ready, 2 * layer + 2)
                for n in range(2 * NT):
                    k, i = divmod(n, NT)
                    pool.indirect_dma_start(out=slots_d[layer],
                                            out_offset=bass.IndirectOffsetOnAxis(ap=sidx[0:R, k, i:i + 1], axis=0),
                                            in_=tok[0:R, i:i + 1], in_offset=None).then_inc(ids_scat, 16)
                pool.wait_ge(ids_scat, 16 * 2 * NT * (layer + 1))
                with nc.allow_non_contiguous_dma(reason="a few thousand token numbers, turned"):
                    pool.dma_start(tidx[0:r, 0:ntile].unsqueeze(2),
                                   slots_d[layer][0:ntile * r, :].rearrange("(b p) o -> p b o", p=r))\
                        .then_inc(ids_in, 16)
                pool.wait_ge(ids_in, 16 * (layer + 1))
                for g in range(NB):
                    pool.wait_ge(xn_st[g], 16 * (1 + 2 * layer))
                for b in range(blocks):
                    if b >= 2:
                        pool.wait_ge(*gather_end[layer, b - 2])
                    for t in range(tiles):
                        c = b * tiles + t
                        pool.indirect_dma_start(out=ffn_xe(layer, b)[0:r, t, :], out_offset=None, in_=xn_d,
                                                in_offset=bass.IndirectOffsetOnAxis(ap=tidx[0:r, c:c + 1], axis=0))\
                            .then_inc(xe_full[b % 2], 16)
                for q in range(4):
                    pool.wait_ge(y_st[q], 16 * ((E * 8 // 4) if layer == 0 else (E * 8 + BLK * 4) // 4))
                for n in range(2 * NT):
                    i, k = divmod(n, 2)
                    if n >= 4:
                        pool.wait_ge(yg_used, 2 * NT * layer + n - 3)
                    pool.indirect_dma_start(out=y_slot(layer, n), out_offset=None, in_=y_d[layer],
                                            in_offset=bass.IndirectOffsetOnAxis(ap=gidx[0:R, k, i:i + 1], axis=0))\
                        .then_inc(yg_full[n % 4], 16)

        @block.scalar
        def _(act):
            s = Bank(PS, s_full, s_free)
            n_unit, n_piece, n_res, n_ln, n_silu = [0], [0], [0], [0], [0]

            def next_unit(routed=False):
                if n_unit[0] == mark["routed"] and not routed:
                    return
                if n_unit[0] < len(units) and units[n_unit[0]].kind == "split":
                    u = units[n_unit[0]]
                    act.wait_ge(ws_full[u.stage % 2], 16 * (u.stage // 2 + 1))
                    if u.place >= 2:
                        act.wait_ge(*places[u.place - 2].end)
                    for a in (0, UNIT // 2):
                        act.copy(WH[:, u.place % 2, a:a + UNIT // 2], WS[:, u.stage % 2, a:a + UNIT // 2])\
                           .then_inc(wh_done, 1)
                n_unit[0] += 1

            def hi_pieces(views, lead=None, extra=None):
                for j, src in enumerate(views):
                    if lead and j < NPIECE and j % 4 == 0:
                        lead(j // 4)
                    if j % NPIECE == 8:
                        next_unit()
                    g = n_piece[0]
                    n_piece[0] += 1
                    if g >= 4:
                        act.wait_ge(*xs_end[g - 4])
                    hi = split_ring(g)[0].rearrange("p (k t) -> p k t", k=src.shape[1])
                    act.copy(hi, src).then_inc(xh_done, 1)
                    if extra:
                        extra(j)

            def ln_sqrt(g):
                two_ = slice(2 * g, 2 * g + 2)
                var, std = rbf[0:R, 160:170], rbf[0:R, 176:186]
                n_ln[0] += 1
                act.wait_ge(ln_var, n_ln[0])
                act.activation(std[:, two_], var[:, two_], ACT.Sqrt).then_inc(ln_std, 1)

            def turned_tile(i, k0):
                act.copy(cols(B2)[:, k0:k0 + 4, i * R:(i + 1) * R],
                         s.read(act)[:, 0:4 * R].rearrange("p (k t) -> p k t", t=R)).then_inc(s_free, 1)

            def turned_pair(b):
                for i in (2 * b, 2 * b + 1):
                    for k0 in (0, 4):
                        turned_tile(i, k0)
                act.wait_ge(s_free, s.n)

            def store_xn(src, g, base):
                act.wait_ge(xn_ready, base + 2 * g + 2)
                act.dma_start(xn_d[2 * g * R:2 * (g + 1) * R, :].rearrange("(t p) d -> p t d", p=R),
                              src[:, 2 * g:2 * g + 2, :]).then_inc(xn_st[g], 16)

            def piece_at(j, lag):
                return (j - lag) // 4 if j >= lag and (j - lag) % 4 == 0 else None

            def residual_piece(src, m):
                if m >= 4:
                    act.wait_ge(res_used, NQ * NB * n_res[0] + m - 3)
                act.dma_start(two(RB[0:R, m % 4, :]), dpair(src, *divmod(m, NB))).then_inc(res_full[m % 4], 16)

            def linear_residual(at, src, lead=None, store=None):
                def store_piece(m):
                    act.wait_ge(res_used, NQ * NB * n_res[0] + m + 1)
                    act.dma_start(dpair(store[0], *divmod(m, NB)), pair(B3, *divmod(m, NB))).then_inc(store[1], 16)

                def extra(j):
                    m = piece_at(j, 9)
                    if m is not None and m + 4 < NQ * NB:
                        residual_piece(src, m + 4)
                    m = piece_at(j, 10)
                    if m is not None and store:
                        store_piece(m)

                if n_res[0]:
                    act.wait_ge(res_used, NQ * NB * n_res[0])
                for m in range(4):
                    residual_piece(src, m)
                hi_pieces(row_pieces(at), lead=lead, extra=extra)
                if store:
                    store_piece(NQ * NB - 2)
                    store_piece(NQ * NB - 1)
                n_res[0] += 1

            def square(g):
                n = g % (NQ * NB)
                act.wait_ge(v_free, mark["k0" if g < NQ * NB else "q"] + n + 1)
                act.activation(RB[0:R, 2 + n % 2, :], RB[0:R, n % 2, :], ACT.Square).then_inc(sq_done, 1)

            def norm(g):
                act.wait_ge(ss_done, g + 1)
                act.activation(nr8[0:R, :], hs8[0:R, :], ACT.Sqrt).then_inc(nrm_done, 1)

            def turned_heads(n):
                q, b = divmod(n, NB)
                act.copy(cols(B3)[:, 2 * q:2 * q + 2, 2 * b * R:2 * (b + 1) * R],
                         s.read(act)[:, 0:4 * R].rearrange("p (k t) -> p k t", k=2)).then_inc(s_free, 1)

            def split_rows(scale=None):
                for half in range(2):
                    hc = slice(half * HALF, (half + 1) * HALF)
                    for i in range(NT):
                        if scale is None:
                            act.copy(rows(B2, FR)[:, i, hc], rows(B1)[:, i, hc]).then_inc(rh_done, 1)
                        else:
                            act.activation(rows(B2, FR)[:, i, hc], rows(B1)[:, i, hc], ACT.Copy,
                                           scale=scale[0:R, i:i + 1]).then_inc(rh_done, 1)
                for c in range(T // AC):
                    next_unit()

            def norm_turned(src, base):
                ln_sqrt(0)
                for b in range(NB):
                    if b + 1 < NB:
                        ln_sqrt(b + 1)
                    store_xn(src, b, base)
                    for i in (2 * b, 2 * b + 1):
                        turned_tile(i, 4)

            def experts(layer):
                blocks, tiles, r, hidden, _ = ffn_shape(layer)
                wid, mt = tiles * r, hidden // P
                hT = ffn_hT(layer)
                piece0 = 0 if layer == 0 else E * 8

                def turned_block(b):
                    xeT = ffn_xeT(layer, b)
                    for k in range(KD):
                        n = t_at[layer, b] + k
                        act.wait_ge(v_full, n + 1)
                        act.copy(xeT[:, 0, k, :], PV[:, n % 3, 0:wid]).then_inc(th_done, 1)

                turned_block(0)
                for b in range(blocks):
                    for mh in range(mt // 2):
                        next_unit()
                        for m in range(2):
                            n = n_silu[0] + m
                            if n >= 4:
                                act.wait_ge(hl_done, n - 3)
                            act.activation(RB[:, n % 4, 0:wid], s.read(act)[:, 0:wid], ACT.Silu).then_inc(s_free, 1)
                        next_unit()
                        for m in range(2):
                            n = n_silu[0]
                            n_silu[0] += 1
                            act.wait_ge(v_free, up_at[layer, b * mt + 2 * mh + m])
                            act.copy(hT[:, 0, 2 * mh + m, :], RB[:, n % 4, 0:wid]).then_inc(hh_done, 1)
                    if b + 1 < blocks:
                        turned_block(b + 1)
                    npiece = tiles * D // HALF
                    for p in range(npiece):
                        if p % (UNIT // mt // HALF * tiles) == 0:
                            next_unit()
                        j = piece0 + b * npiece + p
                        if j % 2 == 0:
                            continue
                        if j >= 4:
                            act.wait_ge(y_st[j % 4], 16 * (j // 4))
                        act.copy(ffn_y(layer, j % 4)[0:r, :], s.read(act)[0:r, :]).then_inc(s_free, 1)
                        for jj, pp, done in ((j - 1, p - 1, v_free), (j, p, s_free)):
                            nd, t = divmod(pp, tiles) if layer == 0 else (pp % 2, pp // 2)
                            act.wait_ge(done, y_at[jj])
                            act.dma_start(y_d[layer][(b * tiles + t) * r:(b * tiles + t + 1) * r,
                                                     nd * HALF:(nd + 1) * HALF],
                                          ffn_y(layer, jj % 4)[0:r, :]).then_inc(y_st[jj % 4], 16)

            ln_sqrt(0)
            ln_sqrt(1)
            next_unit()

            def lead_x(b):
                if b and b + 1 < NB:
                    ln_sqrt(b + 1)
                turned_pair(b)

            hi_pieces(row_pieces(B2), lead=lead_x)

            def heads(j):
                n = piece_at(j, 8)
                if n is not None:
                    square(n)
                n = piece_at(j, 9)
                if n is not None:
                    norm(n)
                n = piece_at(j, 15)
                if n is not None:
                    turned_heads(n)

            hi_pieces(row_pieces(B2), extra=heads)
            last = NQ * NB - 1
            square(last - 1)
            norm(last - 1)
            turned_heads(last - 2)
            square(last)
            norm(last)
            turned_heads(last - 1)
            turned_heads(last)
            for h in range(NH):
                act.wait_ge(kp_used, NT * (h + 1))
                kvp = PA[:, h % 2, 0:2 * P].rearrange("p (f c d) -> p f c d", f=2, c=2)
                dst = KV[:, h, :, :].rearrange("p f (c d) -> p f c d", c=2)
                if h % 2 == 0:
                    act.copy(dst, kvp).then_inc(kv_free, 1)
                else:
                    act.copy(dst[:, :, 1, :], kvp[:, :, 0, :]).then_inc(ac, 1)
                    act.copy(dst[:, :, 0, :], kvp[:, :, 1, :]).then_inc(kv_free, 1)
            for n in range(NQ * NB):
                square(NQ * NB + n)
                norm(NQ * NB + n)
                turned_heads(n)
                if n % NB == 1:
                    next_unit()
            for step in range(3 * KD):
                cn = CH[step % 3][1]
                acc = (PA, PS)[step % 2]
                act.wait_ge(qp_used, 4 * (step + 1))
                if step:
                    act.wait_ge(acc_free, 2 * step)
                act.copy(RB[0:64, 3, 0:cn], acc[64:128, 0, 0:cn]).then_inc(den_done, 1)
                act.copy(RB[64:128, 3, 0:cn], acc[0:64, 1, 0:cn]).then_inc(den_done, 1)
            act.wait_ge(acc_free, NH * 3)
            linear_residual(B1, A["x"])

            hi_pieces(row_pieces(B2))
            for c in range(T // AC):
                next_unit()
            act.wait_ge(v_free, mark["deg"] + 5)
            act.dma_start(deg_d, rbf[0:1, 0:T]).then_inc(deg_stored, 16)
            act.wait_ge(dg_in, 1)
            act.activation(dinv[0:R, :], dcol[0:R, :], ACT.Sqrt).then_inc(dg_sqrt, 1)
            act.wait_ge(xl_done, mark["xl_gcn"])
            act.wait_ge(dg_in, 2)
            split_rows(dinv)

            norm_turned(rows(B1), NT)
            pe_ = rbf[0:R, 512:512 + NT * E]
            act.wait_ge(sm_in, 1)
            act.activation(pe_, pe_, ACT.Exp).then_inc(sm_exp, 1)
            experts(0)

            def x2_pair(g):
                ln_sqrt(g)
                act.wait_ge(yg_used, 4 * (g + 1))
                act.dma_start(x2_d[2 * g * R:2 * (g + 1) * R, :].rearrange("(t p) d -> p t d", p=R),
                              rows(B3)[:, 2 * g:2 * g + 2, :]).then_inc(x2_stored, 16)

            def lead_x2(b):
                if b and b + 1 < NB:
                    x2_pair(b + 1)
                store_xn(rows(B1), b, 2 * NT)
                turned_pair(b)

            x2_pair(0)
            x2_pair(1)
            hi_pieces(row_pieces(B2), lead=lead_x2)
            hi_pieces(col_pieces(B2))
            hi_pieces(col_pieces(B2))
            for m in range(3 * KD):
                pr, c = divmod(m, 3)
                c0, cn = CH[c]
                act.copy(cols(B1)[:, pr, c0:c0 + cn], s.read(act)[:, 0:cn]).then_inc(s_free, 1)
            act.wait_ge(s_free, s.n)
            act.wait_ge(deg_stored, 16)
            act.dma_start(degs, deg_d[0, :].partition_broadcast(P)).then_inc(dinv_in, 16)
            act.wait_ge(x2_stored, 16 * NB)
            linear_residual(B1, x2_d, store=(xm_d, xm_stored))

            def store_own(m):
                act.wait_ge(v_free, mark["ws0"] + m + 1)
                act.dma_start(dpair(hs_d, *divmod(m, NB)), two(RB[0:R, m % 4, :])).then_inc(hs_st[m % 4], 16)

            def own_part(j):
                m = piece_at(j, 10)
                if m is not None:
                    store_own(m)

            hi_pieces(row_pieces(B2), extra=own_part)
            store_own(last - 1)
            store_own(last)
            act.wait_ge(xn_back, 16)
            act.wait_ge(xl_done, mark["xl_ws0"])
            split_rows()
            act.wait_ge(v_free, mark["agg1"])
            for q in range(4):
                act.wait_ge(hs_st[q], 16 * NQ * NB // 4)
            linear_residual(B3, hs_d)
            act.wait_ge(xm_stored, 16 * NQ * NB)
            linear_residual(B2, xm_d, lead=turned_pair, store=(xs_d, xs_stored))
            act.wait_ge(xl_done, mark["xl_ws1"])
            split_rows()
            act.wait_ge(v_free, mark["agg2"])
            act.wait_ge(xs_stored, 16 * NQ * NB)
            linear_residual(B3, xs_d)

            norm_turned(rows(B3), 3 * NT)
            act.wait_ge(sm_in, 2)
            d2 = rbf[0:R, 512:512 + NT]
            act.activation(d2, d2, ACT.Exp).then_inc(sm_exp, 1)
            next_unit(True)
            experts(1)

        @block.vector
        def _(ve):
            d = Chain(ve, dv)
            v, eq = Bank(PV, v_full, v_free), Bank(PA, eq_full, eq_free, 2)
            n_unit, n_piece, n_half, n_rows = [0], [0], [0], [0]
            n_bias, n_res, n_ln, n_hid, n_turned = [0], [0], [0], [0], [0]

            def next_unit(routed=False):
                if n_unit[0] == mark["routed"] and not routed:
                    return
                if n_unit[0] < len(units) and units[n_unit[0]].kind == "split":
                    u = units[n_unit[0]]
                    for a in (0, UNIT // 2):
                        n_half[0] += 1
                        ve.wait_ge(wh_done, n_half[0])
                        ve.tensor_tensor(WH[:, u.place % 2, UNIT + a:UNIT + a + UNIT // 2],
                                         WS[:, u.stage % 2, a:a + UNIT // 2],
                                         WH[:, u.place % 2, a:a + UNIT // 2].bitcast(F32),
                                         ALU.subtract).then_inc(wl_done, 1)
                n_unit[0] += 1

            def lo_pieces(views, evac, lead=None, after=None):
                for j, src in enumerate(views):
                    if lead and j < NPIECE and j % 4 == 0:
                        lead(j // 4)
                    if j % NPIECE == 8:
                        next_unit()
                    g = n_piece[0]
                    n_piece[0] += 1
                    hi, lo = (h.rearrange("p (k t) -> p k t", k=src.shape[1]) for h in split_ring(g))
                    ve.wait_ge(xh_done, g + 1)
                    ve.tensor_tensor(lo, src, hi.bitcast(F32), ALU.subtract).then_inc(xl_done, 1)
                    if evac and j >= 7 and j % 4 == 3:
                        evac((j - 7) // 4)
                    if after:
                        after(j)
                if evac:
                    evac(NQ * NB - 1)

            def bias(m):
                if m % NB == 0:
                    ve.wait_ge(b_full[n_bias[0] % 2], 16 * (n_bias[0] // 2 + 1))
                    n_bias[0] += 1
                return BI[0:R, (n_bias[0] - 1) % 2, :].unsqueeze(1).to_broadcast([R, 2, QC])

            def emptied(ins):
                ins.then_inc(v_free, 1)

            def bank2():
                return two(v.read(ve))[0:R, :, :]

            def ln_group(g, x, xn):
                st = rbf[0:R, 0:120].rearrange("p (i c s) -> p i c s", i=NT, c=2)
                mv = rbf[0:R, 128:148].rearrange("p (i s) -> p i s", s=2)
                var, std, rstd = (rbf[0:R, a + 2 * g:a + 2 * g + 2] for a in (160, 176, 192))
                n_ln[0] += 1
                for i in (2 * g, 2 * g + 1):
                    for c in range(2):
                        d(ve.bn_stats(st[:, i, c, :], x[:, i, c * HALF:(c + 1) * HALF]))
                d.sync()
                for i in (2 * g, 2 * g + 1):
                    d(ve.bn_aggr(mv[:, i, :], st[:, i, :, :]))
                d.sync()
                ve.tensor_scalar(var, mv[:, 2 * g:2 * g + 2, 1], 1e-5, None, ALU.add).then_inc(ln_var, 1)
                ve.wait_ge(ln_std, n_ln[0])
                d(ve.reciprocal(rstd, std))
                d.sync()
                for i in (2 * g, 2 * g + 1):
                    ve.tensor_scalar(xn[:, i, :], x[:, i, :], mv[:, i, 0:1], rstd[:, i - 2 * g:i - 2 * g + 1],
                                     ALU.subtract, ALU.mult).then_inc(xn_ready, 1)

            def norm_turned(x, xn):
                ln_group(0, x, xn)
                for b in range(NB):
                    if b + 1 < NB:
                        ln_group(b + 1, x, xn)
                    for i in (2 * b, 2 * b + 1):
                        emptied(ve.tensor_copy(cols(B2)[:, 0:4, i * R:(i + 1) * R],
                                               v.read(ve)[:, 0:4 * R].rearrange("p (k t) -> p k t", t=R)))

            def add_residual(at, with_bias, relu=False):
                def evac(m):
                    q, b = divmod(m, NB)
                    o = pair(at, q, b)
                    piece = two(RB[0:R, m % 4, :])
                    n = NQ * NB * n_res[0] + m
                    if with_bias:
                        bi = bias(m)
                        emptied(ve.tensor_tensor(o, bank2(), bi, ALU.add))
                        ve.wait_ge(v_free, v.n)
                        ve.wait_ge(res_full[m % 4], 16 * (n // 4 + 1))
                        ve.tensor_tensor(o, o, piece, ALU.add).then_inc(res_used, 1)
                    else:
                        ve.wait_ge(res_full[m % 4], 16 * (n // 4 + 1))
                        emptied(ve.tensor_tensor(o, bank2(), piece, ALU.add))
                        ve.wait_ge(v_free, v.n)
                        if relu:
                            ve.tensor_scalar(o, o, 0.0, None, ALU.max).then_inc(res_used, 1)
                        else:
                            ve.nop().then_inc(res_used, 1)
                return evac

            def residual_done():
                n_res[0] += 1
                ve.wait_ge(res_used, NQ * NB * n_res[0])

            def split_rows(scale=None):
                for half in range(2):
                    hc = slice(half * HALF, (half + 1) * HALF)
                    for i in range(NT):
                        n_rows[0] += 1
                        ve.wait_ge(rh_done, n_rows[0])
                        if scale is None:
                            ins = ve.tensor_tensor(rows(B1, FR)[:, i, hc], rows(B1)[:, i, hc],
                                                   rows(B2, FR)[:, i, hc].bitcast(F32), ALU.subtract)
                        else:
                            ins = ve.scalar_tensor_tensor(out=rows(B1, FR)[:, i, hc], in0=rows(B1)[:, i, hc],
                                                          scalar=scale[0:R, i:i + 1], in1=rows(B2, FR)[:, i, hc].bitcast(F32),
                                                          op0=ALU.mult, op1=ALU.subtract)
                        ins.then_inc(rl_done, 1)

            def experts(layer):
                blocks, tiles, r, hidden, _ = ffn_shape(layer)
                wid, mt = tiles * r, hidden // P
                hT = ffn_hT(layer)
                piece0 = 0 if layer == 0 else E * 8

                def turned_block(b):
                    xeT = ffn_xeT(layer, b)
                    for k in range(KD):
                        bank = v.read(ve)
                        n_turned[0] += 1
                        ve.wait_ge(th_done, n_turned[0])
                        emptied(ve.tensor_tensor(xeT[:, 1, k, :], bank[:, 0:wid], xeT[:, 0, k, :].bitcast(F32),
                                                 ALU.subtract))

                turned_block(0)
                for b in range(blocks):
                    for mh in range(mt // 2):
                        next_unit()
                        next_unit()
                        for m in range(2):
                            bank = v.read(ve)
                            n = b * mt + 2 * mh + m
                            ve.wait_ge(s_free, gate_at[layer, n])
                            g = RB[:, (n_hid[0] + m) % 4, 0:wid]
                            emptied(ve.tensor_tensor(g, bank[:, 0:wid], g, ALU.mult))
                        for m in range(2):
                            g = RB[:, n_hid[0] % 4, 0:wid]
                            n_hid[0] += 1
                            ve.wait_ge(hh_done, n_hid[0])
                            ve.tensor_tensor(hT[:, 1, 2 * mh + m, :], g, hT[:, 0, 2 * mh + m, :].bitcast(F32),
                                             ALU.subtract).then_inc(hl_done, 1)
                    if b + 1 < blocks:
                        turned_block(b + 1)
                    npiece = tiles * D // HALF
                    for p in range(npiece):
                        if p % (UNIT // mt // HALF * tiles) == 0:
                            next_unit()
                        j = piece0 + b * npiece + p
                        if j % 2 == 0:
                            if j >= 4:
                                ve.wait_ge(y_st[j % 4], 16 * (j // 4))
                            emptied(ve.tensor_copy(ffn_y(layer, j % 4)[0:r, :], v.read(ve)[0:r, :]))
                ve.wait_ge(hl_done, n_hid[0])

            def combine(layer, res, g):
                for n in range(4 * g, 4 * g + 4):
                    i, k = divmod(n, 2)
                    ve.wait_ge(yg_full[n % 4], 16 * (5 * layer + n // 4 + 1))
                    if k:
                        ve.wait_ge(yg_used, 2 * NT * layer + n)
                    ve.scalar_tensor_tensor(out=res[:, i, :], in0=y_slot(layer, n),
                                            scalar=wk[0:R, k, i:i + 1], in1=res[:, i, :],
                                            op0=ALU.mult, op1=ALU.add).then_inc(yg_used, 1)
                ve.wait_ge(yg_used, 2 * NT * layer + 4 * (g + 1))

            small = {}

            def sm(name, n, at):
                small[name] = rbf[0:R, at:at + n]
                return small[name]

            def top2(val):
                mx = sm("mx", NT * E, 1280).rearrange("p (i e) -> p i e", e=E)
                mi = rbf[0:R, 1376:1376 + NT * E].bitcast(U32).rearrange("p (i e) -> p i e", e=E)
                ek = sm("ek", 2 * NT, 1472).rearrange("p (k i) -> p k i", k=2)
                for i in range(NT):
                    d(ve.max(mx[:, i, :], val[:, i, :]))
                d.sync()
                for i in range(NT):
                    d(ve.max_index(mi[:, i, :], mx[:, i, :], val[:, i, :]))
                d.sync()
                d(ve.tensor_copy(ek, mi[:, :, 0:2].rearrange("p i k -> p k i")))
                d.sync()
                return mx, ek

            def onehots(o, ek, k):
                d(ve.tensor_tensor(o, iot8[0:R, :].unsqueeze(1).to_broadcast([R, NT, E]),
                                   ek[:, k, :].unsqueeze(2).to_broadcast([R, NT, E]), ALU.is_equal))

            def ln_x(g):
                ve.wait_ge(x_in[g], 16)
                ln_group(g, rows(B3), rows(B3))

            ln_x(0)
            ln_x(1)
            next_unit()
            ve.memset(v_heads[:, 160, :], 1.0).then_inc(ones_col, 1)
            d(ve.memset(ecnt[:, :], 0.0))
            d(ve.memset(first, 0.0))

            def edges(j):
                if j == NPIECE - 4:
                    ve.wait_ge(edges_in, 32)
                    ve.wait_ge(consts, 8)
                    d(ve.tensor_copy(srcc, srcf.bitcast(I32)))
                    d(ve.tensor_copy(keyf, dstf.bitcast(I32)))
                    d.sync()
                    ve.scalar_tensor_tensor(out=keyf, in0=srcc, scalar=float(T), in1=keyf, op0=ALU.mult,
                                            op1=ALU.add).then_inc(key_ready, 1)
                    ve.wait_ge(key_ready, 1)
                if j < 3:
                    return
                for m in range(edge_batches(j - 3), edge_batches(j - 2)):
                    bank = eq.read(ve)
                    d.sync()
                    if m:
                        ve.wait_ge(eq_free, m)
                    for q in range(4):
                        g = 4 * m + q
                        key = keyf[:, g:g + 1]
                        row = bank[:, q * P:(q + 1) * P]
                        d(ve.scalar_tensor_tensor(out=eqs[:, q, :], in0=row, scalar=key, in1=low[:, :],
                                                  op0=ALU.is_equal, op1=ALU.mult, accum_out=first[:, g:g + 1]))
                        ins = ve.tensor_scalar(eqs[:, 4 + q, :], row, key, None, ALU.is_equal, ALU.add,
                                               accum_out=ecnt[:, g:g + 1])
                        if q == 3:
                            ins.then_inc(eq_free, 1)
                        else:
                            d(ins)

            def evac_v(m):
                if m == 0:
                    ve.wait_ge(table_zero, 16 * 5)
                bi = bias(m)
                emptied(ve.tensor_tensor(pair(B1, *divmod(m, NB)), bank2(), bi, ALU.add))

            def lead_x(b):
                if b and b + 1 < NB:
                    ln_x(b + 1)

            lo_pieces(row_pieces(B2), evac_v, lead=lead_x, after=edges)
            for j in range(NQ * NPIECE, NQ * NPIECE + 3):
                edges(j)
            d.sync()
            ve.wait_ge(eq_free, GROUPS // 4)
            d(ve.tensor_scalar(first, first, 0.0, None, ALU.is_equal))
            d.sync()
            ve.tensor_tensor(ecnt[:, :], ecnt[:, :], first, ALU.mult).then_inc(eidx_ready, 1)
            d(ve.scalar_tensor_tensor(out=srcc, in0=keyf, scalar=dumpc[:, 0:1], in1=first,
                                      op0=ALU.subtract, op1=ALU.mult))
            d.sync()
            ve.tensor_scalar(eidx[:, :], srcc, dumpc[:, 0:1], None, ALU.add).then_inc(eidx_ready, 1)

            def heads_bias(g):
                n = g % (NQ * NB)
                bi = bias(n)
                if n >= 2:
                    ve.wait_ge(s_full, mark["k_s"] + g - 1)
                emptied(ve.tensor_tensor(two(RB[0:R, n % 2, :]), bank2(), bi, ALU.add))

            def heads_sums(g):
                ve.wait_ge(sq_done, g + 1)
                ve.tensor_reduce(hs8[0:R, :], RB[0:R, 2 + g % 2, :].rearrange("p (h e) -> p h e", e=HD), AX, ALU.add)\
                  .then_inc(ss_done, 1)

            def heads_scaled(g):
                t8 = RB[0:R, g % 2, :].rearrange("p (h e) -> p h e", e=HD)
                ve.wait_ge(nrm_done, g + 1)
                d(ve.tensor_scalar(nr8[0:R, :], nr8[0:R, :], 1e-8, None, ALU.add))
                d.sync()
                d(ve.reciprocal(nr8[0:R, :], nr8[0:R, :]))
                d.sync()
                ve.tensor_tensor(t8, t8, nr8[0:R, :].unsqueeze(2).to_broadcast([R, 8, HD]), ALU.mult)\
                  .then_inc(qn_done, 1)

            def heads_k(j):
                if j >= 7 and j % 4 == 3:
                    heads_bias((j - 7) // 4)
                if j >= 8 and j % 4 == 0:
                    heads_sums((j - 8) // 4)
                if j >= 9 and j % 4 == 1:
                    heads_scaled((j - 9) // 4)

            lo_pieces(row_pieces(B2), None, after=heads_k)
            last = NQ * NB - 1
            heads_sums(last - 1)
            heads_scaled(last - 1)
            heads_bias(last)
            heads_sums(last)
            heads_scaled(last)
            for n in range(NH * NT):
                if n >= 4:
                    ve.wait_ge(kp_used, n - 3)
                emptied(ve.tensor_scalar(RB[0:R, n % 4, 0:F0], v.read(ve)[0:R, 0:F0], 0.0, 0.1, ALU.max, ALU.add))
            for n in range(NQ * NB):
                heads_bias(NQ * NB + n)
                heads_sums(NQ * NB + n)
                heads_scaled(NQ * NB + n)
                if n % NB == 1:
                    next_unit()

            def attend(step):
                pr, c = divmod(step, 3)
                c0, cn = CH[c]
                acc = (PA, PS)[step % 2]
                rd = RB[:, 3, 0:cn]
                ve.wait_ge(den_done, 2 * (step + 1))
                d(ve.tensor_scalar(rd, rd, 1e-6, None, ALU.max))
                d.sync()
                d(ve.reciprocal(rd, rd))
                d.sync()
                for hh in range(2):
                    b = slice(64 * hh, 64 * hh + 64)
                    ve.tensor_tensor(cols(B1)[b, pr, c0:c0 + cn], acc[b, hh, 0:cn], RB[b, 3, 0:cn], ALU.mult)\
                      .then_inc(acc_free, 1)

            for n in range(NH * 6):
                cn = CH[n // 4 % 3][1]
                if n >= 3:
                    ve.wait_ge(qp_used, n - 2)
                emptied(ve.tensor_scalar(RB[:, n % 3, 0:cn], v.read(ve)[:, 0:cn], 0.0, 0.1, ALU.max, ALU.add))
                if n >= 5 and n % 4 == 1:
                    attend((n - 5) // 4)
            attend(3 * KD - 1)
            ve.wait_ge(acc_free, NH * 3)
            lo_pieces(row_pieces(B1), add_residual(B3, True))
            residual_done()

            def evac_h(m):
                emptied(ve.tensor_copy(pair(B1, *divmod(m, NB)), bank2()))

            lo_pieces(row_pieces(B2), evac_h)
            for c in range(T // AC):
                next_unit()
                emptied(ve.tensor_copy(rbf[:, c * AC:(c + 1) * AC], v.read(ve)[:, 0:AC]))
            for g in range(3):
                nq = min(4, NT - 4 * g)
                emptied(ve.tensor_copy(dcol[0:R, 4 * g:4 * g + nq],
                                       v.read(ve)[0:R, 0:nq * P].rearrange("p (q c) -> p q c", c=P)[:, :, 0]))
            ve.wait_ge(v_free, v.n)
            ve.tensor_scalar(dcol[0:R, :], dcol[0:R, :], 1.0, None, ALU.add).then_inc(dg_in, 1)
            d(ve.tensor_reduce(dmaxf[0:1, 0:1], rbf[0:1, 0:T], AX, ALU.max))
            d.sync()
            ve.tensor_copy(dmax[0:1, 0:1], dmaxf[0:1, 0:1]).then_inc(dmax_ready, 1)
            ve.wait_ge(dg_sqrt, 1)
            ve.reciprocal(dinv[0:R, :], dinv[0:R, :]).then_inc(dg_in, 1)
            ve.wait_ge(dg_in, 2)
            split_rows(dinv)
            ve.wait_ge(rl_done, n_rows[0])
            ve.wait_ge(deg_stored, 16)
            ve.wait_ge(gcn_b_in, 16)
            n = 0
            for c in range(T // AC):
                next_unit()
                for half in range(2):
                    hc = slice(half * HALF, (half + 1) * HALF)
                    for i in (2 * c, 2 * c + 1):
                        t = RB[0:R, n % 4, :]
                        n += 1
                        emptied(ve.tensor_tensor(t, v.read(ve)[0:R, :], rows(B2, FR)[:, i, hc].bitcast(F32),
                                                 ALU.add))
                        ve.wait_ge(v_free, v.n)
                        d(ve.tensor_tensor(t, t, rows(B1, FR)[:, i, hc].bitcast(F32), ALU.add))
                        d.sync()
                        d(ve.scalar_tensor_tensor(out=t, in0=t, scalar=dinv[0:R, i:i + 1], in1=gcn_b[:, hc],
                                                  op0=ALU.mult, op1=ALU.add))
                        d.sync()
                        d(ve.scalar_tensor_tensor(out=rows(B3)[:, i, hc], in0=t, scalar=0.0, in1=rows(B3)[:, i, hc],
                                                  op0=ALU.max, op1=ALU.add))
            d.sync()

            norm_turned(rows(B3), rows(B1))
            lg = sm("lg", NT * E, 512).rearrange("p (i e) -> p i e", e=E)
            pr = sm("pr", NT * E, 608).rearrange("p (i e) -> p i e", e=E)
            z = sm("z", NT, 704)
            emptied(ve.tensor_copy(small["lg"], v.read(ve)[0:R, 0:NT * E]))
            ve.wait_ge(v_free, v.n)
            d(ve.tensor_reduce(z, lg, AX, ALU.max))
            d.sync()
            ve.tensor_tensor(lg, lg, z.unsqueeze(2).to_broadcast([R, NT, E]), ALU.subtract).then_inc(sm_in, 1)
            ve.wait_ge(sm_exp, 1)
            d(ve.tensor_reduce(z, lg, AX, ALU.add))
            d.sync()
            d(ve.reciprocal(z, z))
            d.sync()
            d(ve.tensor_tensor(pr, lg, z.unsqueeze(2).to_broadcast([R, NT, E]), ALU.mult))
            d.sync()
            mx, ek = top2(pr)
            d(ve.tensor_tensor(z, mx[:, :, 0], mx[:, :, 1], ALU.add))
            d.sync()
            d(ve.tensor_scalar(z, z, 1e-9, None, ALU.add))
            d.sync()
            d(ve.reciprocal(z, z))
            d.sync()
            gts = rbf[0:R, 1024:1024 + 3 * NT * E].rearrange("p (a i e) -> p a i e", a=3, e=E)
            for k in range(2):
                d(ve.tensor_tensor(wk[0:R, k, :], mx[:, :, k], z, ALU.mult))
                onehots(gts[:, 1 + k, :, :], ek, k)
            d.sync()
            d(ve.tensor_tensor(gts[:, 0, :, :], gts[:, 1, :, :],
                               wk[0:R, 0, :].unsqueeze(2).to_broadcast([R, NT, E]), ALU.mult))
            d(ve.tensor_tensor(pr, gts[:, 2, :, :], wk[0:R, 1, :].unsqueeze(2).to_broadcast([R, NT, E]), ALU.mult))
            d.sync()
            ve.tensor_tensor(gts[:, 0, :, :], gts[:, 0, :, :], pr, ALU.add).then_inc(gates_ready, 1)
            gT = F[0:E, B2:B2 + 3 * T].rearrange("p (a t) -> p a t", t=T)
            for a in range(3):
                for g in range(3):
                    w = min(4, NT - 4 * g) * R
                    emptied(ve.tensor_copy(gT[:, a, 4 * g * R:4 * g * R + w], v.read(ve)[0:E, 0:w]))
            rk = sm("rk", 7 * 2 * NT, 0).rearrange("p (a k i) -> p a k i", a=7, k=2)
            scr = RB[0:R, 3, :]
            scr2 = F[0:R, B2 + 4000:B2 + 4000 + HALF]
            d(ve.memset(small["rk"], 0.0))
            d.sync()
            for n in range(2 * NT):
                k, i = divmod(n, NT)
                for c0 in range(0, T, HALF):
                    cn = min(HALF, T - c0)
                    ve.wait_ge(v_free, v.n)
                    d.sync()
                    bank = v.read(ve)[0:R, :]
                    own = (i * R, (i + 1) * R)
                    c = c0 // HALF
                    g = wk[0:R, k, i:i + 1]
                    a, b = max(own[0], c0), min(own[1], c0 + cn)
                    if a < b:
                        d(ve.scalar_tensor_tensor(out=scr2[:, 0:b - a], in0=bank[:, a - c0:b - c0], scalar=g,
                                                  in1=low[0:R, a - own[0]:b - own[0]], op0=ALU.is_equal, op1=ALU.mult,
                                                  accum_out=rk[:, 5 if a > own[0] else 6, k, i:i + 1]))
                    m = min(max(own[0] - c0, 0), cn)
                    parts = [(0, m, ALU.is_ge), (m, cn, ALU.is_gt)]
                    parts = [x for x in parts if x[0] < x[1]]
                    for q, (a, b, op) in enumerate(parts):
                        dst = rk[:, c if (q == 0) else 3 + 0, k, i:i + 1]
                        ins = ve.tensor_scalar(scr[:, a:b], bank[:, a:b], g, None, op, ALU.add, accum_out=dst)
                        if q == len(parts) - 1:
                            emptied(ins)
                        else:
                            d(ins)
            d.sync()
            ve.wait_ge(v_free, v.n)
            rank = sm("rank", 2 * NT, 160).rearrange("p (k i) -> p k i", k=2)
            keep = sm("keep", 2 * NT, 192).rearrange("p (k i) -> p k i", k=2)
            slot = sm("slot", 2 * NT, 224).rearrange("p (k i) -> p k i", k=2)
            dump = sm("dump", 2 * NT, 256).rearrange("p (k i) -> p k i", k=2)
            d(ve.tensor_tensor(rank, rk[:, 0, :, :], rk[:, 1, :, :], ALU.add))
            for a in range(2, 7):
                d.sync()
                d(ve.tensor_tensor(rank, rank, rk[:, a, :, :], ALU.add))
            d.sync()
            d(ve.tensor_scalar(keep, rank, float(CAP), None, ALU.is_lt))
            d(ve.scalar_tensor_tensor(out=slot, in0=ek, scalar=float(CAPR), in1=rank, op0=ALU.mult, op1=ALU.add))
            d(ve.tensor_copy(dump[:, 0, :], tok[0:R, :]))
            d.sync()
            d(ve.tensor_scalar(dump[:, 1, :], dump[:, 0, :], float(E * CAPR + T), None, ALU.add))
            d(ve.tensor_scalar(dump[:, 0, :], dump[:, 0, :], float(E * CAPR), None, ALU.add))
            d.sync()
            d(ve.tensor_tensor(wk[0:R, :, :], wk[0:R, :, :], keep, ALU.mult))
            d(ve.tensor_tensor(rank, slot, dump, ALU.subtract))
            d.sync()
            d(ve.tensor_tensor(rank, rank, keep, ALU.mult))
            ve.tensor_tensor(gidx[0:R, :, :], slot, keep, ALU.mult).then_inc(route_ready, 1)
            d.sync()
            ve.tensor_tensor(sidx[0:R, :, :], rank, dump, ALU.add).then_inc(route_ready, 1)
            experts(0)

            def ln_x2(g):
                combine(0, rows(B3), g)
                ln_group(g, rows(B3), rows(B1))

            def lead_x2(b):
                if b and b + 1 < NB:
                    ln_x2(b + 1)

            def evac_v1(m):
                q, b = divmod(m, NB)
                if q == 0:
                    ve.wait_ge(xn_st[b], 16 * 2)
                bi = bias(m)
                emptied(ve.tensor_tensor(pair(B1, q, b), bank2(), bi, ALU.add))

            ln_x2(0)
            ln_x2(1)
            lo_pieces(row_pieces(B2), evac_v1, lead=lead_x2)
            ve.wait_ge(small_in, 32)
            ve.wait_ge(x2_stored, 16 * NB)

            def heads_cols(which):
                def evac(m):
                    q, c = divmod(m, T // AC)
                    emptied(ve.tensor_tensor(cols(B3)[:, 2 * q:2 * q + 2, c * AC:(c + 1) * AC],
                                             v.read(ve)[:, 0:2 * AC].rearrange("p (m t) -> p m t", m=2),
                                             bcol[:, which, 2 * q:2 * q + 2].unsqueeze(2).to_broadcast([P, 2, AC]),
                                             ALU.add))
                return evac

            lo_pieces(col_pieces(B2), heads_cols(0))
            d(ve.memset(kvbd, 0.0))
            for n in range(2 * NT):
                if n >= 4:
                    ve.wait_ge(kp_used, NH * NT + n - 3)
                emptied(ve.tensor_scalar(RB[0:R, n % 4, :], v.read(ve)[0:R, :], 0.0, 0.125, ALU.max, ALU.mult))
            ve.wait_ge(kp_used, NH * NT + 2 * NT)
            d.sync()
            for half in range(2):
                for q in range(4):
                    for hh in range(2):
                        b = slice(64 * hh, 64 * hh + 64)
                        ve.tensor_copy(kvbd[b, 4 * half + q, 64 * hh:64 * hh + 64],
                                       PA[b, half, q * P + 64 * hh:q * P + 64 * hh + 64]).then_inc(kvbd_ready, 1)
            lo_pieces(col_pieces(B2), heads_cols(1))
            for n in range(3 * KD):
                cn = CH[n % 3][1]
                if n >= 4:
                    ve.wait_ge(s_full, mark["qp1_s"] - 3 * KD + n - 3)
                emptied(ve.tensor_scalar(RB[:, n % 4, 0:cn], v.read(ve)[:, 0:cn], 0.0, 0.125, ALU.max, ALU.mult))
            lo_pieces(row_pieces(B1), add_residual(B3, True))
            residual_done()

            ve.wait_ge(dinv_in, 16)
            d(ve.tensor_scalar(degs, degs, 1.0, None, ALU.max))
            d.sync()
            d(ve.reciprocal(degs, degs))

            def evac_own(m):
                if m >= 4:
                    ve.wait_ge(hs_st[m % 4], 16 * (m // 4))
                bi = bias(m)
                emptied(ve.tensor_tensor(two(RB[0:R, m % 4, :]), bank2(), bi, ALU.add))

            lo_pieces(row_pieces(B2), evac_own)

            def means():
                for c in range(T // AC):
                    next_unit()
                    for f in range(KD):
                        emptied(ve.tensor_tensor(cols(B3)[:, f, c * AC:(c + 1) * AC], v.read(ve)[:, 0:AC],
                                                 degs[:, c * AC:(c + 1) * AC], ALU.mult))

            d.sync()
            split_rows()
            ve.wait_ge(xm_stored, 16 * NQ * NB)
            means()
            lo_pieces(row_pieces(B3), add_residual(B1, False, relu=True))
            residual_done()
            lo_pieces(row_pieces(B2), add_residual(B3, True))
            residual_done()
            split_rows()
            ve.wait_ge(xs_stored, 16 * NQ * NB)
            means()
            lo_pieces(row_pieces(B3), add_residual(B1, False))
            residual_done()

            norm_turned(rows(B1), rows(B3))
            emptied(ve.tensor_copy(small["lg"], v.read(ve)[0:R, 0:NT * E]))
            ve.wait_ge(v_free, v.n)
            d(ve.tensor_copy(pr, lg))
            d.sync()
            mx, ek = top2(pr)
            d2 = rbf[0:R, 512:512 + NT]
            ve.tensor_tensor(d2, mx[:, :, 1], mx[:, :, 0], ALU.subtract).then_inc(sm_in, 1)
            ve.wait_ge(sm_exp, 2)
            d(ve.tensor_scalar(z, d2, 1.0, None, ALU.add))
            d.sync()
            d(ve.reciprocal(z, z))
            d.sync()
            d(ve.tensor_copy(wk[0:R, 0, :], z))
            d(ve.tensor_tensor(wk[0:R, 1, :], d2, z, ALU.mult))
            osum = rbf[0:R, 1024:1024 + NT * E].rearrange("p (i e) -> p i e", e=E)
            oh = [rbf[0:R, 1104 + 80 * k:1184 + 80 * k].rearrange("p (i e) -> p i e", e=E) for k in range(2)]
            for k in range(2):
                onehots(oh[k], ek, k)
            d.sync()
            ve.tensor_tensor(osum, oh[0], oh[1], ALU.add).then_inc(gates_ready, 1)
            pos = sm("pos", NT * E, 800).rearrange("p (i e) -> p i e", e=E)
            tot = sm("tot", NT * E, 896).rearrange("p (i e) -> p i e", e=E)
            bank = v.read(ve)
            d(ve.tensor_copy(small["pos"], bank[0:R, 0:NT * E]))
            emptied(ve.tensor_copy(small["tot"], bank[0:R, P:P + NT * E]))
            ve.wait_ge(v_free, v.n)
            run = sm("run", E, 720)
            nb = sm("nb", E, 736)
            cmp = sm("cmp", E, 752)
            start = sm("start", E, 768)
            d(ve.memset(run, 0.0))
            d.sync()
            for i in range(NT):
                d(ve.tensor_tensor(pos[:, i, :], pos[:, i, :], run, ALU.add))
                d.sync()
                d(ve.tensor_tensor(run, run, tot[:, i, :], ALU.add))
                d.sync()
            d(ve.tensor_scalar(nb, run, 0.0, None, ALU.is_gt))
            for j in range(1, -(-T // 256)):
                d(ve.tensor_scalar(cmp, run, 256.0 * j, None, ALU.is_gt))
                d.sync()
                d(ve.tensor_tensor(nb, nb, cmp, ALU.add))
                d.sync()
            d(ve.memset(start, 0.0))
            d.sync()
            for e in range(1, E):
                d(ve.tensor_tensor(start[:, e:e + 1], start[:, e - 1:e], nb[:, e - 1:e], ALU.add))
                d.sync()
            bl, be, bc = sm("bl", 17, 256), sm("be", 17, 288), sm("bc", 17, 320)
            d(ve.memset(be, 0.0))
            d(ve.tensor_tensor_scan(bl, ones[0:R, 0:17], ones[0:R, 0:17], -1.0, ALU.mult, ALU.add))
            d.sync()
            for e in range(1, E):
                d(ve.tensor_scalar(bc, bl, start[:, e:e + 1], None, ALU.is_ge))
                d.sync()
                d(ve.tensor_tensor(be, be, bc, ALU.add))
                d.sync()
            ve.tensor_copy(eblk[0:R, :], be).then_inc(eblk_ready, 1)
            d(ve.tensor_scalar(start, start, 256.0, None, ALU.mult))
            d.sync()
            d(ve.tensor_tensor(pos, pos, start.unsqueeze(1).to_broadcast([R, NT, E]), ALU.add))
            d.sync()
            slot = sm("slot", 2 * NT, 224).rearrange("p (k i) -> p k i", k=2)
            for k in range(2):
                d(ve.tensor_tensor(oh[k], oh[k], pos, ALU.mult))
                d.sync()
                d(ve.tensor_reduce(slot[:, k, :], oh[k], AX, ALU.add))
            d.sync()
            ve.tensor_copy(gidx[0:R, :, :], slot).then_inc(route_ready, 1)
            ve.tensor_copy(sidx[0:R, :, :], slot).then_inc(route_ready, 1)
            next_unit(True)
            experts(1)
            for g in range(NB):
                combine(1, rows(B1), g)


_NAMES = ['x', 'src', 'dst', 'L0_gnn_W', 'L0_gnn_b', 'L0_mix_Wq', 'L0_mix_bq', 'L0_mix_Wk', 'L0_mix_bk',
          'L0_mix_Wv', 'L0_mix_bv', 'L0_mix_Wo', 'L0_mix_bo', 'L0_mix_projection', 'L0_ffn_router_gate',
          'L0_ffn_gate_w', 'L0_ffn_up_w', 'L0_ffn_down_w', 'L1_gnn_W_self0', 'L1_gnn_W_neigh0', 'L1_gnn_b0',
          'L1_gnn_W_self1', 'L1_gnn_W_neigh1', 'L1_gnn_b1', 'L1_mix_Wq', 'L1_mix_bq', 'L1_mix_Wk', 'L1_mix_bk',
          'L1_mix_Wv', 'L1_mix_bv', 'L1_mix_Wo', 'L1_mix_bo', 'L1_mix_P', 'L1_ffn_w12', 'L1_ffn_w3',
          'L1_ffn_gate_w']


def _layout(name, a, np):
    if name in ("src", "dst"):
        pad = np.full(P * GROUPS - EDGES, T if name == "src" else 0, a.dtype)
        return np.concatenate([a, pad]).reshape(P, GROUPS)
    if name == "L0_mix_projection":
        return a.reshape(KD, 2, F0, HD).transpose(1, 3, 0, 2).reshape(P, KD, F0)
    if name == "L1_mix_P":
        o = np.zeros((2, HD, KD, 2, HD), a.dtype)
        for h in range(2):
            o[h, :, :, h, :] = a.reshape(KD, 2, HD, HD)[:, h].transpose(2, 0, 1)
        return o.reshape(P, KD, P)
    if name in ("L1_mix_bk", "L1_mix_bq"):
        return a.reshape(KD, P).T
    if name in ("L1_mix_Wq", "L1_mix_Wk", "L1_mix_Wv", "L1_mix_Wo", "L1_ffn_gate_w"):
        return a.T
    if name in ("L1_ffn_w12", "L1_ffn_w3"):
        return a.transpose(0, 2, 1)
    return a


def kernel(**inputs):
    import numpy as np
    import concourse.bacc as bacc
    from concourse.bass_utils import run_bass_kernel_spmd

    nc = bacc.Bacc("TRN2", target_bir_lowering=False, num_devices=1)
    arrays, aps = {}, {}
    for name in _NAMES:
        a = np.ascontiguousarray(_layout(name, np.asarray(inputs[name]), np))
        arrays[f"in_{name}"] = a
        aps[name] = nc.dram_tensor(f"in_{name}", a.shape, mybir.dt.from_np(a.dtype), kind="ExternalInput").ap()
    out = nc.dram_tensor("out_x", (T, D), F32, kind="ExternalOutput").ap()
    build(nc, aps, out)
    r = run_bass_kernel_spmd(nc, [arrays], core_ids=[0])
    return r.results[0]["out_x"]
```

```python
from contextlib import ExitStack

import concourse.bass as bass
from concourse import mybir

F32 = mybir.dt.float32
F32R = mybir.dt.float32r
I32 = mybir.dt.int32
U32 = mybir.dt.uint32
ALU = mybir.AluOpType
ACT = mybir.ActivationFunctionType
AX = mybir.AxisListType.X

P = 128
T = 1250
D = 1024
R = 125
NT = T // R
NB = NT // 2
KD = D // P
HALF = 512
QC = 256
NQ = D // QC
NH, HD = 16, 64
F0 = 256
E = 8
EDGES = 21250
GROUPS = 168
TABLE = 128 * 13056
DUMP = T * T + 1
CAP, CAPR = 391, 392
CH = [(0, 418), (418, 416), (834, 416)]
AC = 250
UNIT = 2048
PIECE = 500
NPIECE = 20
EQC = 40
ZC = 2048
HOTS = 5
LATE = 1024.0
BLK = 17
FIXED = (E, 2 * T // 256 + 1)
NFILL = -(-(BLK - FIXED[1]) * 256 // 1024)
NZERO = -(-(TABLE // P) // ZC)

B1 = 0
B2 = B1 + 161 * 64
KVO = B2 + NT * D
PTO = KVO + NH * 2 * P
B3 = PTO + KD * F0
ARENA = B3 + NT * D


class Arena:

    def __init__(self, buffers):
        self.buffers = buffers

    def __getitem__(self, index):
        parts, cols = index
        start, t = [x for x in self.buffers if x[0] <= cols.start][-1]
        return t[parts, cols.start - start:cols.stop - start]


class Chain:

    def __init__(self, eng, sem):
        self.eng, self.sem, self.n = eng, sem, 0

    def __call__(self, ins):
        ins.then_inc(self.sem, 1)
        self.n += 1
        return self.n

    def sync(self):
        self.eng.wait_ge(self.sem, self.n)


class Bank:

    def __init__(self, tensor, full, free, size=3):
        self.t, self.full, self.free, self.size, self.n = tensor, full, free, size, 0

    def take(self, pe):
        if self.n >= self.size:
            pe.wait_ge(self.free, self.n - self.size + 1)
        self.n += 1
        return self.t[:, (self.n - 1) % self.size, :]

    def read(self, eng):
        eng.wait_ge(self.full, self.n + 1)
        self.n += 1
        return self.t[:, (self.n - 1) % self.size, :]


class Unit:

    def __init__(self, kind, stage, place, number):
        self.kind, self.stage, self.place, self.number, self.end = kind, stage, place, number, None


def build(nc, A, out):
    ctx = ExitStack()
    with ctx:
        def sb(name, shape, dt=F32):
            return ctx.enter_context(nc.sbuf_tensor(name, shape, dt))

        def sem(name):
            return ctx.enter_context(nc.semaphore(name))

        def dram(name, shape, dt=F32):
            return nc.dram_tensor(name, shape, dt).ap()

        with nc.sbuf_tensor("b1", [P, B2 - B1], F32) as b1, nc.sbuf_tensor("b2", [P, B3 - B2], F32) as b2:
            pass
        FR = Arena([(B1, sb("b1_split", [P, B2 - B1], F32R)), (B2, sb("b2_split", [P, B3 - B2], F32R))])
        F = Arena([(B1, b1), (B2, b2), (B3, sb("b3", [P, ARENA - B3]))])
        WS = sb("WS", [P, 2, UNIT])
        with nc.sbuf_tensor("WH_plain", [P, 2, 2 * UNIT], F32) as WHF:
            pass
        WH = sb("WH", [P, 2, 2 * UNIT], F32R)
        RB = sb("RB", [P, 4, HALF])
        BI = sb("BI", [P, 2, QC])
        ident = sb("ident", [P, P])
        ones = sb("ones", [P, P])
        low = sb("low", [P, P])
        up = sb("up", [P, P])
        ecnt = sb("ecnt", [P, GROUPS])
        eidx = sb("eidx", [P, GROUPS], I32)
        dcol = sb("dcol", [P, NT])
        dinv = sb("dinv", [P, NT])
        gate_sb = sb("gate_sb", [P, KD, E])
        bcol = sb("bcol", [P, 2, KD])
        hs8 = sb("hs8", [P, 8])
        nr8 = sb("nr8", [P, 8])
        wk = sb("wk", [P, 2, NT])
        gidx = sb("gidx", [P, 2, NT], I32)
        tok = sb("tok", [P, NT])
        rowno = sb("rowno", [P, P])
        tile0 = [sb("tile0_0", [P, E * 4 + 1]), sb("tile0_1", [P, BLK * 2 + 1])]
        dmaxf = sb("dmaxf", [P, 1])
        dmax = sb("dmax", [P, 1], I32)
        dumpc = sb("dumpc", [P, 1])
        tidx = sb("tidx", [P, 34], I32)
        nsel = sb("nsel", [P, E], I32)
        eblk = sb("eblk", [P, BLK + 1], I32)
        iot8 = sb("iot8", [P, E])

        PV = ctx.enter_context(nc.psum_tensor("PV", [P, 3, HALF], F32))
        PS = ctx.enter_context(nc.psum_tensor("PS", [P, 3, HALF], F32))
        PA = ctx.enter_context(nc.psum_tensor("PA", [P, 2, HALF], F32))

        at_d = dram("at_d", [TABLE, 1])
        xn_d = dram("xn_d", [T, D])
        x2_d = dram("x2_d", [T, D])
        xm_d = dram("xm_d", [T, D])
        xs_d = dram("xs_d", [T, D])
        hs_d = dram("hs_d", [T, D])
        key_d = dram("key_d", [GROUPS, P])
        deg_d = dram("deg_d", [1, T])
        y_d = [dram("y0_d", [E * CAPR, D]), dram("y1_d", [BLK * 256, D])]

        rbf = RB[:, :, :].rearrange("p a b -> p (a b)")

        def rows(at, t=F):
            return t[0:R, at:at + NT * D].rearrange("p (i d) -> p i d", d=D)

        def cols(at, t=F):
            return t[:, at:at + KD * T].rearrange("p (k t) -> p k t", t=T)

        def split_ring(g):
            first_q, after_q = mark["q_pieces"]
            at = (B1 if first_q <= g < after_q else KVO) + (g % 4) * 2 * PIECE
            return FR[:, at:at + PIECE], FR[:, at + PIECE:at + 2 * PIECE]

        def unit_parts(u):
            return WH[:, u.place % 2, 0:UNIT], WH[:, u.place % 2, UNIT:2 * UNIT]

        def row_pieces(at):
            return [cols(at)[:, 4 * kh:4 * kh + 4, i * R:(i + 1) * R]
                    for q in range(NQ) for i in range(NT) for kh in range(2)]

        def col_pieces(at):
            return [cols(at)[:, 2 * kq:2 * kq + 2, c * AC:(c + 1) * AC]
                    for q in range(NQ) for c in range(T // AC) for kq in range(4)]

        def pair(at, q, b):
            return rows(at)[:, 2 * b:2 * b + 2, q * QC:(q + 1) * QC]

        def dpair(t, q, b):
            return t[2 * b * R:2 * (b + 1) * R, q * QC:(q + 1) * QC].rearrange("(t p) n -> p t n", p=R)

        def two(ap):
            return ap.rearrange("p (t n) -> p t n", t=2)

        KV = F[:, KVO:PTO].rearrange("p (h f d) -> p h f d", h=NH, f=2)
        PT = F[:, PTO:B3].rearrange("p (k f) -> p k f", f=F0)
        proj = [half[:, pr * 2 * F0:(pr + 1) * 2 * F0] for half in (F[:, PTO:B3], WHF[:, 1, 0:UNIT])
                for pr in range(KD // 2)]

        def q_feats(n):
            return RB[:, n % 6, :] if n % 6 < 4 else WHF[:, 1, UNIT + (n % 6 - 4) * HALF:UNIT + (n % 6 - 3) * HALF]

        def q_norm(step):
            return WHF[:, 1, UNIT + (2 + step % 2) * HALF:UNIT + (3 + step % 2) * HALF]

        def q_acc(step):
            return PA if step % 2 == 0 else PS[:, 0:2, :]

        def kv_acc(pr):
            return PA if pr % 2 == 0 else PS[:, 0:2, :]
        kvbd = PT[:, :, P:2 * P]
        pbd = PT[:, :, 0:P]
        gcn_b = F[0:R, PTO:PTO + D]
        degs = F[:, PTO:PTO + T]
        v_heads = F[0:R, B1:B2].rearrange("p (n d) -> p n d", d=HD)
        at_rows = at_d[0:T * T, :].rearrange("(j p d) o -> p j (d o)", p=R, d=T)
        eqs = F[:, PTO + 5 * GROUPS:PTO + 5 * GROUPS + 4 * P].rearrange("p (q c) -> p q c", c=P)
        later = F[:, PTO + 5 * GROUPS + 4 * P:PTO + 5 * GROUPS + 5 * P]
        keyt = F[0:GROUPS // 2, PTO + 5 * GROUPS:PTO + 5 * GROUPS + 4 * P]

        def key_rows(c):
            return F[:, B3 + (c % 2) * EQC * P:B3 + (c % 2 + 1) * EQC * P]

        keyf, first, srcf, dstf, srcc = (F[:, PTO + a * GROUPS:PTO + (a + 1) * GROUPS] for a in range(5))

        def ln_stats(g):
            at = KVO + 8 * PIECE + (g % 2) * 48
            s = F[0:R, at:at + 48]
            return (s[:, 0:24].rearrange("p (i c s) -> p i c s", i=2, c=2),
                    s[:, 24:28].rearrange("p (i s) -> p i s", s=2), s[:, 28:30], s[:, 32:34], s[:, 36:38])

        XN_TILES = (2, 4)

        def xn_tile(layer, i):
            if layer == 0:
                return F[0:R, PTO + D:PTO + 2 * D] if i % 2 == 0 else rbf[0:R, D:2 * D]
            return F[0:R, B2 + (i % 4) * D:B2 + (i % 4 + 1) * D]

        def xn_cols(layer, b):
            at = (KVO, B2 + 4 * D)[layer] + (b % 2) * KD * 2 * R
            return F[:, at:at + KD * 2 * R].rearrange("p (k t) -> p k t", k=KD)

        def edge_batches(j):
            return max(0, j - NPIECE) * (GROUPS // 4) // ((NQ - 1) * NPIECE)

        def ffn_shape(layer):
            return ((E, 4, CAPR // 4, 512, B1), (BLK, 2, P, 256, B3))[layer]

        def ffn_xe(layer, b):
            _, tiles, _, _, at = ffn_shape(layer)
            at += (b % 2) * tiles * D
            return F[:, at:at + tiles * D].rearrange("p (t d) -> p t d", d=D)

        def choice_hots(layer):
            blocks, tiles, r, _, _ = ffn_shape(layer)
            at, n, w = B2 + (5, 8)[layer] * D, 2 * NT, blocks * tiles
            views, widths = [], (r, w + 1, w)
            for width in widths:
                views.append(FR[0:R, at:at + n * width].rearrange("p (n c) -> p n c", c=width))
                at += n * width
            return views

        def ffn_y(layer, slot):
            at = ffn_shape(layer)[4] + 8 * D + slot * HALF
            return F[:, at:at + HALF]

        def ffn_xeT(layer, b):
            _, tiles, r, _, _ = ffn_shape(layer)
            n = 2 * KD * tiles * r
            at = B2 + (b % 2) * n
            return FR[:, at:at + n].rearrange("p (a k t) -> p a k t", a=2, k=KD)

        def ffn_turns(layer, mh, which, m):
            turns = ((2, 1, 1, 1, 1, 1, 1, 0), (2, 2, 2, 2))[layer]
            at = 4 * mh + 2 * which + m
            return range(sum(turns[0:at]), sum(turns[0:at + 1]))

        def ffn_hT(layer):
            _, tiles, r, hidden, _ = ffn_shape(layer)
            at = B2 + 4 * KD * tiles * r
            n = 2 * hidden // P * tiles * r
            return FR[:, at:at + n].rearrange("p (a k t) -> p a k t", a=2, k=hidden // P)

        def y_slot(layer, n):
            if layer == 1:
                at = B3 + (n % 4) * D
            elif n < 12:
                at = B1 + (6 + n % 4) * D
            else:
                at = (PTO, PTO + D, B1 + 8 * D, B1 + 9 * D)[n % 4]
            return F[0:R, at:at + D]

        v_full, v_free = sem("v_full"), sem("v_free")
        s_full, s_free = sem("s_full"), sem("s_free")
        eq_in = [sem("eq_in0"), sem("eq_in1")]
        eq_used = sem("eq_used")
        key_stored = sem("key_stored")
        t_full, t_free = sem("t_full"), sem("t_free")
        dv, pl, ac = sem("dve_step"), sem("pool_step"), sem("act_step")
        ws_full = [sem(f"ws_full{i}") for i in range(2)]
        wc_full = [sem(f"wc_full{i}") for i in range(2)]
        wh_done, wl_done = sem("wh_done"), sem("wl_done")
        xh_done, xl_done, xs_used = sem("xh_done"), sem("xl_done"), sem("xs_used")
        rh_done, rl_done = sem("rh_done"), sem("rl_done")
        b_full = [sem(f"b_full{i}") for i in range(2)]
        x_in = [sem(f"x_in{i}") for i in range(5)]
        edges_in, small_in, pt_in, gate_in, rg1_in = (sem(n) for n in
                                                      ("edges_in", "small_in", "pt_in", "gate_in", "rg1_in"))
        gcn_b_in, p1_in = sem("gcn_b_in"), sem("p1_in")
        consts = sem("consts")
        key_ready = sem("key_ready")
        eidx_ready, zero_ready, table_zero, scattered = (sem(n) for n in
                                                         ("eidx_ready", "zero_ready", "table_zero", "scattered"))
        ln_var, ln_std, xn_ready = (sem(n) for n in ("ln_var", "ln_std", "xn_ready"))
        xn_st = [sem(f"xn_st{i}") for i in range(NB)]
        xn_rt = [sem(f"xn_rt{i}") for i in range(NB)]
        ones_col = sem("ones_col")
        sq_done, ss_done, nrm_done, qn_done = (sem(n) for n in ("sq_done", "ss_done", "nrm_done", "qn_done"))
        qa_full, qa_free, qa_done, gz_ready = (sem(n) for n in ("qa_full", "qa_free", "qa_done", "gz_ready"))
        kp_used, kv_free, qp_used, acc_free, den_done = (
            sem(n) for n in ("kp_used", "kv_free", "qp_used", "acc_free", "den_done"))
        res_full = [sem(f"res_full{i}") for i in range(4)]
        res_used = sem("res_used")
        hs_st = [sem(f"hs_st{i}") for i in range(4)]
        deg_stored, dg_in, dg_sqrt = sem("deg_stored"), sem("dg_in"), sem("dg_sqrt")
        dmax_ready = sem("dmax_ready")
        rt_full = sem("rt_full")
        sm_in, sm_exp, route_ready = (sem(n) for n in ("sm_in", "sm_exp", "route_ready"))
        gates_ready, nsel_ready = sem("gates_ready"), sem("nsel_ready")
        hot_ready = sem("hot_ready")
        xe_full = [sem("xe_full0"), sem("xe_full1")]
        th_done, hh_done, hl_done = sem("th_done"), sem("hh_done"), sem("hl_done")
        y_filled = sem("y_filled")
        y_st = [sem(f"y_st{i}") for i in range(4)]
        yg_full = [sem(f"yg_full{i}") for i in range(4)]
        yg_used = sem("yg_used")
        x2_stored, xm_stored, xs_stored, xn_back, dinv_in, kvbd_ready = (
            sem(n) for n in ("x2_stored", "xm_stored", "xs_stored", "xn_back", "dinv_in", "kvbd_ready"))
        eblk_ready, out_stored = sem("eblk_ready"), sem("out_stored")

        block = ctx.enter_context(nc.Block())
        mark = {"q_pieces": (0, 0)}
        units = []
        places = []
        staged = []
        xs_end = []
        bias_end = []
        rt_s = {}
        gather_end = {}
        gate_at, up_at, y_at = {}, {}, {}

        @block.tensor
        def _(pe):
            v, s = Bank(PV, v_full, v_free), Bank(PS, s_full, s_free)
            tr = Bank(PA, t_full, t_free, 2)
            count = {"split": 0, "used": 0, "piece": 0, "counts": [0, 0]}

            def unit(kind):
                u = Unit(kind, len(staged), len(places), count["split"])
                units.append(u)
                places.append(u)
                if kind == "split":
                    staged.append(u)
                    count["split"] += 1
                    pe.wait_ge(wl_done, 2 * count["split"])
                else:
                    at = u.place % 2
                    count["counts"][at] += 1
                    pe.wait_ge(wc_full[at], 16 * count["counts"][at])
                return u

            def piece():
                count["piece"] += 1
                pe.wait_ge(xl_done, count["piece"])
                return split_ring(count["piece"] - 1)

            def piece_used(mm, ends_bank):
                if ends_bank:
                    mm.then_inc(v_full, 1)
                    xs_end.append((v_full, v.n))
                else:
                    mm.then_inc(xs_used, 1)
                    count["used"] += 1
                    xs_end.append((xs_used, count["used"]))

            def three(o, a, b, start, stop, **kw):
                pe.matmul(o, a[0], b[0], start=start, stop=False, **kw)
                pe.matmul(o, a[0], b[1], start=False, stop=False, **kw)
                return pe.matmul(o, a[1], b[0], start=False, stop=stop, **kw)

            def turn_tile(row):
                for k0 in (0, 4):
                    bank = s.take(pe)
                    for k in range(4):
                        mm = pe.transpose(bank[:, k * R:(k + 1) * R], row[:, (k0 + k) * P:(k0 + k + 1) * P],
                                          ident[0:R, 0:R])
                    mm.then_inc(s_full, 1)

            def turn_pair(layer, b):
                for i in (2 * b, 2 * b + 1):
                    pe.wait_ge(xn_ready, (1 + 2 * layer) * NT + i + 1)
                    turn_tile(xn_tile(layer, i))
                rt_s[layer, b] = s.n

            def route_pair(layer, b):
                if b == 0:
                    pe.wait_ge((gate_in, rg1_in)[layer], 16)
                pe.wait_ge(s_free, rt_s[layer, b])
                for t in range(2):
                    i = 2 * b + t
                    for k in range(KD):
                        mm = pe.matmul(PA[0:R, 0, i * E:(i + 1) * E], xn_cols(layer, b)[:, k, t * R:(t + 1) * R],
                                       gate_sb[:, k, :], start=(k == 0), stop=(k == KD - 1))
                if b == NB - 1:
                    mm.then_inc(rt_full, 1)

            def linear_rows(name, bias=True, lead=None, between=None):
                mark[name] = v.n
                for q in range(NQ):
                    if lead is None or q:
                        u = unit("split")
                        w = [h.rearrange("p (k n) -> p k n", k=KD) for h in unit_parts(u)]
                    for b in range(NB):
                        if lead is not None and q == 0:
                            lead(b)
                            if b == 0:
                                u = unit("split")
                                w = [h.rearrange("p (k n) -> p k n", k=KD) for h in unit_parts(u)]
                        bank = two(v.take(pe))
                        for t in range(2):
                            for kh in range(2):
                                x = [h.rearrange("p (k t) -> p k t", k=4) for h in piece()]
                                for k in range(4):
                                    mm = three(bank[0:R, t, :], [h[:, k, :] for h in x],
                                               [h[:, 4 * kh + k, :] for h in w],
                                               kh + k == 0, kh * 4 + k == KD - 1)
                                piece_used(mm, t + kh == 2)
                        if between:
                            between(q * NB + b)
                    u.end = (v_full, v.n)
                    if bias:
                        bias_end.append(v.n)

            def linear_cols():
                for q in range(NQ):
                    u = unit("split")
                    w = [h.rearrange("p (k n) -> p k n", k=KD) for h in unit_parts(u)]
                    for c in range(T // AC):
                        bank = v.take(pe)
                        for kq in range(4):
                            x = [h.rearrange("p (k t) -> p k t", k=2) for h in piece()]
                            for k2 in range(2):
                                k = 2 * kq + k2
                                for m in range(2):
                                    mm = three(bank[:, m * AC:(m + 1) * AC],
                                               [h[:, k, m * P:(m + 1) * P] for h in w], [h[:, k2, :] for h in x],
                                               k + m == 0, k == KD - 1, skip_group_check=True)
                            piece_used(mm, kq == 3)
                    u.end = (v_full, v.n)

            def count_rows(u):
                return WH[0:R, u.place % 2, 0:NT * AC].rearrange("p (j d) -> p j d", d=AC)

            def either(product):
                before = (v.n, s.n), len(units), len(places), count["counts"][:]
                most = pe.value_load(dmax[0:1, 0:1], min_val=0, max_val=EDGES)
                with pe.If(most < 4097):
                    product(F32R)
                (v.n, s.n), count["counts"] = before[0], before[3]
                del units[before[1]:], places[before[2]:]
                with pe.Else():
                    product(F32)

            def neighbours_cols(parts, base, dt):
                for c in range(T // AC):
                    u = unit("counts")
                    at = count_rows(u).bitcast(dt)
                    for f in range(KD):
                        if c == 0 and f % 4 == 0:
                            pe.wait_ge(rl_done, base + NT * (1 + f // 4))
                        bank = v.take(pe)
                        for j in range(NT):
                            for a, part in enumerate(parts):
                                mm = pe.matmul(bank[:, 0:AC], part[:, j, f * P:(f + 1) * P].bitcast(dt), at[:, j, :],
                                               start=(j + a == 0), stop=(j + a == NT))
                        mm.then_inc(v_full, 1)
                    u.end = (v_full, v.n)

            def row_tokens(layer):
                blocks, tiles, r, _, _ = ffn_shape(layer)
                at_row, _, at_tile = choice_hots(layer)
                bank = v.take(pe)
                for n in range(2 * NT):
                    if n % HOTS == 0:
                        pe.wait_ge(hot_ready, (layer * 2 * NT + n) // HOTS + 1)
                    mm = pe.matmul(bank[0:r, 0:blocks * tiles], at_row[:, n, :], at_tile[:, n, :],
                                   start=(n == 0), stop=(n == 2 * NT - 1))
                mm.then_inc(v_full, 1)
                mark["rows", layer] = v.n

            def experts(layer):
                blocks, tiles, r, hidden, _ = ffn_shape(layer)
                wid, mt = tiles * r, hidden // P
                hT = ffn_hT(layer)
                hidden_base = 0 if layer == 0 else E * 4

                def turn_bank(b, k):
                    if k == 0:
                        pe.wait_ge(xe_full[b % 2], 16 * (4 * 4 * layer + tiles * (b // 2 + 1)))
                    xe = ffn_xe(layer, b)
                    bank = tr.take(pe)
                    for t in range(tiles):
                        mm = pe.transpose(bank[:, t * r:(t + 1) * r], xe[0:r, t, k * P:(k + 1) * P],
                                          ident[0:r, 0:r])
                    mm.then_inc(t_full, 1)
                    if k == KD - 1:
                        gather_end[layer, b] = (t_full, tr.n)

                def project(b, mh, which, full):
                    ring = (s, v)[which]
                    xeT = ffn_xeT(layer, b)
                    wid = full * r
                    u = unit("split")
                    w = [h.rearrange("p (k n) -> p k n", k=KD) for h in unit_parts(u)]
                    for m in range(2):
                        bank = ring.take(pe)
                        for k in range(KD):
                            mm = three(bank[:, 0:wid], [h[:, k, m * P:(m + 1) * P] for h in w],
                                       [xeT[:, a, k, 0:wid] for a in range(2)], k == 0, k == KD - 1)
                        mm.then_inc(ring.full, 1)
                        (gate_at, up_at)[which][layer, b * mt + 2 * mh + m] = ring.n
                        if m == 1:
                            u.end = (ring.full, ring.n)
                        if b + 1 < blocks:
                            for k in ffn_turns(layer, mh, which, m):
                                turn_bank(b + 1, k)

                def first_gate(b, full):
                    pe.wait_ge(t_free, gather_end[layer, b][1])
                    project(b, 0, 0, full)

                def down(b, full):
                    pe.wait_ge(hl_done, hidden_base + mt * (b + 1))
                    dcols = UNIT // mt
                    for nd in range(D // dcols):
                        u = unit("split")
                        w = [h.rearrange("p (k n) -> p k n", k=mt) for h in unit_parts(u)]
                        for t in range(tiles):
                            for n0 in range(0, dcols, HALF):
                                j = len(y_at)
                                ring = (v, s)[j % 2]
                                bank = ring.take(pe)
                                for k in range(mt if t < full else 1):
                                    if t >= full:
                                        mm = pe.matmul(bank[0:r, :], hT[:, 0, 0, 0:r], w[0][:, 0, n0:n0 + HALF],
                                                       start=True, stop=True)
                                        continue
                                    mm = three(bank[0:r, :], [hT[:, a, k, t * r:(t + 1) * r] for a in range(2)],
                                               [h[:, k, n0:n0 + HALF] for h in w], k == 0, k == mt - 1)
                                mm.then_inc(ring.full, 1)
                                y_at[j] = ring.n
                        u.end = (ring.full, ring.n)

                if layer == 0:
                    pe.wait_ge(nsel_ready, 1)
                    chosen = [pe.value_load(nsel[0:1, e:e + 1], min_val=0, max_val=T) for e in range(E)]
                else:
                    pe.wait_ge(eblk_ready, 1)
                    used = pe.value_load(eblk[0:1, BLK:BLK + 1], min_val=0, max_val=BLK)
                for k in range(KD):
                    turn_bank(0, k)

                def sized(b, step):
                    if layer == 1:
                        step(tiles)
                        return
                    before = (v.n, s.n, tr.n), (units[:], places[:], staged[:]), dict(count), dict(y_at)
                    with pe.If(chosen[b] < (tiles - 1) * r + 1):
                        step(tiles - 1)
                    (v.n, s.n, tr.n), lists = before[0], before[1]
                    units[:], places[:], staged[:] = lists
                    count.update(before[2])
                    for j in set(y_at) - set(before[3]):
                        del y_at[j]
                    with pe.Else():
                        step(tiles)

                def hidden_columns(b, full):
                    project(b, 0, 1, full)
                    for mh in range(1, mt // 2):
                        project(b, mh, 0, full)
                        project(b, mh, 1, full)

                def block(b):
                    if layer == 1 or b == 0:
                        sized(b, lambda full: first_gate(b, full))
                    sized(b, lambda full: hidden_columns(b, full))
                    if layer == 0 and b + 1 < blocks:
                        sized(b + 1, lambda full: first_gate(b + 1, full))
                    sized(b, lambda full: down(b, full))

                for b in range(FIXED[layer]):
                    block(b)
                for b in range(FIXED[layer], blocks):
                    with pe.If(used > b):
                        block(b)

            pe.wait_ge(consts, 8)

            def lead_norm(b, base, src):
                for i in (2 * b, 2 * b + 1):
                    pe.wait_ge(xn_ready, base + i + 1)
                    turn_tile(src[:, i, :])
                if b == NB - 1:
                    mark["lead_s"] = s.n

            linear_rows("v0", lead=lambda b: lead_norm(b, 0, rows(B3)))

            def turn_heads(n):
                pe.wait_ge(qn_done, n + 1)
                bank = s.take(pe)
                for kk in range(2):
                    for t in range(2):
                        mm = pe.transpose(bank[:, (2 * kk + t) * R:(2 * kk + t + 1) * R],
                                          RB[0:R, n % 2, t * QC + kk * P:t * QC + (kk + 1) * P], ident[0:R, 0:R])
                mm.then_inc(s_full, 1)

            mark["k_s"] = s.n
            linear_rows("k0", between=lambda n: turn_heads(n - 2) if n >= 2 else None)
            turn_heads(NQ * NB - 2)
            turn_heads(NQ * NB - 1)
            pe.wait_ge(s_free, s.n)
            pe.wait_ge(pt_in, 16)
            pe.wait_ge(ones_col, 1)
            mark["kp"] = v.n
            for n in range(KD * NT + 2):
                if n < KD * NT:
                    pr, i = divmod(n, NT)
                    if n == KD // 2 * NT:
                        pe.wait_ge(pt_in, 32)
                    pe.matmul(v.take(pe)[0:R, :], cols(B3)[:, pr, i * R:(i + 1) * R], proj[pr],
                              start=True, stop=True).then_inc(v_full, 1)
                if n >= 2:
                    m = n - 2
                    pr, i = divmod(m, NT)
                    pe.wait_ge(v_free, mark["kp"] + m + 1)
                    if i == 0 and pr >= 2:
                        pe.wait_ge(kv_free, 2 * (pr - 1))
                    for hh in range(2):
                        at = i * NH + 2 * pr + hh
                        for f in range(2):
                            mm = pe.matmul(kv_acc(pr)[:, hh, f * P:(f + 1) * P].rearrange("p (c d) -> p c d", c=2),
                                           RB[0:R, m % 4, hh * F0 + f * P:hh * F0 + (f + 1) * P],
                                           v_heads[:, at:161:160 - at, :],
                                           start=(i == 0 and f == 0), stop=(i == NT - 1),
                                           skip_group_check=True)
                    mm.then_inc(kp_used, 1)
            pe.wait_ge(kv_free, NH)
            mark["q_pieces"] = (count["piece"], count["piece"] + NQ * NPIECE)
            linear_rows("q", between=lambda n: turn_heads(NQ * NB + n - 2) if n >= 2 else None)
            turn_heads(2 * NQ * NB - 2)
            turn_heads(2 * NQ * NB - 1)
            pe.wait_ge(s_free, s.n)
            mark["qp"] = v.n
            for n in range(NH * 6 + 4):
                if n < NH * 6:
                    step, hh, f = n // 4, n // 2 % 2, n % 2
                    pr, c = divmod(step, 3)
                    c0, cn = CH[c]
                    if n == NH * 3:
                        pe.wait_ge(pt_in, 48)
                    if f == 0:
                        bank, done = v.take(pe), v_full
                    else:
                        if n >= 2:
                            pe.wait_ge(qa_free, n // 2)
                        bank, done = PS[:, 2, :], qa_full
                    at = hh * F0 + f * P
                    pe.matmul(bank[:, 0:cn], proj[pr][:, at:at + P], cols(B3)[:, pr, c0:c0 + cn],
                              start=True, stop=True).then_inc(done, 1)
                if n >= 4:
                    m = n - 4
                    step, hh, f = m // 4, m // 2 % 2, m % 2
                    pr, c = divmod(step, 3)
                    cn = CH[c][1]
                    if f == 0:
                        pe.wait_ge(v_free, mark["qp"] + m // 2 + 1)
                    else:
                        pe.wait_ge(qa_done, m // 2 + 1)
                    if m % 4 == 0 and step >= 2:
                        pe.wait_ge(acc_free, 2 * (step - 1))
                    pe.matmul(q_acc(step)[:, hh, 0:cn], KV[:, 2 * pr + hh, f, :], q_feats(m)[:, 0:cn],
                              start=(f == 0), stop=(f == 1)).then_inc(qp_used, 1)
            pe.wait_ge(acc_free, NH * 3)
            linear_rows("wo0")

            linear_rows("gcn", bias=False)
            mark["deg"] = v.n
            mark["xl_gcn"] = count["piece"]
            for c in range(T // AC):
                u = unit("counts")
                at = count_rows(u).bitcast(F32)
                bank = v.take(pe)
                for j in range(NT):
                    mm = pe.matmul(bank[:, 0:AC], ones[0:R, :], at[:, j, :], start=(j == 0), stop=(j == NT - 1))
                mm.then_inc(v_full, 1)
                u.end = (v_full, v.n)
            pe.wait_ge(v_free, v.n)
            for g in range(3):
                bank = v.take(pe)
                for q in range(min(4, NT - 4 * g)):
                    i = 4 * g + q
                    mm = pe.transpose(bank[0:R, q * P:(q + 1) * P], rbf[:, i * R:(i + 1) * R], ident[:, :])
                mm.then_inc(v_full, 1)

            def neighbours_rows(dt):
                for c in range(T // AC):
                    u = unit("counts")
                    at = count_rows(u).bitcast(dt)
                    for half in range(2):
                        if c == 0:
                            pe.wait_ge(rl_done, NT * (1 + half))
                        for t in range(2):
                            bank = v.take(pe)
                            for j in range(NT):
                                for a, part in enumerate((rows(B2, FR), rows(B1, FR))):
                                    mm = pe.matmul(bank[0:R, :], at[:, j, t * R:(t + 1) * R],
                                                   part[:, j, half * HALF:(half + 1) * HALF].bitcast(dt),
                                                   start=(j + a == 0), stop=(j + a == NT))
                            mm.then_inc(v_full, 1)
                    u.end = (v_full, v.n)
                    if c >= 1:
                        turn_pair(0, c - 1)
                    if c >= 2:
                        route_pair(0, c - 2)

            pe.wait_ge(dmax_ready, 1)
            either(neighbours_rows)
            route_pair(0, NB - 2)
            turn_pair(0, NB - 1)
            route_pair(0, NB - 1)

            pe.wait_ge(gates_ready, 1)
            gts = rbf[0:R, 1024:1024 + 3 * NT * E].rearrange("p (a i e) -> p a i e", a=3, e=E)
            for a in range(3):
                for g in range(3):
                    bank = v.take(pe)
                    for q in range(min(4, NT - 4 * g)):
                        mm = pe.transpose(bank[0:E, q * R:(q + 1) * R], gts[:, a, 4 * g + q, :], ident[0:R, 0:R])
                    mm.then_inc(v_full, 1)
            pe.matmul(v.take(pe)[0:R, 0:2 * NT * E], ones[0:R, 0:R],
                      rbf[0:R, 1024 + NT * E:1024 + 3 * NT * E], start=True, stop=True).then_inc(v_full, 1)
            pe.wait_ge(v_free, v.n)
            gT = F[:, B2:B2 + 3 * T].rearrange("p (a t) -> p a t", t=T)
            for n in range(2 * NT):
                k, i = divmod(n, NT)
                for c0 in range(0, T, HALF):
                    cn = min(HALF, T - c0)
                    pe.matmul(v.take(pe)[0:R, 0:cn], gT[:, 1 + k, i * R:(i + 1) * R], gT[:, 0, c0:c0 + cn],
                              start=True, stop=True).then_inc(v_full, 1)
            row_tokens(0)
            experts(0)

            linear_rows("v1", lead=lambda b: lead_norm(b, 2 * NT, rows(B1)))
            pe.wait_ge(small_in, 32)
            linear_cols()
            pe.wait_ge(v_free, v.n)
            pe.wait_ge(p1_in, 16)
            mark["kp1"] = v.n
            for n in range(2 * NT + 2):
                if n < 2 * NT:
                    i, half = divmod(n, 2)
                    bank = v.take(pe)
                    for q in range(4):
                        pr = 4 * half + q
                        mm = pe.matmul(bank[0:R, q * P:(q + 1) * P], cols(B3)[:, pr, i * R:(i + 1) * R],
                                       pbd[:, pr, :], start=True, stop=True)
                    mm.then_inc(v_full, 1)
                if n >= 2:
                    m = n - 2
                    i, half = divmod(m, 2)
                    pe.wait_ge(v_free, mark["kp1"] + m + 1)
                    for q in range(4):
                        pr = 4 * half + q
                        mm = pe.matmul(PA[:, half, q * P:(q + 1) * P], RB[0:R, m % 4, q * P:(q + 1) * P],
                                       rows(B1)[:, i, pr * P:(pr + 1) * P], start=(i == 0 and q == 0),
                                       stop=(i == NT - 1), skip_group_check=True)
                    mm.then_inc(kp_used, 1)
            linear_cols()
            pe.wait_ge(v_free, v.n)
            pe.wait_ge(kvbd_ready, NH)
            mark["qp1"] = v.n
            for n in range(3 * KD + 2):
                if n < 3 * KD:
                    pr, c = divmod(n, 3)
                    c0, cn = CH[c]
                    pe.matmul(v.take(pe)[:, 0:cn], pbd[:, pr, :], cols(B3)[:, pr, c0:c0 + cn],
                              start=True, stop=True).then_inc(v_full, 1)
                if n >= 2:
                    m = n - 2
                    pr, c = divmod(m, 3)
                    pe.wait_ge(v_free, mark["qp1"] + m + 1)
                    pe.matmul(s.take(pe)[:, 0:CH[c][1]], kvbd[:, pr, :], RB[:, m % 4, 0:CH[c][1]],
                              start=True, stop=True).then_inc(s_full, 1)
            mark["qp1_s"] = s.n
            linear_rows("wo1")
            mark["xl_wo1"] = count["piece"]

            linear_rows("ws0")
            mark["xl_ws0"] = count["piece"]
            either(lambda dt: neighbours_cols((rows(B2, FR), rows(B1, FR)), 2 * NT, dt))
            mark["agg1"] = v.n
            linear_rows("wn0", bias=False)

            def lead_h1(b):
                pe.wait_ge(res_used, 2 * NQ * NB + (NQ - 1) * NB + b + 1)
                for i in (2 * b, 2 * b + 1):
                    turn_tile(rows(B1)[:, i, :])
                if b == NB - 1:
                    mark["lead_s"] = s.n

            linear_rows("ws1", lead=lead_h1)
            mark["xl_ws1"] = count["piece"]
            either(lambda dt: neighbours_cols((rows(B2, FR), rows(B1, FR)), 4 * NT, dt))
            mark["agg2"] = v.n

            def norm_1(n):
                b = n - (NQ - 1) * NB
                if b >= 2:
                    turn_pair(1, b - 2)
                if b >= 3:
                    route_pair(1, b - 3)

            linear_rows("wn1", bias=False, between=norm_1)
            route_pair(1, NB - 3)
            turn_pair(1, NB - 2)
            route_pair(1, NB - 2)
            turn_pair(1, NB - 1)
            route_pair(1, NB - 1)

            pe.wait_ge(gates_ready, 2)
            bank = v.take(pe)
            osum = rbf[0:R, 1024:1024 + NT * E]
            pe.matmul(bank[0:R, 0:NT * E], up[0:R, 0:R], osum, start=True, stop=True)
            pe.matmul(bank[0:R, P:P + NT * E], ones[0:R, 0:R], osum, start=True, stop=True).then_inc(v_full, 1)
            row_tokens(1)
            mark["routed"] = len(units)
            experts(1)

        @block.sync
        def _(sp):
            n_unit, n_bias = [0], [0]
            n_counts = [0, 0]

            def load(src, k=KD, lead=None):
                u = units[n_unit[0]]
                n_unit[0] += 1
                if u.stage >= 2:
                    sp.wait_ge(wl_done, 2 * (u.stage - 1))
                dst = WS[:, u.stage % 2, :]
                if lead:
                    dst = dst.rearrange("p (a k n) -> p a k n", a=1, k=k)
                else:
                    dst = dst.rearrange("p (k n) -> p k n", k=k)
                sp.dma_start(dst, src).then_inc(ws_full[u.stage % 2], 16)

            def counts():
                for c in range(T // AC):
                    u = units[n_unit[0]]
                    n_unit[0] += 1
                    sp.wait_ge(*places[u.place - 2].end)
                    sp.dma_start(WH[0:R, u.place % 2, 0:NT * AC].bitcast(F32).rearrange("p (j d) -> p j d", d=AC),
                                 at_rows[:, :, c * AC:(c + 1) * AC]).then_inc(wc_full[u.place % 2], 16)

            def bias(vec, q):
                n = n_bias[0]
                n_bias[0] += 1
                if n >= 2:
                    sp.wait_ge(v_free, bias_end[n - 2])
                sp.dma_start(BI[0:R, n % 2, :], vec[q * QC:(q + 1) * QC].partition_broadcast(R))\
                  .then_inc(b_full[n % 2], 16)

            def square(w, q):
                load(w[:, q * QC:(q + 1) * QC].rearrange("(k p) n -> p k n", p=P))

            def linear(w, vec=None):
                for q in range(NQ):
                    square(w, q)
                    if vec is not None:
                        bias(vec, q)

            x_v = A["x"].rearrange("(i p) d -> p i d", p=R)
            for g in range(NB):
                sp.dma_start(rows(B3)[:, 2 * g:2 * g + 2, :], x_v[:, 2 * g:2 * g + 2, :]).then_inc(x_in[g], 16)
                if g == 1:
                    square(A["L0_mix_Wv"], 0)
                    bias(A["L0_mix_bv"], 0)
            for a, (col, name) in enumerate(((srcf, "src"), (dstf, "dst"))):
                sp.dma_start(col.bitcast(I32), A[name][0].rearrange("(p g) -> p g", p=P)).then_inc(edges_in, 16)
                sp.dma_start(keyt[:, 2 * P * a:2 * P * (a + 1)].bitcast(I32),
                             A[name][1].rearrange("(p g) -> p g", p=GROUPS // 2)).then_inc(edges_in, 16)
            for q in range(1, NQ):
                square(A["L0_mix_Wv"], q)
                bias(A["L0_mix_bv"], q)
            sp.dma_start(gate_sb[:, :, :], A["L0_ffn_router_gate"].rearrange("(k p) e -> p k e", p=P))\
              .then_inc(gate_in, 16)
            sp.dma_start(bcol[:, 0, :], A["L1_mix_bk"]).then_inc(small_in, 16)
            sp.dma_start(bcol[:, 1, :], A["L1_mix_bq"]).then_inc(small_in, 16)
            for q in range(NQ):
                square(A["L0_mix_Wk"], q)
                bias(A["L0_mix_bk"], q)
                if q == 2:
                    sp.wait_ge(eidx_ready, 2)
                    sp.dma_start(F[:, PTO:B3], A["L0_mix_projection"][:, 0:UNIT]).then_inc(pt_in, 16)
            for q in range(NQ):
                square(A["L0_mix_Wq"], q)
                bias(A["L0_mix_bq"], q)
                if q == 1:
                    sp.wait_ge(*places[2 * NQ - 1].end)
                    sp.dma_start(WHF[:, 1, 0:UNIT], A["L0_mix_projection"][:, UNIT:2 * UNIT]).then_inc(pt_in, 16)
            for r0 in range(FIXED[1] * 256, BLK * 256, 1024):
                r1 = min(r0 + 1024, BLK * 256)
                sp.dma_start(y_d[1][r0:r1, :], A["x"][0:r1 - r0, :]).then_inc(y_filled, 16)
            for q in range(NQ):
                square(A["L0_mix_Wo"], q)
                bias(A["L0_mix_bo"], q)
                if q == 1:
                    sp.wait_ge(*places[3 * NQ - 1].end)
                    sp.dma_start(WHF[:, 1, 0:UNIT], A["L0_mix_projection"][:, UNIT:2 * UNIT]).then_inc(pt_in, 16)
            linear(A["L0_gnn_W"])
            sp.wait_ge(scattered, 16 * GROUPS)
            counts()
            sp.wait_ge(v_full, mark["deg"])
            sp.dma_start(gcn_b, A["L0_gnn_b"].partition_broadcast(R)).then_inc(gcn_b_in, 16)
            counts()
            gate_w, up_w, down_w = A["L0_ffn_gate_w"], A["L0_ffn_up_w"], A["L0_ffn_down_w"]
            square(gate_w[0], 0)
            for e in range(E):
                square(up_w[e], 0)
                square(gate_w[e], 1)
                square(up_w[e], 1)
                if e + 1 < E:
                    square(gate_w[e + 1], 0)
                for m in range(2):
                    load(down_w[e][:, m * HALF:(m + 1) * HALF].rearrange("(k p) n -> p k n", p=P), 4)
            for q in range(NQ):
                if q == 2:
                    sp.wait_ge(rt_full, 1)
                    sp.wait_ge(yg_used, 2 * NT)
                    sp.dma_start(gate_sb[:, :, :], A["L1_ffn_gate_w"].rearrange("(k p) e -> p k e", p=P))\
                      .then_inc(rg1_in, 16)
                    sp.dma_start(pbd, A["L1_mix_P"]).then_inc(p1_in, 16)
                square(A["L1_mix_Wv"], q)
                bias(A["L1_mix_bv"], q)
            linear(A["L1_mix_Wk"])
            linear(A["L1_mix_Wq"])
            linear(A["L1_mix_Wo"], A["L1_mix_bo"])
            for q in range(NQ):
                square(A["L1_gnn_W_self0"], q)
                bias(A["L1_gnn_b0"], q)
                if q == 1:
                    sp.wait_ge(xl_done, mark["xl_wo1"])
                    for g in range(NB):
                        sp.wait_ge(xn_st[g], 16)
                    sp.dma_start(rows(B1)[:, :, :], xn_d.rearrange("(i p) d -> p i d", p=R)).then_inc(xn_back, 16)
            counts()
            linear(A["L1_gnn_W_neigh0"])
            linear(A["L1_gnn_W_self1"], A["L1_gnn_b1"])
            counts()
            linear(A["L1_gnn_W_neigh1"])
            sp.wait_ge(eblk_ready, 1)

            def gate_up(e, m):
                load(A["L1_ffn_w12"][e][:, :, m * QC:(m + 1) * QC].rearrange("a (k p) n -> p a k n", p=P), KD, True)

            def down(e):
                load(A["L1_ffn_w3"][e].rearrange("a (k p) n -> p a k n", p=P), 2, True)

            def expert(b):
                return bass.DynSlice(sp.value_load(eblk[0:1, b:b + 1], min_val=0, max_val=E - 1), 1)

            def block(b):
                e = expert(b)
                gate_up(e, 1)
                down(e)
                if b + 1 < BLK:
                    gate_up(expert(b + 1), 0)

            used = sp.value_load(eblk[0:1, BLK:BLK + 1], min_val=0, max_val=BLK)
            gate_up(expert(0), 0)
            for b in range(FIXED[1]):
                block(b)
            for b in range(FIXED[1], BLK):
                with sp.If(used > b):
                    block(b)
            for i in range(NT):
                sp.wait_ge(yg_used, 2 * NT + 2 * (i + 1))
                sp.dma_start(out[i * R:(i + 1) * R, :], rows(B1)[:, i, :]).then_inc(out_stored, 16)
            sp.wait_ge(out_stored, 16 * NT)

        @block.gpsimd
        def _(pool):
            pool.memset(rbf[:, 0:ZC], 0.0).then_inc(zero_ready, 1)
            pool.memset(ident[:, :], 0.0).then_inc(consts, 1)
            pool.memset(ones[:, :], 1.0).then_inc(consts, 1)
            pool.iota(tok[:, :], [[R, NT]], base=0, channel_multiplier=1,
                      allow_small_or_imprecise_dtypes=True).then_inc(consts, 1)
            pool.iota(iot8[:, :], [[1, E]], base=0, channel_multiplier=0,
                      allow_small_or_imprecise_dtypes=True).then_inc(consts, 1)
            pool.wait_ge(consts, 4)
            pool.affine_select(out=ident[:, :], in_=ident[:, :], compare_op=ALU.not_equal, fill=1.0, base=0,
                               pattern=[[-1, P]], channel_multiplier=1).then_inc(consts, 1)
            pool.affine_select(out=low[:, :], in_=ones[:, :], compare_op=ALU.is_gt, fill=0.0, base=0,
                               pattern=[[-1, P]], channel_multiplier=1).then_inc(consts, 1)
            pool.affine_select(out=up[:, :], in_=ones[:, :], compare_op=ALU.is_gt, fill=0.0, base=0,
                               pattern=[[1, P]], channel_multiplier=-1).then_inc(consts, 1)
            pool.iota(dumpc[:, :], [[0, 1]], base=DUMP, channel_multiplier=1,
                      allow_small_or_imprecise_dtypes=True).then_inc(consts, 1)
            pool.wait_ge(zero_ready, 1)
            pool.wait_ge(x_in[NB - 1], 16)
            table = at_d.rearrange("(p c) o -> p (c o)", p=P)
            for a in range(0, TABLE // P, ZC):
                n = min(ZC, TABLE // P - a)
                pool.dma_start(table[:, a:a + n], rbf[:, 0:n]).then_inc(table_zero, 16)
            pool.wait_ge(key_ready, 1)
            pool.dma_start(key_d.rearrange("(p a) c -> p (a c)", a=2), keyt[:, 0:2 * P]).then_inc(key_stored, 16)
            pool.wait_ge(key_stored, 16)
            for c in range(-(-GROUPS // EQC)):
                if c < 2:
                    pool.wait_ge(v_full, mark["v0"] + (3, NB)[c])
                else:
                    pool.wait_ge(eq_used, (c - 1) * EQC // 4)
                n = min(EQC, GROUPS - c * EQC)
                pool.dma_start(key_rows(c)[:, 0:n * P],
                               key_d.rearrange("g c -> (g c)")[c * EQC * P:(c * EQC + n) * P].partition_broadcast(P))\
                    .then_inc(eq_in[c % 2], 16)
            pool.wait_ge(table_zero, 16 * NZERO)
            pool.wait_ge(eidx_ready, 2)
            for g in range(GROUPS):
                if g:
                    pool.wait_ge(scattered, 16 * g)
                pool.indirect_dma_start(out=at_d, out_offset=bass.IndirectOffsetOnAxis(ap=eidx[:, g:g + 1], axis=0),
                                        in_=ecnt[:, g:g + 1], in_offset=None, compute_op=ALU.add)\
                    .then_inc(scattered, 16)

            pool.iota(rowno[:, :], [[1, P]], base=0, channel_multiplier=0,
                      allow_small_or_imprecise_dtypes=True).then_inc(consts, 1)
            for layer in range(2):
                blocks, tiles, r, _, _ = ffn_shape(layer)
                pool.iota(tile0[layer][:, :], [[r, blocks * tiles + 1]], base=0, channel_multiplier=0,
                          allow_small_or_imprecise_dtypes=True).then_inc(consts, 1)

            pool.wait_ge(rt_full, 1)
            pool.memset(F[:, B2:B2 + 3 * T], 0.0).then_inc(gz_ready, 1)

            for layer in range(2):
                blocks, tiles, r, _, _ = ffn_shape(layer)
                pool.wait_ge(v_free, mark["rows", layer])
                for g in range(NB):
                    pool.wait_ge(xn_rt[g], 16 * 2 * (1 + layer))
                def gather(b):
                    if b >= 2:
                        pool.wait_ge(*gather_end[layer, b - 2])
                    for t in range(tiles):
                        c = b * tiles + t
                        pool.indirect_dma_start(out=ffn_xe(layer, b)[0:r, t, :], out_offset=None, in_=xn_d,
                                                in_offset=bass.IndirectOffsetOnAxis(ap=tidx[0:r, c:c + 1], axis=0))\
                            .then_inc(xe_full[b % 2], 16)

                if layer == 1:
                    used = pool.value_load(eblk[0:1, BLK:BLK + 1], min_val=0, max_val=BLK)
                for b in range(min(FIXED[layer] + 1, blocks)):
                    gather(b)
                for b in range(FIXED[layer] + 1, blocks):
                    with pool.If(used > b - 1):
                        gather(b)
                pool.wait_ge(route_ready, layer + 1)
                if layer == 1:
                    pool.wait_ge(y_filled, 16 * NFILL)
                def results_stored(pieces):
                    for q in range(4):
                        pool.wait_ge(y_st[q], 16 * pieces // 4)

                results_stored(E * 8 + layer * FIXED[1] * 4)
                for b in range(FIXED[layer], blocks):
                    with pool.If(used > b):
                        results_stored(E * 8 + (b + 1) * 4)
                for n in range(2 * NT):
                    i, k = divmod(n, 2)
                    if n >= 4:
                        pool.wait_ge(yg_used, 2 * NT * layer + n - 3)
                    pool.indirect_dma_start(out=y_slot(layer, n), out_offset=None, in_=y_d[layer],
                                            in_offset=bass.IndirectOffsetOnAxis(ap=gidx[0:R, k, i:i + 1], axis=0))\
                        .then_inc(yg_full[n % 4], 16)

        @block.scalar
        def _(act):
            s = Bank(PS, s_full, s_free)
            n_unit, n_piece, n_res, n_ln, n_silu, n_hid, n_turned = [0], [0], [0], [0], [0], [0], [0]

            def next_unit(routed=False):
                if n_unit[0] == mark["routed"] and not routed:
                    return
                if n_unit[0] < len(units) and units[n_unit[0]].kind == "split":
                    u = units[n_unit[0]]
                    act.wait_ge(ws_full[u.stage % 2], 16 * (u.stage // 2 + 1))
                    if u.place >= 2:
                        act.wait_ge(*places[u.place - 2].end)
                    for a in (0, UNIT // 2):
                        act.copy(WH[:, u.place % 2, a:a + UNIT // 2], WS[:, u.stage % 2, a:a + UNIT // 2])\
                           .then_inc(wh_done, 1)
                n_unit[0] += 1

            def hi_pieces(views, lead=None, extra=None):
                for j, src in enumerate(views):
                    if lead and j < NPIECE and j % 4 == 0:
                        lead(j // 4)
                    if j % NPIECE == 8:
                        next_unit()
                    g = n_piece[0]
                    n_piece[0] += 1
                    if g >= 4:
                        act.wait_ge(*xs_end[g - 4])
                    hi = split_ring(g)[0].rearrange("p (k t) -> p k t", k=src.shape[1])
                    act.copy(hi, src).then_inc(xh_done, 1)
                    if extra:
                        extra(j)

            def ln_sqrt(g):
                _, _, var, std, _ = ln_stats(g)
                n_ln[0] += 1
                act.wait_ge(ln_var, n_ln[0])
                act.activation(std, var, ACT.Sqrt).then_inc(ln_std, 1)

            def turned_tile(i, k0):
                act.copy(cols(B2)[:, k0:k0 + 4, i * R:(i + 1) * R],
                         s.read(act)[:, 0:4 * R].rearrange("p (k t) -> p k t", t=R)).then_inc(s_free, 1)

            def turned_pair(b):
                for i in (2 * b, 2 * b + 1):
                    for k0 in (0, 4):
                        turned_tile(i, k0)
                act.wait_ge(s_free, s.n)

            def store_xn(src, g, base):
                act.wait_ge(xn_ready, base + 2 * g + 2)
                act.dma_start(xn_d[2 * g * R:2 * (g + 1) * R, :].rearrange("(t p) d -> p t d", p=R),
                              src[:, 2 * g:2 * g + 2, :]).then_inc(xn_st[g], 16)

            def piece_at(j, lag):
                return (j - lag) // 4 if j >= lag and (j - lag) % 4 == 0 else None

            def residual_piece(src, m):
                if m >= 4:
                    act.wait_ge(res_used, NQ * NB * n_res[0] + m - 3)
                act.dma_start(two(RB[0:R, m % 4, :]), dpair(src, *divmod(m, NB))).then_inc(res_full[m % 4], 16)

            def linear_residual(at, src, lead=None, store=None, also=None):
                def store_piece(m):
                    act.wait_ge(res_used, NQ * NB * n_res[0] + m + 1)
                    act.dma_start(dpair(store[0], *divmod(m, NB)), pair(B3, *divmod(m, NB))).then_inc(store[1], 16)

                def extra(j):
                    m = piece_at(j, 9)
                    if m is not None and m + 4 < NQ * NB:
                        residual_piece(src, m + 4)
                    m = piece_at(j, 10)
                    if m is not None and store:
                        store_piece(m)
                    if also:
                        also(j)

                if n_res[0]:
                    act.wait_ge(res_used, NQ * NB * n_res[0])
                for m in range(4):
                    residual_piece(src, m)
                hi_pieces(row_pieces(at), lead=lead, extra=extra)
                if store:
                    store_piece(NQ * NB - 2)
                    store_piece(NQ * NB - 1)
                n_res[0] += 1

            def square(g):
                n = g % (NQ * NB)
                act.wait_ge(v_free, mark["k0" if g < NQ * NB else "q"] + n + 1)
                act.activation(RB[0:R, 2 + n % 2, :], RB[0:R, n % 2, :], ACT.Square).then_inc(sq_done, 1)

            def norm(g):
                act.wait_ge(ss_done, g + 1)
                act.activation(nr8[0:R, :], hs8[0:R, :], ACT.Sqrt).then_inc(nrm_done, 1)

            def turned_heads(n):
                q, b = divmod(n, NB)
                act.copy(cols(B3)[:, 2 * q:2 * q + 2, 2 * b * R:2 * (b + 1) * R],
                         s.read(act)[:, 0:4 * R].rearrange("p (k t) -> p k t", k=2)).then_inc(s_free, 1)

            def split_rows(scale=None):
                for half in range(2):
                    hc = slice(half * HALF, (half + 1) * HALF)
                    for i in range(NT):
                        if scale is None:
                            act.copy(rows(B2, FR)[:, i, hc], rows(B1)[:, i, hc]).then_inc(rh_done, 1)
                        else:
                            act.activation(rows(B2, FR)[:, i, hc], rows(B1)[:, i, hc], ACT.Copy,
                                           scale=scale[0:R, i:i + 1]).then_inc(rh_done, 1)

            def store_normed(layer, b):
                for i in (2 * b, 2 * b + 1):
                    act.wait_ge(xn_ready, (1 + 2 * layer) * NT + i + 1)
                    act.dma_start(xn_d[i * R:(i + 1) * R, :], xn_tile(layer, i)).then_inc(xn_rt[b], 16)

            def routed_pair(layer, b):
                for t in range(2):
                    for k0 in (0, 4):
                        act.copy(xn_cols(layer, b)[:, k0:k0 + 4, t * R:(t + 1) * R],
                                 s.read(act)[:, 0:4 * R].rearrange("p (k t) -> p k t", t=R)).then_inc(s_free, 1)

            def experts(layer):
                blocks, tiles, r, hidden, _ = ffn_shape(layer)
                wid, mt = tiles * r, hidden // P
                hT = ffn_hT(layer)
                piece0 = 0 if layer == 0 else E * 8

                def turned_bank(b, k):
                    n = n_turned[0]
                    n_turned[0] += 1
                    act.wait_ge(t_full, n + 1)
                    act.copy(ffn_xeT(layer, b)[:, 0, k, :], PA[:, n % 2, 0:wid]).then_inc(th_done, 1)

                def next_block(b, mh, which, m):
                    if b + 1 < blocks:
                        for k in ffn_turns(layer, mh, which, m):
                            turned_bank(b + 1, k)

                if layer == 1:
                    act.wait_ge(y_filled, 16 * NFILL)
                    act.wait_ge(eblk_ready, 1)
                    used = act.value_load(eblk[0:1, BLK:BLK + 1], min_val=0, max_val=BLK)
                for k in range(KD):
                    turned_bank(0, k)

                def gate(b, mh):
                    next_unit()
                    for m in range(2):
                        n = n_silu[0]
                        n_silu[0] += 1
                        if n >= 4:
                            act.wait_ge(hl_done, n - 3)
                        act.activation(RB[:, n % 4, 0:wid], s.read(act)[:, 0:wid], ACT.Silu).then_inc(s_free, 1)
                        next_block(b, mh, 0, m)

                def up_(b, mh):
                    next_unit()
                    for m in range(2):
                        n = n_hid[0]
                        n_hid[0] += 1
                        act.wait_ge(v_free, up_at[layer, b * mt + 2 * mh + m])
                        act.copy(hT[:, 0, 2 * mh + m, :], RB[:, n % 4, 0:wid]).then_inc(hh_done, 1)
                        next_block(b, mh, 1, m)

                def results(b):
                    npiece = tiles * D // HALF
                    for p in range(npiece):
                        if p % (UNIT // mt // HALF * tiles) == 0:
                            next_unit()
                        j = piece0 + b * npiece + p
                        if j % 2 == 0:
                            continue
                        if j >= 4:
                            act.wait_ge(y_st[j % 4], 16 * (j // 4))
                        act.copy(ffn_y(layer, j % 4)[0:r, :], s.read(act)[0:r, :]).then_inc(s_free, 1)
                        for jj, pp, done in ((j - 1, p - 1, v_free), (j, p, s_free)):
                            nd, t = divmod(pp, tiles) if layer == 0 else (pp % 2, pp // 2)
                            act.wait_ge(done, y_at[jj])
                            act.dma_start(y_d[layer][(b * tiles + t) * r:(b * tiles + t + 1) * r,
                                                     nd * HALF:(nd + 1) * HALF],
                                          ffn_y(layer, jj % 4)[0:r, :]).then_inc(y_st[jj % 4], 16)

                def block(b):
                    if layer == 1 or b == 0:
                        gate(b, 0)
                    up_(b, 0)
                    for mh in range(1, mt // 2):
                        gate(b, mh)
                        up_(b, mh)
                    if layer == 0 and b + 1 < blocks:
                        gate(b + 1, 0)
                    results(b)

                for b in range(FIXED[layer]):
                    block(b)
                for b in range(FIXED[layer], blocks):
                    with act.If(used > b):
                        block(b)

            ln_sqrt(0)
            ln_sqrt(1)
            next_unit()

            def lead_x(b):
                if b and b + 1 < NB:
                    ln_sqrt(b + 1)
                turned_pair(b)

            hi_pieces(row_pieces(B2), lead=lead_x)

            last = NQ * NB - 1

            def head_pieces(g):
                def heads(j):
                    n = piece_at(j, 8)
                    if n is not None:
                        square(g + n)
                    n = piece_at(j, 9)
                    if n is not None:
                        norm(g + n)
                    n = piece_at(j, 15)
                    if n is not None:
                        turned_heads(n)

                hi_pieces(row_pieces(B2), extra=heads)
                square(g + last - 1)
                norm(g + last - 1)
                turned_heads(last - 2)
                square(g + last)
                norm(g + last)
                turned_heads(last - 1)
                turned_heads(last)

            act.wait_ge(eq_used, GROUPS // 4)
            head_pieces(0)
            for h in range(NH):
                if h % 2 == 0:
                    act.wait_ge(kp_used, NT * (h // 2 + 1))
                kvp = kv_acc(h // 2)[:, h % 2, 0:2 * P].rearrange("p (f c d) -> p f c d", f=2, c=2)
                dst = KV[:, h, :, :].rearrange("p f (c d) -> p f c d", c=2)
                if h % 2 == 0:
                    act.copy(dst, kvp).then_inc(kv_free, 1)
                else:
                    act.copy(dst[:, :, 1, :], kvp[:, :, 0, :]).then_inc(ac, 1)
                    act.copy(dst[:, :, 0, :], kvp[:, :, 1, :]).then_inc(kv_free, 1)
            head_pieces(NQ * NB)

            def normalisers(step):
                cn = CH[step % 3][1]
                act.wait_ge(qp_used, 4 * (step + 1))
                if step >= 2:
                    act.wait_ge(acc_free, 2 * (step - 1))
                act.copy(q_norm(step)[0:64, 0:cn], q_acc(step)[64:128, 0, 0:cn]).then_inc(den_done, 1)
                act.copy(q_norm(step)[64:128, 0:cn], q_acc(step)[0:64, 1, 0:cn]).then_inc(den_done, 1)

            for n in range(1, NH * 6, 2):
                cn = CH[n // 4 % 3][1]
                q = q_feats(n)[:, 0:cn]
                if n >= 6:
                    act.wait_ge(qp_used, n - 5)
                act.wait_ge(qa_full, n // 2 + 1)
                act.activation(q, PS[:, 2, 0:cn], ACT.Relu).then_inc(qa_free, 1)
                act.wait_ge(qa_free, n // 2 + 1)
                act.activation(q, q, ACT.Copy, bias=0.1).then_inc(qa_done, 1)
                if n >= 7 and n % 4 == 3:
                    normalisers((n - 7) // 4)
            normalisers(3 * KD - 1)
            act.wait_ge(acc_free, NH * 3)
            linear_residual(B1, A["x"])

            hi_pieces(row_pieces(B2))
            for c in range(T // AC):
                next_unit()
            act.wait_ge(v_free, mark["deg"] + 5)
            act.dma_start(deg_d, rbf[0:1, 0:T]).then_inc(deg_stored, 16)
            act.wait_ge(dg_in, 1)
            act.activation(dinv[0:R, :], dcol[0:R, :], ACT.Sqrt).then_inc(dg_sqrt, 1)
            act.wait_ge(xl_done, mark["xl_gcn"])
            act.wait_ge(dg_in, 2)
            split_rows(dinv)
            for c in range(T // AC):
                next_unit()
                if c:
                    routed_pair(0, c - 1)
                ln_sqrt(c)
                store_normed(0, c)
            routed_pair(0, NB - 1)

            pe_ = rbf[0:R, 512:512 + NT * E]
            act.wait_ge(sm_in, 1)
            act.activation(pe_, pe_, ACT.Exp).then_inc(sm_exp, 1)
            experts(0)

            def store_x2(j):
                g = j - NPIECE
                if not 0 <= g < NB:
                    return
                act.wait_ge(yg_used, 4 * (g + 1))
                act.dma_start(x2_d[2 * g * R:2 * (g + 1) * R, :].rearrange("(t p) d -> p t d", p=R),
                              rows(B3)[:, 2 * g:2 * g + 2, :]).then_inc(x2_stored, 16)

            def lead_x2(b):
                if b and b + 1 < NB:
                    ln_sqrt(b + 1)
                store_xn(rows(B1), b, 2 * NT)
                turned_pair(b)

            ln_sqrt(0)
            ln_sqrt(1)
            hi_pieces(row_pieces(B2), lead=lead_x2, extra=store_x2)
            hi_pieces(col_pieces(B2))
            hi_pieces(col_pieces(B2))
            for m in range(3 * KD):
                pr, c = divmod(m, 3)
                c0, cn = CH[c]
                act.copy(cols(B1)[:, pr, c0:c0 + cn], s.read(act)[:, 0:cn]).then_inc(s_free, 1)
            act.wait_ge(s_free, s.n)
            act.wait_ge(deg_stored, 16)
            act.dma_start(degs, deg_d[0, :].partition_broadcast(P)).then_inc(dinv_in, 16)
            act.wait_ge(x2_stored, 16 * NB)
            linear_residual(B1, x2_d, store=(xm_d, xm_stored))

            def store_own(m):
                act.wait_ge(v_free, mark["ws0"] + m + 1)
                act.dma_start(dpair(hs_d, *divmod(m, NB)), two(RB[0:R, m % 4, :])).then_inc(hs_st[m % 4], 16)

            def own_part(j):
                m = piece_at(j, 10)
                if m is not None:
                    store_own(m)

            hi_pieces(row_pieces(B2), extra=own_part)
            store_own(last - 1)
            store_own(last)
            act.wait_ge(xn_back, 16)
            act.wait_ge(xl_done, mark["xl_ws0"])
            split_rows()
            for c in range(T // AC):
                next_unit()
            act.wait_ge(v_free, mark["agg1"])
            for q in range(4):
                act.wait_ge(hs_st[q], 16 * NQ * NB // 4)
            linear_residual(B3, hs_d)
            act.wait_ge(xm_stored, 16 * NQ * NB)
            linear_residual(B2, xm_d, lead=turned_pair, store=(xs_d, xs_stored))
            act.wait_ge(xl_done, mark["xl_ws1"])
            split_rows()
            for c in range(T // AC):
                next_unit()
            act.wait_ge(v_free, mark["agg2"])
            act.wait_ge(xs_stored, 16 * NQ * NB)

            def norm_1(j):
                m = piece_at(j, 8)
                b = -1 if m is None else m - (NQ - 1) * NB
                if b >= 1:
                    store_normed(1, b - 1)
                    routed_pair(1, b - 1)
                if b >= 0:
                    ln_sqrt(b)

            linear_residual(B3, xs_d, also=norm_1)
            for j in (NQ * NPIECE, NQ * NPIECE + 4):
                norm_1(j)
            store_normed(1, NB - 1)
            routed_pair(1, NB - 1)

            act.wait_ge(sm_in, 2)
            d2 = rbf[0:R, 512:512 + NT]
            act.activation(d2, d2, ACT.Exp).then_inc(sm_exp, 1)
            next_unit(True)
            experts(1)

        @block.vector
        def _(ve):
            d = Chain(ve, dv)
            v = Bank(PV, v_full, v_free)
            n_unit, n_piece, n_half, n_rows = [0], [0], [0], [0]
            n_bias, n_res, n_ln, n_hid, n_turned = [0], [0], [0], [0], [0]

            def next_unit(routed=False):
                if n_unit[0] == mark["routed"] and not routed:
                    return
                if n_unit[0] < len(units) and units[n_unit[0]].kind == "split":
                    u = units[n_unit[0]]
                    for a in (0, UNIT // 2):
                        n_half[0] += 1
                        ve.wait_ge(wh_done, n_half[0])
                        ve.tensor_tensor(WH[:, u.place % 2, UNIT + a:UNIT + a + UNIT // 2],
                                         WS[:, u.stage % 2, a:a + UNIT // 2],
                                         WH[:, u.place % 2, a:a + UNIT // 2].bitcast(F32),
                                         ALU.subtract).then_inc(wl_done, 1)
                n_unit[0] += 1

            def lo_pieces(views, evac, lead=None, after=None):
                for j, src in enumerate(views):
                    if lead and j < NPIECE and j % 4 == 0:
                        lead(j // 4)
                    if j % NPIECE == 8:
                        next_unit()
                    g = n_piece[0]
                    n_piece[0] += 1
                    hi, lo = (h.rearrange("p (k t) -> p k t", k=src.shape[1]) for h in split_ring(g))
                    ve.wait_ge(xh_done, g + 1)
                    ve.tensor_tensor(lo, src, hi.bitcast(F32), ALU.subtract).then_inc(xl_done, 1)
                    if evac and j >= 7 and j % 4 == 3:
                        evac((j - 7) // 4)
                    if after:
                        after(j)
                if evac:
                    evac(NQ * NB - 1)

            def bias(m):
                if m % NB == 0:
                    ve.wait_ge(b_full[n_bias[0] % 2], 16 * (n_bias[0] // 2 + 1))
                    n_bias[0] += 1
                return BI[0:R, (n_bias[0] - 1) % 2, :].unsqueeze(1).to_broadcast([R, 2, QC])

            def emptied(ins):
                ins.then_inc(v_free, 1)

            def bank2():
                return two(v.read(ve))[0:R, :, :]

            def ln_group(g, x, xn):
                st, mv, var, std, rstd = ln_stats(g)
                n_ln[0] += 1
                d.sync()
                for t in range(2):
                    for c in range(2):
                        d(ve.bn_stats(st[:, t, c, :], x(2 * g + t)[:, c * HALF:(c + 1) * HALF]))
                d.sync()
                for t in range(2):
                    d(ve.bn_aggr(mv[:, t, :], st[:, t, :, :]))
                d.sync()
                ve.tensor_scalar(var, mv[:, :, 1], 1e-5, None, ALU.add).then_inc(ln_var, 1)
                ve.wait_ge(ln_std, n_ln[0])
                d(ve.reciprocal(rstd, std))
                d.sync()
                for t in range(2):
                    ve.tensor_scalar(xn(2 * g + t), x(2 * g + t), mv[:, t, 0:1], rstd[:, t:t + 1],
                                     ALU.subtract, ALU.mult).then_inc(xn_ready, 1)

            def row(at):
                return lambda i: rows(at)[:, i, :]

            def ln_routed(layer, b):
                back = XN_TILES[layer] // 2
                if b >= back:
                    ve.wait_ge(s_full, rt_s[layer, b - back])
                    ve.wait_ge(xn_rt[b - back], 16 * 2 * (layer + 1))
                ln_group(b, row((B3, B1)[layer]), lambda i: xn_tile(layer, i))

            def scores(layer):
                ve.wait_ge(rt_full, layer + 1)
                for b in range(NB - XN_TILES[layer] // 2, NB):
                    ve.wait_ge(xn_rt[b], 16 * 2 * (layer + 1))
                d(ve.tensor_copy(small["lg"], PA[0:R, 0, 0:NT * E]))
                d.sync()

            def add_residual(at, with_bias, relu=False):
                def evac(m):
                    q, b = divmod(m, NB)
                    o = pair(at, q, b)
                    piece = two(RB[0:R, m % 4, :])
                    n = NQ * NB * n_res[0] + m
                    if with_bias:
                        bi = bias(m)
                        emptied(ve.tensor_tensor(o, bank2(), bi, ALU.add))
                        ve.wait_ge(v_free, v.n)
                        ve.wait_ge(res_full[m % 4], 16 * (n // 4 + 1))
                        ve.tensor_tensor(o, o, piece, ALU.add).then_inc(res_used, 1)
                    else:
                        ve.wait_ge(res_full[m % 4], 16 * (n // 4 + 1))
                        emptied(ve.tensor_tensor(o, bank2(), piece, ALU.add))
                        ve.wait_ge(v_free, v.n)
                        if relu:
                            ve.tensor_scalar(o, o, 0.0, None, ALU.max).then_inc(res_used, 1)
                        else:
                            ve.nop().then_inc(res_used, 1)
                return evac

            def residual_done():
                n_res[0] += 1
                ve.wait_ge(res_used, NQ * NB * n_res[0])

            def split_rows(scale=None):
                for half in range(2):
                    hc = slice(half * HALF, (half + 1) * HALF)
                    for i in range(NT):
                        n_rows[0] += 1
                        ve.wait_ge(rh_done, n_rows[0])
                        if scale is None:
                            ins = ve.tensor_tensor(rows(B1, FR)[:, i, hc], rows(B1)[:, i, hc],
                                                   rows(B2, FR)[:, i, hc].bitcast(F32), ALU.subtract)
                        else:
                            ins = ve.scalar_tensor_tensor(out=rows(B1, FR)[:, i, hc], in0=rows(B1)[:, i, hc],
                                                          scalar=scale[0:R, i:i + 1], in1=rows(B2, FR)[:, i, hc].bitcast(F32),
                                                          op0=ALU.mult, op1=ALU.subtract)
                        ins.then_inc(rl_done, 1)

            def row_tokens(layer):
                blocks, tiles, r, _, _ = ffn_shape(layer)
                w = blocks * tiles
                at_row, bounds, at_tile = choice_hots(layer)
                past = bounds.bitcast(F32)
                tile = sm("tile", 2 * NT, 384)
                row = sm("row", 2 * NT, 416)

                def wide(ap, width):
                    return ap.unsqueeze(2).to_broadcast([R, 2 * NT, width])

                def each(ap, n):
                    return ap.unsqueeze(1).to_broadcast([R, n, ap.shape[1]])

                ve.wait_ge(consts, 11)
                d.sync()
                d(ve.tensor_tensor(bounds, wide(small["slot"], w + 1), each(tile0[layer][0:R, :], 2 * NT), ALU.is_ge))
                d.sync()
                d(ve.tensor_reduce(tile, past[:, :, 1:], AX, ALU.add))
                d(ve.tensor_tensor(at_tile, past[:, :, 0:w], past[:, :, 1:], ALU.subtract))
                d.sync()
                d(ve.scalar_tensor_tensor(out=row, in0=tile, scalar=-float(r), in1=small["slot"],
                                          op0=ALU.mult, op1=ALU.add))
                d(ve.tensor_tensor(at_tile, at_tile.bitcast(F32), wide(small["number"], w), ALU.mult))
                d.sync()
                for n in range(0, 2 * NT, HOTS):
                    ve.tensor_tensor(at_row[:, n:n + HOTS, :],
                                     row[:, n:n + HOTS].unsqueeze(2).to_broadcast([R, HOTS, r]),
                                     each(rowno[0:R, 0:r], HOTS), ALU.is_equal).then_inc(hot_ready, 1)
                emptied(ve.tensor_copy(tidx[0:r, 0:w], v.read(ve)[0:r, 0:w]))

            def experts(layer):
                blocks, tiles, r, hidden, _ = ffn_shape(layer)
                wid, mt = tiles * r, hidden // P
                hT = ffn_hT(layer)
                piece0 = 0 if layer == 0 else E * 8

                def turned_bank(b, k):
                    xeT = ffn_xeT(layer, b)
                    bank = PA[:, n_turned[0] % 2, 0:wid]
                    n_turned[0] += 1
                    ve.wait_ge(th_done, n_turned[0])
                    ve.tensor_tensor(xeT[:, 1, k, :], bank, xeT[:, 0, k, :].bitcast(F32),
                                     ALU.subtract).then_inc(t_free, 1)

                def next_block(b, mh, which, m):
                    if b + 1 < blocks:
                        for k in ffn_turns(layer, mh, which, m):
                            turned_bank(b + 1, k)

                if layer == 1:
                    ve.wait_ge(eblk_ready, 1)
                    used = ve.value_load(eblk[0:1, BLK:BLK + 1], min_val=0, max_val=BLK)
                for k in range(KD):
                    turned_bank(0, k)

                def gate(b, mh):
                    next_unit()
                    for m in range(2):
                        next_block(b, mh, 0, m)

                def up_(b, mh):
                    next_unit()
                    for m in range(2):
                        bank = v.read(ve)
                        ve.wait_ge(s_free, gate_at[layer, b * mt + 2 * mh + m])
                        g = RB[:, n_hid[0] % 4, 0:wid]
                        n_hid[0] += 1
                        emptied(ve.tensor_tensor(g, bank[:, 0:wid], g, ALU.mult))
                        ve.wait_ge(hh_done, n_hid[0])
                        ve.tensor_tensor(hT[:, 1, 2 * mh + m, :], g, hT[:, 0, 2 * mh + m, :].bitcast(F32),
                                         ALU.subtract).then_inc(hl_done, 1)
                        next_block(b, mh, 1, m)

                def results(b):
                    npiece = tiles * D // HALF
                    for p in range(npiece):
                        if p % (UNIT // mt // HALF * tiles) == 0:
                            next_unit()
                        j = piece0 + b * npiece + p
                        if j % 2 == 0:
                            if j >= 4:
                                ve.wait_ge(y_st[j % 4], 16 * (j // 4))
                            emptied(ve.tensor_copy(ffn_y(layer, j % 4)[0:r, :], v.read(ve)[0:r, :]))

                def block(b):
                    if layer == 1 or b == 0:
                        gate(b, 0)
                    up_(b, 0)
                    for mh in range(1, mt // 2):
                        gate(b, mh)
                        up_(b, mh)
                    if layer == 0 and b + 1 < blocks:
                        gate(b + 1, 0)
                    results(b)

                for b in range(FIXED[layer]):
                    block(b)
                ve.wait_ge(hl_done, n_hid[0])
                for b in range(FIXED[layer], blocks):
                    with ve.If(used > b):
                        block(b)
                        ve.wait_ge(hl_done, n_hid[0])

            def combine(layer, res, g):
                for n in range(4 * g, 4 * g + 4):
                    i, k = divmod(n, 2)
                    ve.wait_ge(yg_full[n % 4], 16 * (5 * layer + n // 4 + 1))
                    if k:
                        ve.wait_ge(yg_used, 2 * NT * layer + n)
                    ve.scalar_tensor_tensor(out=res[:, i, :], in0=y_slot(layer, n),
                                            scalar=wk[0:R, k, i:i + 1], in1=res[:, i, :],
                                            op0=ALU.mult, op1=ALU.add).then_inc(yg_used, 1)
                ve.wait_ge(yg_used, 2 * NT * layer + 4 * (g + 1))

            small = {}

            def sm(name, n, at):
                small[name] = rbf[0:R, at:at + n]
                return small[name]

            def top2(val):
                mx = sm("mx", NT * E, 1280).rearrange("p (i e) -> p i e", e=E)
                mi = rbf[0:R, 1376:1376 + NT * E].bitcast(U32).rearrange("p (i e) -> p i e", e=E)
                ek = sm("ek", 2 * NT, 1472).rearrange("p (k i) -> p k i", k=2)
                for i in range(NT):
                    d(ve.max(mx[:, i, :], val[:, i, :]))
                d.sync()
                for i in range(NT):
                    d(ve.max_index(mi[:, i, :], mx[:, i, :], val[:, i, :]))
                d.sync()
                d(ve.tensor_copy(ek, mi[:, :, 0:2].rearrange("p i k -> p k i")))
                d.sync()
                return mx, ek

            def onehots(o, ek, k):
                d(ve.tensor_tensor(o, iot8[0:R, :].unsqueeze(1).to_broadcast([R, NT, E]),
                                   ek[:, k, :].unsqueeze(2).to_broadcast([R, NT, E]), ALU.is_equal))

            def ln_x(g):
                ve.wait_ge(x_in[g], 16)
                ln_group(g, row(B3), row(B3))

            ln_x(0)
            ln_x(1)
            next_unit()
            ve.memset(v_heads[:, 160, :], 1.0).then_inc(ones_col, 1)
            d(ve.memset(ecnt[:, :], 0.0))

            def edges(j):
                if j == 4:
                    ve.wait_ge(edges_in, 64)
                    ve.wait_ge(consts, 8)
                    keyt1 = keyt[:, 2 * P:4 * P]
                    d(ve.tensor_copy(keyt[:, 0:2 * P], keyt[:, 0:2 * P].bitcast(I32)))
                    d(ve.tensor_copy(keyt1, keyt1.bitcast(I32)))
                    d(ve.tensor_copy(srcc, srcf.bitcast(I32)))
                    d(ve.tensor_copy(keyf, dstf.bitcast(I32)))
                    d.sync()
                    ve.scalar_tensor_tensor(out=keyt[:, 0:2 * P], in0=keyt[:, 0:2 * P], scalar=float(T), in1=keyt1,
                                            op0=ALU.mult, op1=ALU.add).then_inc(key_ready, 1)
                    d(ve.scalar_tensor_tensor(out=keyf, in0=srcc, scalar=float(T), in1=keyf, op0=ALU.mult,
                                              op1=ALU.add))
                    d(ve.tensor_scalar(later, low[:, :], LATE, 1.0, ALU.mult, ALU.add))
                for m in range(edge_batches(j), edge_batches(j + 1)):
                    c = 4 * m // EQC
                    if m == 0:
                        ve.wait_ge(key_stored, 16)
                    if 4 * m % EQC == 0:
                        ve.wait_ge(eq_in[c % 2], 16 * (c // 2 + 1))
                    d.sync()
                    if m:
                        ve.wait_ge(eq_used, m)
                    for q in range(4):
                        g = 4 * m + q
                        ins = ve.scalar_tensor_tensor(out=eqs[:, q, :],
                                                      in0=key_rows(c)[:, (g - c * EQC) * P:(g - c * EQC + 1) * P],
                                                      scalar=keyf[:, g:g + 1], in1=later, op0=ALU.is_equal,
                                                      op1=ALU.mult, accum_out=ecnt[:, g:g + 1])
                        if q == 3:
                            ins.then_inc(eq_used, 1)
                        else:
                            d(ins)

            def evac_v(m):
                bi = bias(m)
                emptied(ve.tensor_tensor(pair(B1, *divmod(m, NB)), bank2(), bi, ALU.add))

            def lead_x(b):
                if b and b + 1 < NB:
                    ln_x(b + 1)

            lo_pieces(row_pieces(B2), evac_v, lead=lead_x, after=edges)
            d.sync()
            ve.wait_ge(eq_used, GROUPS // 4)
            d(ve.tensor_scalar(first, ecnt[:, :], LATE, None, ALU.is_lt))
            d.sync()
            ve.tensor_tensor(ecnt[:, :], ecnt[:, :], first, ALU.mult).then_inc(eidx_ready, 1)
            d(ve.scalar_tensor_tensor(out=srcc, in0=keyf, scalar=dumpc[:, 0:1], in1=first,
                                      op0=ALU.subtract, op1=ALU.mult))
            d.sync()
            ve.tensor_scalar(eidx[:, :], srcc, dumpc[:, 0:1], None, ALU.add).then_inc(eidx_ready, 1)

            def heads_bias(g):
                n = g % (NQ * NB)
                bi = bias(n)
                if n >= 2:
                    ve.wait_ge(s_full, mark["k_s"] + g - 1)
                emptied(ve.tensor_tensor(two(RB[0:R, n % 2, :]), bank2(), bi, ALU.add))

            def heads_sums(g):
                ve.wait_ge(sq_done, g + 1)
                ve.tensor_reduce(hs8[0:R, :], RB[0:R, 2 + g % 2, :].rearrange("p (h e) -> p h e", e=HD), AX, ALU.add)\
                  .then_inc(ss_done, 1)

            def heads_scaled(g):
                t8 = RB[0:R, g % 2, :].rearrange("p (h e) -> p h e", e=HD)
                ve.wait_ge(nrm_done, g + 1)
                d(ve.tensor_scalar(nr8[0:R, :], nr8[0:R, :], 1e-8, None, ALU.add))
                d.sync()
                d(ve.reciprocal(nr8[0:R, :], nr8[0:R, :]))
                d.sync()
                ve.tensor_tensor(t8, t8, nr8[0:R, :].unsqueeze(2).to_broadcast([R, 8, HD]), ALU.mult)\
                  .then_inc(qn_done, 1)

            last = NQ * NB - 1

            def head_pieces(g):
                def heads(j):
                    if j >= 7 and j % 4 == 3:
                        heads_bias(g + (j - 7) // 4)
                    if j >= 8 and j % 4 == 0:
                        heads_sums(g + (j - 8) // 4)
                    if j >= 9 and j % 4 == 1:
                        heads_scaled(g + (j - 9) // 4)

                lo_pieces(row_pieces(B2), None, after=heads)
                heads_sums(g + last - 1)
                heads_scaled(g + last - 1)
                heads_bias(g + last)
                heads_sums(g + last)
                heads_scaled(g + last)

            ve.wait_ge(table_zero, 16 * NZERO)
            head_pieces(0)
            for n in range(KD * NT):
                if n >= 4:
                    ve.wait_ge(kp_used, n - 3)
                emptied(ve.tensor_scalar(RB[0:R, n % 4, :], v.read(ve)[0:R, :], 0.0, 0.1, ALU.max, ALU.add))
            head_pieces(NQ * NB)

            def attend(step):
                pr, c = divmod(step, 3)
                c0, cn = CH[c]
                rd = q_norm(step)[:, 0:cn]
                ve.wait_ge(den_done, 2 * (step + 1))
                d(ve.tensor_scalar(rd, rd, 1e-6, None, ALU.max))
                d.sync()
                d(ve.reciprocal(rd, rd))
                d.sync()
                for hh in range(2):
                    b = slice(64 * hh, 64 * hh + 64)
                    ve.tensor_tensor(cols(B1)[b, pr, c0:c0 + cn], q_acc(step)[b, hh, 0:cn], rd[b, :], ALU.mult)\
                      .then_inc(acc_free, 1)

            for n in range(0, NH * 6, 2):
                cn = CH[n // 4 % 3][1]
                if n >= 6:
                    ve.wait_ge(qp_used, n - 5)
                emptied(ve.tensor_scalar(q_feats(n)[:, 0:cn], v.read(ve)[:, 0:cn], 0.0, 0.1, ALU.max, ALU.add))
                if n >= 6 and n % 4 == 2:
                    attend((n - 6) // 4)
            attend(3 * KD - 1)
            ve.wait_ge(acc_free, NH * 3)
            lo_pieces(row_pieces(B1), add_residual(B3, True))
            residual_done()

            def evac_h(m):
                emptied(ve.tensor_copy(pair(B1, *divmod(m, NB)), bank2()))

            lo_pieces(row_pieces(B2), evac_h)
            for c in range(T // AC):
                next_unit()
                emptied(ve.tensor_copy(rbf[:, c * AC:(c + 1) * AC], v.read(ve)[:, 0:AC]))
            for g in range(3):
                nq = min(4, NT - 4 * g)
                emptied(ve.tensor_copy(dcol[0:R, 4 * g:4 * g + nq],
                                       v.read(ve)[0:R, 0:nq * P].rearrange("p (q c) -> p q c", c=P)[:, :, 0]))
            ve.wait_ge(v_free, v.n)
            ve.tensor_scalar(dcol[0:R, :], dcol[0:R, :], 1.0, None, ALU.add).then_inc(dg_in, 1)
            d(ve.tensor_reduce(dmaxf[0:1, 0:1], rbf[0:1, 0:T], AX, ALU.max))
            d.sync()
            ve.tensor_copy(dmax[0:1, 0:1], dmaxf[0:1, 0:1]).then_inc(dmax_ready, 1)
            ve.wait_ge(dg_sqrt, 1)
            ve.reciprocal(dinv[0:R, :], dinv[0:R, :]).then_inc(dg_in, 1)
            ve.wait_ge(dg_in, 2)
            split_rows(dinv)
            ve.wait_ge(rl_done, n_rows[0])
            ve.wait_ge(deg_stored, 16)
            ve.wait_ge(gcn_b_in, 16)
            n = 0
            for c in range(T // AC):
                next_unit()
                for half in range(2):
                    hc = slice(half * HALF, (half + 1) * HALF)
                    for i in (2 * c, 2 * c + 1):
                        t = RB[0:R, n % 2, :]
                        n += 1
                        emptied(ve.tensor_tensor(t, v.read(ve)[0:R, :], rows(B2, FR)[:, i, hc].bitcast(F32),
                                                 ALU.add))
                        ve.wait_ge(v_free, v.n)
                        d(ve.tensor_tensor(t, t, rows(B1, FR)[:, i, hc].bitcast(F32), ALU.add))
                        d.sync()
                        d(ve.scalar_tensor_tensor(out=t, in0=t, scalar=dinv[0:R, i:i + 1], in1=gcn_b[:, hc],
                                                  op0=ALU.mult, op1=ALU.add))
                        d.sync()
                        d(ve.scalar_tensor_tensor(out=rows(B3)[:, i, hc], in0=t, scalar=0.0, in1=rows(B3)[:, i, hc],
                                                  op0=ALU.max, op1=ALU.add))
                ln_routed(0, c)
            d.sync()

            lg = sm("lg", NT * E, 512).rearrange("p (i e) -> p i e", e=E)
            pr = sm("pr", NT * E, 608).rearrange("p (i e) -> p i e", e=E)
            z = sm("z", NT, 704)
            scores(0)
            d(ve.tensor_reduce(z, lg, AX, ALU.max))
            d.sync()
            ve.tensor_tensor(lg, lg, z.unsqueeze(2).to_broadcast([R, NT, E]), ALU.subtract).then_inc(sm_in, 1)
            ve.wait_ge(sm_exp, 1)
            d(ve.tensor_reduce(z, lg, AX, ALU.add))
            d.sync()
            d(ve.reciprocal(z, z))
            d.sync()
            d(ve.tensor_tensor(pr, lg, z.unsqueeze(2).to_broadcast([R, NT, E]), ALU.mult))
            d.sync()
            mx, ek = top2(pr)
            d(ve.tensor_tensor(z, mx[:, :, 0], mx[:, :, 1], ALU.add))
            d.sync()
            d(ve.tensor_scalar(z, z, 1e-9, None, ALU.add))
            d.sync()
            d(ve.reciprocal(z, z))
            d.sync()
            gts = rbf[0:R, 1024:1024 + 3 * NT * E].rearrange("p (a i e) -> p a i e", a=3, e=E)
            for k in range(2):
                d(ve.tensor_tensor(wk[0:R, k, :], mx[:, :, k], z, ALU.mult))
                onehots(gts[:, 1 + k, :, :], ek, k)
            d.sync()
            d(ve.tensor_tensor(gts[:, 0, :, :], gts[:, 1, :, :],
                               wk[0:R, 0, :].unsqueeze(2).to_broadcast([R, NT, E]), ALU.mult))
            d(ve.tensor_tensor(pr, gts[:, 2, :, :], wk[0:R, 1, :].unsqueeze(2).to_broadcast([R, NT, E]), ALU.mult))
            d.sync()
            ve.tensor_tensor(gts[:, 0, :, :], gts[:, 0, :, :], pr, ALU.add).then_inc(gates_ready, 1)
            gT = F[0:E, B2:B2 + 3 * T].rearrange("p (a t) -> p a t", t=T)
            ve.wait_ge(gz_ready, 1)
            for a in range(3):
                for g in range(3):
                    w = min(4, NT - 4 * g) * R
                    emptied(ve.tensor_copy(gT[:, a, 4 * g * R:4 * g * R + w], v.read(ve)[0:E, 0:w]))
            nself = sm("nself", E, 160)
            per_e = v.read(ve)[0:R, 0:2 * NT * E].rearrange("p (c e) -> p e c", e=E)
            emptied(ve.tensor_reduce(nself, per_e, AX, ALU.add))
            ve.wait_ge(v_free, v.n)
            ve.tensor_copy(nsel[0:R, :], nself).then_inc(nsel_ready, 1)
            rk = sm("rk", 7 * 2 * NT, 0).rearrange("p (a k i) -> p a k i", a=7, k=2)
            scr = RB[0:R, 3, :]
            scr2 = F[0:R, B2 + 4000:B2 + 4000 + HALF]
            d(ve.memset(small["rk"], 0.0))
            d.sync()
            for n in range(2 * NT):
                k, i = divmod(n, NT)
                for c0 in range(0, T, HALF):
                    cn = min(HALF, T - c0)
                    ve.wait_ge(v_free, v.n)
                    d.sync()
                    bank = v.read(ve)[0:R, :]
                    own = (i * R, (i + 1) * R)
                    c = c0 // HALF
                    g = wk[0:R, k, i:i + 1]
                    a, b = max(own[0], c0), min(own[1], c0 + cn)
                    if a < b:
                        d(ve.scalar_tensor_tensor(out=scr2[:, 0:b - a], in0=bank[:, a - c0:b - c0], scalar=g,
                                                  in1=low[0:R, a - own[0]:b - own[0]], op0=ALU.is_equal, op1=ALU.mult,
                                                  accum_out=rk[:, 5 if a > own[0] else 6, k, i:i + 1]))
                    m = min(max(own[0] - c0, 0), cn)
                    parts = [(0, m, ALU.is_ge), (m, cn, ALU.is_gt)]
                    parts = [x for x in parts if x[0] < x[1]]
                    for q, (a, b, op) in enumerate(parts):
                        dst = rk[:, c if (q == 0) else 3 + 0, k, i:i + 1]
                        ins = ve.tensor_scalar(scr[:, a:b], bank[:, a:b], g, None, op, ALU.add, accum_out=dst)
                        if q == len(parts) - 1:
                            emptied(ins)
                        else:
                            d(ins)
            d.sync()
            ve.wait_ge(v_free, v.n)
            rank = sm("rank", 2 * NT, 160).rearrange("p (k i) -> p k i", k=2)
            keep = sm("keep", 2 * NT, 192).rearrange("p (k i) -> p k i", k=2)
            slot = sm("slot", 2 * NT, 224).rearrange("p (k i) -> p k i", k=2)
            number = sm("number", 2 * NT, 352).rearrange("p (k i) -> p k i", k=2)
            d(ve.tensor_tensor(rank, rk[:, 0, :, :], rk[:, 1, :, :], ALU.add))
            for a in range(2, 7):
                d.sync()
                d(ve.tensor_tensor(rank, rank, rk[:, a, :, :], ALU.add))
            d.sync()
            d(ve.tensor_scalar(keep, rank, float(CAP), None, ALU.is_lt))
            d(ve.scalar_tensor_tensor(out=slot, in0=ek, scalar=float(CAPR), in1=rank, op0=ALU.mult, op1=ALU.add))
            d.sync()
            d(ve.tensor_tensor(wk[0:R, :, :], wk[0:R, :, :], keep, ALU.mult))
            for k in range(2):
                d(ve.tensor_tensor(number[:, k, :], tok[0:R, :], keep[:, k, :], ALU.mult))
            ve.tensor_tensor(gidx[0:R, :, :], slot, keep, ALU.mult).then_inc(route_ready, 1)
            row_tokens(0)
            experts(0)

            def ln_x2(g):
                combine(0, rows(B3), g)
                ln_group(g, row(B3), row(B1))

            def lead_x2(b):
                if b and b + 1 < NB:
                    ln_x2(b + 1)

            def evac_v1(m):
                q, b = divmod(m, NB)
                if q == 0:
                    ve.wait_ge(xn_st[b], 16)
                bi = bias(m)
                emptied(ve.tensor_tensor(pair(B1, q, b), bank2(), bi, ALU.add))

            ln_x2(0)
            ln_x2(1)
            lo_pieces(row_pieces(B2), evac_v1, lead=lead_x2)
            ve.wait_ge(small_in, 32)
            ve.wait_ge(x2_stored, 16 * NB)

            def heads_cols(which):
                def evac(m):
                    q, c = divmod(m, T // AC)
                    emptied(ve.tensor_tensor(cols(B3)[:, 2 * q:2 * q + 2, c * AC:(c + 1) * AC],
                                             v.read(ve)[:, 0:2 * AC].rearrange("p (m t) -> p m t", m=2),
                                             bcol[:, which, 2 * q:2 * q + 2].unsqueeze(2).to_broadcast([P, 2, AC]),
                                             ALU.add))
                return evac

            lo_pieces(col_pieces(B2), heads_cols(0))
            d(ve.memset(kvbd, 0.0))
            for n in range(2 * NT):
                if n >= 4:
                    ve.wait_ge(kp_used, KD * NT + n - 3)
                emptied(ve.tensor_scalar(RB[0:R, n % 4, :], v.read(ve)[0:R, :], 0.0, 0.125, ALU.max, ALU.mult))
            ve.wait_ge(kp_used, KD * NT + 2 * NT)
            d.sync()
            for half in range(2):
                for q in range(4):
                    for hh in range(2):
                        b = slice(64 * hh, 64 * hh + 64)
                        ve.tensor_copy(kvbd[b, 4 * half + q, 64 * hh:64 * hh + 64],
                                       PA[b, half, q * P + 64 * hh:q * P + 64 * hh + 64]).then_inc(kvbd_ready, 1)
            lo_pieces(col_pieces(B2), heads_cols(1))
            for n in range(3 * KD):
                cn = CH[n % 3][1]
                if n >= 4:
                    ve.wait_ge(s_full, mark["qp1_s"] - 3 * KD + n - 3)
                emptied(ve.tensor_scalar(RB[:, n % 4, 0:cn], v.read(ve)[:, 0:cn], 0.0, 0.125, ALU.max, ALU.mult))
            lo_pieces(row_pieces(B1), add_residual(B3, True))
            residual_done()

            ve.wait_ge(dinv_in, 16)
            d(ve.tensor_scalar(degs, degs, 1.0, None, ALU.max))
            d.sync()
            d(ve.reciprocal(degs, degs))

            def evac_own(m):
                if m >= 4:
                    ve.wait_ge(hs_st[m % 4], 16 * (m // 4))
                bi = bias(m)
                emptied(ve.tensor_tensor(two(RB[0:R, m % 4, :]), bank2(), bi, ALU.add))

            lo_pieces(row_pieces(B2), evac_own)

            def means():
                for c in range(T // AC):
                    next_unit()
                    for f in range(KD):
                        emptied(ve.tensor_tensor(cols(B3)[:, f, c * AC:(c + 1) * AC], v.read(ve)[:, 0:AC],
                                                 degs[:, c * AC:(c + 1) * AC], ALU.mult))

            d.sync()
            split_rows()
            ve.wait_ge(xm_stored, 16 * NQ * NB)
            means()
            lo_pieces(row_pieces(B3), add_residual(B1, False, relu=True))
            residual_done()
            lo_pieces(row_pieces(B2), add_residual(B3, True))
            residual_done()
            split_rows()
            ve.wait_ge(xs_stored, 16 * NQ * NB)
            means()
            add_last = add_residual(B1, False)

            def add_and_norm(m):
                add_last(m)
                if m >= (NQ - 1) * NB:
                    ln_routed(1, m - (NQ - 1) * NB)

            lo_pieces(row_pieces(B3), add_and_norm)
            residual_done()

            scores(1)
            d(ve.tensor_copy(pr, lg))
            d.sync()
            mx, ek = top2(pr)
            d2 = rbf[0:R, 512:512 + NT]
            ve.tensor_tensor(d2, mx[:, :, 1], mx[:, :, 0], ALU.subtract).then_inc(sm_in, 1)
            ve.wait_ge(sm_exp, 2)
            d(ve.tensor_scalar(z, d2, 1.0, None, ALU.add))
            d.sync()
            d(ve.reciprocal(z, z))
            d.sync()
            d(ve.tensor_copy(wk[0:R, 0, :], z))
            d(ve.tensor_tensor(wk[0:R, 1, :], d2, z, ALU.mult))
            osum = rbf[0:R, 1024:1024 + NT * E].rearrange("p (i e) -> p i e", e=E)
            oh = [rbf[0:R, 1104 + 80 * k:1184 + 80 * k].rearrange("p (i e) -> p i e", e=E) for k in range(2)]
            for k in range(2):
                onehots(oh[k], ek, k)
            d.sync()
            ve.tensor_tensor(osum, oh[0], oh[1], ALU.add).then_inc(gates_ready, 1)
            pos = sm("pos", NT * E, 800).rearrange("p (i e) -> p i e", e=E)
            tot = sm("tot", NT * E, 896).rearrange("p (e i) -> p e i", e=E)
            run = sm("run", NT * E, 0).rearrange("p (e i) -> p e i", e=E)
            more = sm("more", NT * E, 96).rearrange("p (e i) -> p e i", e=E)
            d(ve.memset(more, 1.0))
            d.sync()
            d(ve.memset(more[:, :, 0:1], 0.0))
            bank = v.read(ve)
            d(ve.tensor_copy(small["pos"], bank[0:R, 0:NT * E]))
            emptied(ve.tensor_copy(tot, bank[0:R, P:P + NT * E].rearrange("p (i e) -> p e i", e=E)))
            ve.wait_ge(v_free, v.n)
            nblk = -(-T // 256)
            nb = sm("nb", E, 736)
            cmp = sm("cmp", E * nblk, 192).rearrange("p (e j) -> p e j", e=E)
            end = sm("end", E, 752)
            start = sm("start", E, 768)
            d.sync()
            d(ve.tensor_tensor_scan(small["run"], small["more"], small["tot"], 0.0, ALU.mult, ALU.add))
            d.sync()
            d(ve.tensor_tensor(cmp, run[:, :, NT - 1].unsqueeze(2).to_broadcast([R, E, nblk]),
                               tile0[1][0:R, 0:2 * nblk:2].unsqueeze(1).to_broadcast([R, E, nblk]), ALU.is_gt))
            d(ve.tensor_tensor(tot, run, tot, ALU.subtract))
            d.sync()
            d(ve.tensor_reduce(nb, cmp, AX, ALU.add))
            d(ve.tensor_tensor(pos, pos, tot.rearrange("p e i -> p i e"), ALU.add))
            d.sync()
            d(ve.tensor_tensor_scan(end, ones[0:R, 0:E], nb, 0.0, ALU.mult, ALU.add))
            d.sync()
            d(ve.tensor_tensor(start, end, nb, ALU.subtract))
            be = sm("be", BLK + 1, 288)
            bc = sm("bc", BLK * E, 1280).rearrange("p (b e) -> p b e", e=E)
            d(ve.tensor_tensor(bc[:, :, 0:E - 1], rowno[0:R, 0:BLK].unsqueeze(2).to_broadcast([R, BLK, E - 1]),
                               end[:, 0:E - 1].unsqueeze(1).to_broadcast([R, BLK, E - 1]), ALU.is_ge))
            d.sync()
            d(ve.tensor_reduce(be[:, 0:BLK], bc[:, :, 0:E - 1], AX, ALU.add))
            d(ve.tensor_copy(be[:, BLK:BLK + 1], end[:, E - 1:E]))
            d.sync()
            ve.tensor_copy(eblk[0:R, :], be).then_inc(eblk_ready, 1)
            d(ve.tensor_scalar(start, start, 256.0, None, ALU.mult))
            d.sync()
            d(ve.tensor_tensor(pos, pos, start.unsqueeze(1).to_broadcast([R, NT, E]), ALU.add))
            d.sync()
            slot = sm("slot", 2 * NT, 224).rearrange("p (k i) -> p k i", k=2)
            for k in range(2):
                d(ve.tensor_tensor(oh[k], oh[k], pos, ALU.mult))
                d.sync()
                d(ve.tensor_reduce(slot[:, k, :], oh[k], AX, ALU.add))
            d.sync()
            ve.tensor_copy(gidx[0:R, :, :], slot).then_inc(route_ready, 1)
            for k in range(2):
                d(ve.tensor_copy(number[:, k, :], tok[0:R, :]))
            row_tokens(1)
            next_unit(True)
            experts(1)
            for g in range(NB):
                combine(1, rows(B1), g)


_NAMES = ['x', 'src', 'dst', 'L0_gnn_W', 'L0_gnn_b', 'L0_mix_Wq', 'L0_mix_bq', 'L0_mix_Wk', 'L0_mix_bk',
          'L0_mix_Wv', 'L0_mix_bv', 'L0_mix_Wo', 'L0_mix_bo', 'L0_mix_projection', 'L0_ffn_router_gate',
          'L0_ffn_gate_w', 'L0_ffn_up_w', 'L0_ffn_down_w', 'L1_gnn_W_self0', 'L1_gnn_W_neigh0', 'L1_gnn_b0',
          'L1_gnn_W_self1', 'L1_gnn_W_neigh1', 'L1_gnn_b1', 'L1_mix_Wq', 'L1_mix_bq', 'L1_mix_Wk', 'L1_mix_bk',
          'L1_mix_Wv', 'L1_mix_bv', 'L1_mix_Wo', 'L1_mix_bo', 'L1_mix_P', 'L1_ffn_w12', 'L1_ffn_w3',
          'L1_ffn_gate_w']


def _layout(name, a, np):
    if name in ("src", "dst"):
        pad = np.full(P * GROUPS - EDGES, T if name == "src" else 0, a.dtype)
        e = np.concatenate([a, pad])
        return np.stack([e, e.reshape(P, GROUPS).T.reshape(-1)])
    if name == "L0_mix_projection":
        o = np.zeros((2, HD, KD, 2, F0), a.dtype)
        for h in range(2):
            o[h, :, :, h, :] = a.reshape(KD, 2, F0, HD)[:, h].transpose(2, 0, 1)
        return o.reshape(P, KD * 2 * F0)
    if name == "L1_mix_P":
        o = np.zeros((2, HD, KD, 2, HD), a.dtype)
        for h in range(2):
            o[h, :, :, h, :] = a.reshape(KD, 2, HD, HD)[:, h].transpose(2, 0, 1)
        return o.reshape(P, KD, P)
    if name in ("L1_mix_bk", "L1_mix_bq"):
        return a.reshape(KD, P).T
    if name in ("L1_mix_Wq", "L1_mix_Wk", "L1_mix_Wv", "L1_mix_Wo", "L1_ffn_gate_w"):
        return a.T
    if name in ("L1_ffn_w12", "L1_ffn_w3"):
        return a.transpose(0, 2, 1)
    return a


def kernel(**inputs):
    import numpy as np
    import concourse.bacc as bacc
    from concourse.bass_utils import run_bass_kernel_spmd

    nc = bacc.Bacc("TRN2", target_bir_lowering=False, num_devices=1)
    arrays, aps = {}, {}
    for name in _NAMES:
        a = np.ascontiguousarray(_layout(name, np.asarray(inputs[name]), np))
        arrays[f"in_{name}"] = a
        aps[name] = nc.dram_tensor(f"in_{name}", a.shape, mybir.dt.from_np(a.dtype), kind="ExternalInput").ap()
    out = nc.dram_tensor("out_x", (T, D), F32, kind="ExternalOutput").ap()
    build(nc, aps, out)
    r = run_bass_kernel_spmd(nc, [arrays], core_ids=[0])
    return r.results[0]["out_x"]
```
